# Optimizing a Trainium2 kernel written in Bass

```python
import numpy as np
import jax
import jax.numpy as jnp

def _softmax(x, axis=-1):
    return jax.nn.softmax(x, axis=axis)

def _gelu(x):
    return jax.nn.gelu(x, approximate=True)

def _silu(x):
    return jax.nn.silu(x)

def _sigmoid(x):
    return jax.nn.sigmoid(x)

def _layernorm(x, axis=-1, eps=1e-05):
    m = jnp.mean(x, axis=axis, keepdims=True)
    v = jnp.var(x, axis=axis, keepdims=True)
    return (x - m) / jnp.sqrt(v + eps)

def _scatter_add(tgt, idx, src, axis=0):
    return tgt.at[idx].add(src)

def _segment_sum(src, seg, n):
    return jax.ops.segment_sum(src, seg, n)
kernel_name = 'mk_adaln_d1_jaxref_r4_e3b618'

def setup_inputs(seed: int=0):
    np.random.seed(seed)
    _w = jnp.asarray

    def _L0_attn_setup():
        import jax, jax.numpy as jnp
        import numpy as np
        import math
        HIDDEN = 256
        key = jax.random.key(seed)
        kx, kq, kk, kv = jax.random.split(key, 4)
        B, S, H = (4, 1024, HIDDEN)
        scale = 1.0 / math.sqrt(H)
        x = jax.random.normal(kx, (B, S, H), dtype=jnp.float32)
        Wq = jax.random.normal(kq, (H, H), dtype=jnp.float32) * scale
        Wk = jax.random.normal(kk, (H, H), dtype=jnp.float32) * scale
        Wv = jax.random.normal(kv, (H, H), dtype=jnp.float32) * scale
        return {'x': x, 'Wq': Wq, 'Wk': Wk, 'Wv': Wv}
    _L0_attn_in = _L0_attn_setup()

    def _L0_ffn_setup():
        import jax, jax.numpy as jnp
        import numpy as np
        from jax import lax
        D = 256
        E = 8
        F = 1024
        TOP_K = 2
        key = jax.random.key(seed)
        ks = jax.random.split(key, 8)
        s = 0.02
        return {'x': jax.random.normal(ks[0], (4, 512, D), dtype=jnp.float32), 'gate_w': jax.random.normal(ks[1], (D, E), dtype=jnp.float32) * s, 'gate_b': jnp.zeros((E,), dtype=jnp.float32), 'w1': jax.random.normal(ks[2], (E, D, F), dtype=jnp.float32) * s, 'b1': jnp.zeros((E, F), dtype=jnp.float32), 'w2': jax.random.normal(ks[3], (E, F, D), dtype=jnp.float32) * s, 'b2': jnp.zeros((E, D), dtype=jnp.float32)}
    _L0_ffn_in = _L0_ffn_setup()
    _L0_c = _w((lambda *s: np.random.randn(*s).astype(np.float32) * 0.05)(8, 256))
    _L0_wmod = _w((lambda *s: np.random.randn(*s).astype(np.float32) * 0.05)(256, 6 * 256) * 256 ** (-0.5))
    _d = {'L0_attn_x': _L0_attn_in['x'], 'L0_attn_Wq': _L0_attn_in['Wq'], 'L0_attn_Wk': _L0_attn_in['Wk'], 'L0_attn_Wv': _L0_attn_in['Wv'], 'L0_ffn_gate_w': _L0_ffn_in['gate_w'], 'L0_ffn_gate_b': _L0_ffn_in['gate_b'], 'L0_ffn_w1': _L0_ffn_in['w1'], 'L0_ffn_b1': _L0_ffn_in['b1'], 'L0_ffn_w2': _L0_ffn_in['w2'], 'L0_ffn_b2': _L0_ffn_in['b2'], 'L0_c': _L0_c, 'L0_wmod': _L0_wmod}
    _x0 = _d['L0_attn_x']
    _d['L0_attn_x'] = jax.random.normal(jax.random.fold_in(jax.random.key(seed), 1), (8, 512, 256), dtype=_x0.dtype)
    del _x0
    return _d

def reference(L0_attn_x, L0_attn_Wq, L0_attn_Wk, L0_attn_Wv, L0_ffn_gate_w, L0_ffn_gate_b, L0_ffn_w1, L0_ffn_b1, L0_ffn_w2, L0_ffn_b2, L0_c, L0_wmod):

    def _L0_attn_ref(x, Wq, Wk, Wv):
        import jax, jax.numpy as jnp
        import numpy as np
        import math
        HIDDEN = 256
        B, S, H = x.shape
        q = jnp.einsum('bsh,oh->bso', x, Wq)
        k = jnp.einsum('bsh,oh->bso', x, Wk)
        v = jnp.einsum('bsh,oh->bso', x, Wv)
        scores = jnp.einsum('bqh,bkh->bqk', q, k) / jnp.sqrt(jnp.float32(H))
        causal = jnp.tril(jnp.ones((S, S), dtype=bool))
        scores = jnp.where(causal[None, :, :], scores, -jnp.inf)
        att = jax.nn.softmax(scores, axis=-1)
        return jnp.einsum('bqk,bkh->bqh', att, v)

    def _L0_ffn_ref(x, gate_w, gate_b, w1, b1, w2, b2):
        import jax, jax.numpy as jnp
        import numpy as np
        from jax import lax
        D = 256
        E = 8
        F = 1024
        TOP_K = 2
        B, S, _ = x.shape
        flat = x.reshape(-1, D)
        T = flat.shape[0]
        logits = flat @ gate_w + gate_b
        topv, topi = lax.top_k(logits, TOP_K)
        topw = jax.nn.softmax(topv.astype(jnp.float32), axis=-1).astype(x.dtype)
        routing = jnp.zeros_like(logits).at[jnp.arange(T)[:, None], topi].set(topw)

        def body(acc, params):
            W1e, b1e, W2e, b2e, we = params
            h = jax.nn.gelu(flat @ W1e + b1e, approximate=False)
            out = h @ W2e + b2e
            return (acc + out * we[:, None], None)
        init = jnp.zeros_like(flat)
        final, _ = lax.scan(body, init, (w1, b1, w2, b2, routing.T))
        return final.reshape(B, S, D)
    x = L0_attn_x
    mod = (_silu(L0_c) @ L0_wmod).reshape(L0_c.shape[0], 6, 1, -1)
    sa, ca, ga, sb, cb, gb = (mod[:, 0], mod[:, 1], mod[:, 2], mod[:, 3], mod[:, 4], mod[:, 5])
    ga = (2 * (ga >= 0) - 1) * jnp.maximum(jnp.abs(ga), 0.25)
    gb = (2 * (gb >= 0) - 1) * jnp.maximum(jnp.abs(gb), 0.25)
    h = _layernorm(x, axis=-1) * (1 + ca) + sa
    x = x + ga * _L0_attn_ref(h, L0_attn_Wq, L0_attn_Wk, L0_attn_Wv)
    h = _layernorm(x, axis=-1) * (1 + cb) + sb
    x = x + gb * _L0_ffn_ref(h, L0_ffn_gate_w, L0_ffn_gate_b, L0_ffn_w1, L0_ffn_b1, L0_ffn_w2, L0_ffn_b2)
    return x

_drawn_inputs = setup_inputs


def setup_inputs(seed=0):
    import zlib

    import numpy as np

    out = dict(_drawn_inputs(seed))
    spreads = {'L0_ffn_gate_b': (0.0, 0.49), 'L0_ffn_b1': (0.0, 0.8), 'L0_ffn_b2': (0.0, 0.45)}
    factors = {'L0_ffn_w1': 2.913, 'L0_ffn_w2': 2.717}
    for name, (base, spread) in spreads.items():
        noise = np.random.default_rng([zlib.crc32(name.encode()), seed]).standard_normal(out[name].shape)
        drawn = base * np.exp(spread * noise) if base else spread * noise
        out[name] = jnp.asarray(drawn.astype(out[name].dtype))
    for name, factor in factors.items():
        out[name] = (out[name] * factor).astype(out[name].dtype)
    return out
```

```python
from contextlib import ExitStack

import concourse.bass as bass
from concourse import mybir
from concourse.alu_op_type import AluOpType as ALU

F32 = mybir.dt.float32
F32R = mybir.dt.float32r
BF16 = mybir.dt.bfloat16
I32 = mybir.dt.int32
U32 = mybir.dt.uint32
ACT = mybir.ActivationFunctionType
AX = mybir.AxisListType

P = 128
B, S, D = 8, 512, 256
NB = S // P
KD = D // P
E, F = 8, 1024
KF = F // P
NT = B * S
TT = 256
TB = TT // P
CAP = NT + TT
TILES = 2 * NT // TT + E
GB, RW, ID, ROW = D, 2 * D, 2 * D + E, 2 * D + 2 * E
AUX = ROW - D
FAR = 1 << 20
EPS = 1e-5
MASKED = -3.0e38
LAG = 4


class Batch:

    def __init__(self, val, half, pair):
        self.val, self.half, self.pair = val, half, pair

    def next(self):
        return Batch(self.val + 1, 1 - self.half, self.pair + self.half)

    def prev(self):
        return Batch(self.val - 1, 1 - self.half, self.pair - (1 - self.half))


def wait(eng, sem, count):
    if isinstance(count, int) and count <= 0:
        return
    eng.wait_ge(sem, count + 1)


def start(eng, *sems):
    for sem in sems:
        eng.sem_inc(sem, 1)


class Chain:

    def __init__(self, eng, sem, per, times):
        self.eng, self.sem, self.per, self.base, self.n = eng, sem, per, times * per, 0

    def so_far(self):
        return self.sem, self.base + self.n

    def step(self, ins):
        self.n += 1
        assert self.n <= self.per
        ins.then_inc(self.sem, 1)

    def done(self):
        wait(self.eng, *self.so_far())


def over_batches(eng, iteration):
    first = Batch(0, 0, 0)
    iteration(None, first, None, None)
    iteration(first, first.next(), first, None)
    with eng.Fori(0, (B - 4) // 2) as m:
        for k in (Batch(2 * m + 1, 1, m), Batch(2 * m + 2, 0, m + 1)):
            iteration(k, k.next(), k, k.prev())
    for n in range(B - 3, B + 1):
        k = Batch(n, n % 2, n // 2)
        iteration(k, k.next() if n + 1 < B else None, k if n < B else None, k.prev())


def there(b, more=0):
    return b is not None and not (isinstance(b.val, int) and b.val + more >= B)


def over_experts(eng, expert):
    with eng.Fori(0, (E - 2) // 2) as m:
        expert(2 * m, 0, 2)
        expert(2 * m + 1, 1, 2)
    expert(E - 2, 0, 1)
    expert(E - 1, 1, 0)


def layer(nc, x, Wq, Wk, Wv, gate_w, gate_b, w1, b1, w2, b2, c, wmod, out):
    ctx = ExitStack()
    with ctx:
        def sb(name, shape, dt=F32, where=ctx):
            return where.enter_context(nc.sbuf_tensor(name, shape, dt))

        def sem(name):
            return ctx.enter_context(nc.semaphore(name))

        lists = nc.dram_tensor("lists", [E * CAP, ROW], F32).ap()
        modd = nc.dram_tensor("modd", [B, 6 * D], F32).ap()
        xb = x.rearrange("b (i p) d -> b p i d", p=P)
        outb = out.rearrange("b (i p) d -> b p i d", p=P)
        out_rows = out.rearrange("b s d -> (b s) d")

        ident = sb("ident", [P, P])
        pad = sb("pad", [P, TB, ROW])
        rows80 = sb("rows80", [E * KF + E * KD, P])
        biasT = sb("biasT", [P, E * KF + E * KD])
        tab = sb("tab", [1, 32], I32)
        stage1 = sb("stage1", [P, KD, F])
        stage2 = sb("stage2", [P, KF, D])
        w1h, w1l, w2h, w2l = [], [], [], []

        def expert_weights(n, where):
            w1h.append(sb(f"w1h{n}", [P, KD, F], F32R, where))
            w1l.append(sb(f"w1l{n}", [P, KD, F], F32R, where))
            w2h.append(sb(f"w2h{n}", [P, KF, D], F32R, where))
            w2l.append(sb(f"w2l{n}", [P, KF, D], F32R, where))

        expert_weights(0, ctx)
        bcur = [sb(f"bcur{n}", [P, KF + KD]) for n in range(2)]

        one = ExitStack()

        def s1(name, shape, dt=F32):
            return sb(name, shape, dt, one)

        with ExitStack() as zero:
            wmod_s = sb("wmod_s", [P, KD, 6 * D], F32, zero)
            wq_s = sb("wq_s", [P, KD, D], F32, zero)
            wk_s = sb("wk_s", [P, KD, D], F32, zero)
            wv_s = sb("wv_s", [P, KD, D], F32, zero)
        batch1 = [s1(f"{name}1", shape, F32R) for name, shape in (
            ("hh", [P, KD, S]), ("hl", [P, KD, S]), ("qh", [P, KD, S]), ("ql", [P, KD, S]),
            ("vh", [P, NB, D]), ("vl", [P, NB, D]))]
        maskb = s1("maskb", [P, P], BF16)
        identb = s1("identb", [P, P], BF16)
        trib = s1("trib", [P, P], BF16)
        onesb = s1("onesb", [P, P], BF16)
        mh = s1("mh", [P, KD, D], F32R)
        ml = s1("ml", [P, KD, D], F32R)
        wvh = s1("wvh", [P, KD, D], F32R)
        wvl = s1("wvl", [P, KD, D], F32R)
        gw = s1("gw", [P, KD, E])
        gbias = s1("gbias", [P, NB, E])
        iota8 = s1("iota8", [P, NB, E])
        ecap = s1("ecap", [P, NB, E])
        c_s = s1("c_s", [B, D])
        cT = s1("cT", [P, KD, B])
        ecT = s1("ecT", [P, KD, B])
        mods = s1("mods", [B, 6, D])
        mtmp = s1("mtmp", [B, D])
        mtmp2 = s1("mtmp2", [B, D])
        modT = s1("modT", [P, 4, B])
        xa = [s1(f"xa{n}", [P, NB, D]) for n in range(2)]
        xr = [s1(f"xr{n}", [P, NB, D]) for n in range(2)]
        mb = [s1(f"mb{n}", [P, 3, D]) for n in range(2)]
        mt = [s1(f"mt{n}", [P, 4]) for n in range(2)]
        xn = [s1(f"xn{n}", [P, NB, D]) for n in range(2)]
        st1 = s1("st1", [P, NB, 6])
        mv1 = s1("mv1", [P, NB, 2])
        ln1 = s1("ln1", [P, 4, NB])
        r1 = s1("r1", [P, NB])
        mean1 = s1("mean1", [P, NB])
        st2 = s1("st2", [P, NB, 6])
        mv2 = s1("mv2", [P, NB, 2])
        ln2 = s1("ln2", [P, 4, NB])
        r2 = s1("r2", [P, NB])
        hf = s1("hf", [P, KD, S])
        hh = [s1("hh0", [P, KD, S], F32R), batch1[0]]
        hl = [s1("hl0", [P, KD, S], F32R), batch1[1]]
        qh = [s1("qh0", [P, KD, S], F32R), batch1[2]]
        ql = [s1("ql0", [P, KD, S], F32R), batch1[3]]
        vh = [s1("vh0", [P, NB, D], F32R), batch1[4]]
        vl = [s1("vl0", [P, NB, D], F32R), batch1[5]]
        nmax = s1("nmax", [P, NB])
        rsum = s1("rsum", [P, NB])
        rinv = s1("rinv", [P, NB])
        pr = [s1(f"pr{n}", [P, S]) for n in range(2)]
        pth = [s1(f"pth{n}", [P, NB, P], F32R) for n in range(2)]
        ptl = [s1(f"ptl{n}", [P, NB, P], F32R) for n in range(2)]
        ob = s1("ob", [P, NB, D])
        rows = s1("rows", [P, 2 * NB, ROW])
        rows_i = rows[:, :, :].bitcast(I32)
        h2f = s1("h2f", [P, KD, S])
        lg = s1("lg", [P, NB, E])
        mx = s1("mx", [P, NB, E])
        mxi = s1("mxi", [P, NB, E], U32)
        idxf = s1("idxf", [P, NB, 2])
        o1 = s1("o1", [P, NB, E])
        o2 = s1("o2", [P, NB, E])
        picks = s1("picks", [P, NB, E], BF16)
        before = s1("before", [P, NB + 1, E], BF16)
        dl = s1("dl", [P, NB])
        el = s1("el", [P, NB])
        wt = s1("wt", [P, 3, NB])
        ra = s1("ra", [P, NB, E])
        rb = s1("rb", [P, NB, E])
        pos = s1("pos", [P, NB, E])
        pt1 = s1("pt1", [P, 2, NB, E])
        numbers = s1("numbers", [P, 2 * NB], I32)
        slotf = s1("slotf", [P, 2, NB])
        slots = [s1(f"slots{n}", [P, 2, NB], I32) for n in range(2)]
        cnt = s1("cnt", [1, 4, E])
        cnti = s1("cnti", [1, 2, E], I32)
        unit = s1("unit", [1, E])
        one.close()

        expert_weights(1, ctx)
        xt = sb("xt", [P, TB, D])
        aux = sb("aux", [P, TB, AUX])
        aux_i = aux[:, :, :].bitcast(I32)
        xth = sb("xth", [P, KD, TT], F32R)
        xtl = sb("xtl", [P, KD, TT], F32R)
        gf = sb("gf", [P, KF, TT])
        gh = sb("gh", [P, KF, TT], F32R)
        gl = sb("gl", [P, KF, TT], F32R)
        yT = sb("yT", [P, KD, TT])
        ysc = sb("ysc", [P, TB, D])
        wcur = sb("wcur", [P, TB, 1])

        ps = ctx.enter_context(nc.psum_tensor("ps", [P, 8, 512], F32))
        BANK_T, BANK_QA, BANK_QB, BANK_S, BANK_P, BANK_O = 0, 2, 3, 4, 6, 7
        BANK_H, BANK_Y, BANK_X, BANK_YT = 0, 4, 6, 7

        w_in = sem("w_in")
        consts = sem("consts")
        iotas = sem("iotas")
        setup_pe = sem("setup_pe")
        setup_act = sem("setup_act")
        setup_dve = sem("setup_dve")
        mod_out = sem("mod_out")
        xa_in = [sem(f"xa_in{n}") for n in range(2)]
        xr_in = [sem(f"xr_in{n}") for n in range(2)]
        mb_in = [sem(f"mb_in{n}") for n in range(2)]
        gb_in = [sem(f"gb_in{n}") for n in range(2)]
        x1_out = [sem(f"x1_out{n}") for n in range(2)]
        scattered = [sem(f"scattered{n}") for n in range(2)]
        rows_free = sem("rows_free")
        mt_ready = sem("mt_ready")
        l1a, l1b, l2a, l2b = sem("l1a"), sem("l1b"), sem("l2a"), sem("l2b")
        l1_act, l2_act = sem("l1_act"), sem("l2_act")
        xn_ready = sem("xn_ready")
        t_done = sem("t_done")
        h_full = sem("h_full")
        h_hi, h_lo = sem("h_hi"), sem("h_lo")
        q_done, q_hi, q_lo = sem("q_done"), sem("q_hi"), sem("q_lo")
        v_done, v_hi, v_lo = sem("v_done"), sem("v_hi"), sem("v_lo")
        s_done, neg_max, p_exp = sem("s_done"), sem("neg_max"), sem("p_exp")
        pt_done, pt_hi, pt_lo = sem("pt_done"), sem("pt_hi"), sem("pt_lo")
        o_done, r_inv, o_scaled = sem("o_done"), sem("r_inv"), sem("o_scaled")
        x1_ready = sem("x1_ready")
        h2_mid, h2_ready = sem("h2_mid"), sem("h2_ready")
        gt_done, g_full = sem("gt_done"), sem("g_full")
        lg_done, lg_read = sem("lg_done"), sem("lg_read")
        ra_s, rb_s, rc_s = sem("ra_s"), sem("rb_s"), sem("rc_s")
        el_done = sem("el_done")
        ps_done, ps_read = sem("ps_done"), sem("ps_read")
        cnt_done, tab_s = sem("cnt_done"), sem("tab_s")
        passed = sem("passed")
        over = sem("over")
        pad_out = sem("pad_out")
        st_in = sem("st_in")
        w_hi, w_lo = sem("w_hi"), sem("w_lo")
        b_cur, w_cur = sem("b_cur"), sem("w_cur")
        xt_in, aux_in = sem("xt_in"), sem("aux_in")
        x_done = sem("x_done")
        x_hi, x_lo = sem("x_hi"), sem("x_lo")
        m1_done, g_act, g_hi, g_lo = sem("m1_done"), sem("g_act"), sem("g_hi"), sem("g_lo")
        m2_done, y_act, yt_done, y_sc = sem("m2_done"), sem("y_act"), sem("yt_done"), sem("y_sc")
        added = sem("added")
        y_free = sem("y_free")
        dma_sems = [*xa_in, *xr_in, *mb_in, *gb_in, *x1_out, *scattered, added, aux_in, xt_in, st_in]
        clear = sem("clear")

        L1A, L1B, L2A, L2B, RA, RB, RC = 9, 4, 9, 3, 18, 6, 6
        N_TAB = 10

        block = ctx.enter_context(nc.Block())

        def phase_over(eng):
            eng.wait_ge(over, 4)

        def tile_range(eng, e):
            def load(col, low, high):
                at = tab[0:1, col:col + 1] if isinstance(col, int) else tab[0:1, bass.ds(col, 1)]
                return eng.value_load(at, min_val=low, max_val=high)
            return load(e + 0, 0, TILES - 1), load(e + 1, 1, TILES), load(e + 9, 0, E * CAP)

        def wait_alone(eng, *waits):
            for sm, n in waits:
                (eng.wait_ge if any(sm is d for d in dma_sems) else lambda *w: wait(eng, *w))(sm, n)
            eng.sem_inc(passed, 1)

        @block.sync
        def _(sp):
            for dst, src in (
                (c_s[:, :], c),
                (wmod_s[:, :, :], wmod.rearrange("(j p) n -> p j n", p=P)),
                (wq_s[:, :, :], Wq.rearrange("(j p) h -> p j h", p=P)),
                (wk_s[:, :, :], Wk.rearrange("(j p) h -> p j h", p=P)),
                (wv_s[:, :, :], Wv.rearrange("(j p) h -> p j h", p=P)),
                (gw[:, :, :], gate_w.rearrange("(j p) e -> p j e", p=P)),
                (rows80[0:E * KF, :], b1.rearrange("e (j p) -> (e j) p", p=P)),
                (rows80[E * KF:E * (KF + KD), :], b2.rearrange("e (j p) -> (e j) p", p=P)),
            ):
                sp.dma_start(dst, src).then_inc(w_in, 16)
            for i in range(NB):
                sp.dma_start(gbias[:, i, :], gate_b.partition_broadcast(P)).then_inc(w_in, 16)

            def at(ap, v):
                return ap[bass.ds(v, 1)]

            def load_xa(b):
                sp.dma_start(xa[b.half][:, :, :], at(xb, b.val).rearrange("a p i d -> p (a i) d")) \
                  .then_inc(xa_in[b.half], 16)

            def load_stage(e):
                sp.dma_start(stage1[:, :, :], at(w1, e).rearrange("a (j p) f -> p (a j) f", p=P)).then_inc(st_in, 16)
                sp.dma_start(stage2[:, :, :], at(w2, e).rearrange("a (j p) d -> p (a j) d", p=P)).then_inc(st_in, 16)

            first = Batch(0, 0, 0)
            load_xa(first)
            load_xa(first.next())
            wait(sp, setup_dve, SETUP_MODS)
            sp.dma_start(modd, mods[:, :, :].rearrange("b m d -> b (m d)")).then_inc(mod_out, 16)
            load_stage(0)
            sp.wait_ge(mod_out, 16)

            def load_batch(b):
                sp.dma_start(xr[b.half][:, :, :], at(xb, b.val).rearrange("a p i d -> p (a i) d")) \
                  .then_inc(xr_in[b.half], 16)
                sp.dma_start(mb[b.half][:, :, :].rearrange("p m d -> p (m d)"),
                             at(modd, b.val)[:, 2 * D:5 * D].rearrange("a d -> (a d)").partition_broadcast(P)).then_inc(mb_in[b.half], 16)

            def load_gb(b):
                sp.dma_start(rows[:, b.half * NB:(b.half + 1) * NB, GB:GB + D],
                             at(modd, b.val)[:, 5 * D:6 * D].rearrange("a d -> (a d)").partition_broadcast(P)
                             .unsqueeze(1).to_broadcast([P, NB, D])).then_inc(gb_in[b.half], 16)

            def iteration(k, a, b, g):
                if k is None:
                    load_batch(a)
                    load_gb(a.next())
                    wait(sp, xn_ready, NB)
                    load_xa(a.next().next())
                    return
                if there(k, 3):
                    wait(sp, xn_ready, NB * (k.val + 2))
                    load_xa(k.next().next().next())
                if g is not None:
                    wait(sp, rows_free, g.val)
                    load_gb(g)
                if a is not None:
                    if g is not None:
                        wait(sp, h2_ready, NB * (g.val + 1))
                        sp.wait_ge(x1_out[g.half], 16 * (g.pair + 1))
                    load_batch(a)
                if b is not None:
                    wait(sp, x1_ready, NB * (b.val + 1))
                    sp.dma_start(at(outb, b.val).rearrange("a p i d -> p (a i) d"), xr[b.half][:, :, :]) \
                      .then_inc(x1_out[b.half], 16)

            over_batches(sp, iteration)
            wait(sp, w_lo, 2)
            load_stage(1)
            phase_over(sp)
            for half in range(2):
                sp.wait_ge(x1_out[half], 16 * (B // 2))
                sp.wait_ge(scattered[half], 16 * 2 * NB * (B // 2 + half))
            with sp.Fori(0, E) as e:
                end = sp.value_load(tab[0:1, bass.ds(e + 17, 1)], min_val=0, max_val=E * CAP - TT)
                sp.dma_start(lists[bass.ds(end, TT), :].rearrange("(s p) c -> p s c", p=P), pad[:, :, :]) \
                  .then_inc(pad_out, 16)
            sp.wait_ge(pad_out, 16 * E)

            def load_xt(row):
                sp.dma_start(xt[:, :, :], lists[bass.ds(row, TT), 0:D].rearrange("(s p) d -> p s d", p=P)) \
                  .then_inc(xt_in, 16)

            def expert(e, half, later):
                lo, hi, base = tile_range(sp, e)
                with sp.Fori(lo, hi) as g:
                    row = nc.s_assert_within(sp.snap(g * TT + base), 0, E * CAP - TT,
                                             skip_runtime_bounds_check_because="a list's tiles lie within it")
                    wait(sp, x_done, g)
                    load_xt(row)
                if later == 2:
                    wait(sp, w_lo, 2 * e + 4)
                    load_stage(e + 2)

            over_experts(sp, expert)
            total = sp.value_load(tab[0:1, E:E + 1], min_val=E, max_val=TILES)
            wait(sp, x_done, total)
            load_xt(0)

        @block.gpsimd
        def _(pool):
            start(pool, h_lo, x1_ready, w_lo, rows_free, y_free)
            pool.memset(ident[:, :], 0.0).then_inc(consts, 1)
            pool.memset(maskb[:, :], 0.0).then_inc(consts, 1)
            pool.memset(identb[:, :], 0.0).then_inc(consts, 1)
            pool.memset(trib[:, :], 0.0).then_inc(consts, 1)
            pool.memset(onesb[:, :], 1.0).then_inc(consts, 1)
            pool.wait_ge(consts, 5)
            pool.affine_select(out=ident[:, :], in_=ident[:, :], compare_op=ALU.not_equal, fill=1.0,
                               base=0, pattern=[[-1, P]], channel_multiplier=1).then_inc(consts, 1)
            pool.affine_select(out=identb[:, :], in_=identb[:, :], compare_op=ALU.not_equal, fill=1.0,
                               base=0, pattern=[[-1, P]], channel_multiplier=1).then_inc(consts, 1)
            pool.affine_select(out=maskb[:, :], in_=maskb[:, :], compare_op=ALU.is_ge, fill=MASKED,
                               base=0, pattern=[[-1, P]], channel_multiplier=1).then_inc(consts, 1)
            pool.affine_select(out=trib[:, :], in_=trib[:, :], compare_op=ALU.is_ge, fill=1.0,
                               base=0, pattern=[[-1, P]], channel_multiplier=1).then_inc(consts, 1)
            pool.iota(iota8[:, :, :], [[0, NB], [1, E]], base=0, channel_multiplier=0,
                      allow_small_or_imprecise_dtypes=True).then_inc(iotas, 1)
            pool.iota(ecap[:, :, :], [[0, NB], [1, E]], base=0, channel_multiplier=0,
                      allow_small_or_imprecise_dtypes=True).then_inc(iotas, 1)
            pool.memset(rows[:, :, RW:ROW], 0.0).then_inc(iotas, 1)
            pool.memset(pad[:, :, :], 0.0).then_inc(iotas, 1)
            pool.memset(rows[:, NB:2 * NB, 0:D], 0.0).then_inc(iotas, 1)
            pool.memset(slots[1][:, :, :], E * CAP).then_inc(iotas, 1)
            pool.wait_ge(iotas, 6)
            pool.iota(numbers[:, :], [[P, 2 * NB]], base=-2 * S, channel_multiplier=1).then_inc(iotas, 1)
            pool.iota(pad[:, :, :].bitcast(I32)[:, :, ID], [[0, TB]], base=FAR, channel_multiplier=0).then_inc(iotas, 1)
            pool.tensor_scalar(ecap[:, :, :], ecap[:, :, :], float(CAP), 0.0, ALU.mult, ALU.add).then_inc(iotas, 1)

            def split_rest(e, half):
                wait(pool, w_hi, 2 * (e + 1))
                pool.tensor_tensor(w1l[half][:, :, :], stage1[:, :, :], w1h[half][:, :, :].bitcast(F32),
                                   ALU.subtract).then_inc(w_lo, 1)
                pool.tensor_tensor(w2l[half][:, :, :], stage2[:, :, :], w2h[half][:, :, :].bitcast(F32),
                                   ALU.subtract).then_inc(w_lo, 1)

            def hT_rest(b):
                wait(pool, h_hi, KD * (b.val + 1))
                wait(pool, h_full, KD * (b.val + 1))
                wait(pool, s_done, NB * (b.val - 1))
                pool.tensor_tensor(hl[b.half][:, :, :], hf[:, :, :], hh[b.half][:, :, :].bitcast(F32),
                                   ALU.subtract).then_inc(h_lo, 1)

            def residual(b, i):
                wait(pool, o_scaled, NB * b.val + i + 1)
                if i == 0:
                    pool.wait_ge(xr_in[b.half], 16 * (b.pair + 1))
                pool.tensor_tensor(xr[b.half][:, i, :], xr[b.half][:, i, :], ob[:, i, :], ALU.add) \
                    .then_inc(x1_ready, 1)

            def scatter_begin(b):
                wait_alone(pool, (rc_s, RC * (b.val + 1)), (rb_s, RB * (b.val + 1)),
                           (h2_ready, NB * (b.val + 1)))
                wait_alone(pool, (gb_in[b.half], 16 * (b.pair + 1 + b.half)))

            def scatter(b, i):
                for pick in range(2):
                    pool.indirect_dma_start(
                        lists, bass.IndirectOffsetOnAxis(ap=slots[b.half][:, pick, i:i + 1], axis=0),
                        rows[:, b.half * NB + i, :], None, bounds_check=E * CAP - 1, oob_is_err=False) \
                        .then_inc(scattered[b.half], 16)

            def iteration(k, a, b, g):
                if k is None:
                    hT_rest(a)
                    split_rest(0, 0)
                    return
                gone = g.prev() if g is not None else None
                if gone is not None:
                    scatter_begin(gone)
                    scatter(gone, 0)
                    scatter(gone, 1)
                if a is not None:
                    hT_rest(a)
                for i in range(NB):
                    if b is not None:
                        residual(b, i)
                    if gone is not None and i < 2:
                        scatter(gone, 2 + i)
                if gone is not None:
                    wait_alone(pool, (scattered[gone.half], 16 * 2 * NB * (gone.pair + 1 + gone.half)))
                    pool.sem_inc(rows_free, 1)

            over_batches(pool, iteration)
            last = Batch(B - 1, (B - 1) % 2, (B - 1) // 2)
            scatter_begin(last)
            for i in range(NB):
                scatter(last, i)
            for half in range(2):
                pool.wait_ge(scattered[half], 16 * 2 * NB * (B // 2 + half))
            pool.engine_nop().then_inc(over, 1)
            phase_over(pool)
            pool.wait_ge(clear, 5)
            pool.wait_ge(pad_out, 16 * E)
            for half in range(2):
                pool.wait_ge(x1_out[half], 16 * (B // 2))

            def add_rows(g):
                wait_alone(pool, (y_sc, 2 * g + 2))
                for s in range(TB):
                    pool.indirect_dma_start(
                        out_rows, bass.IndirectOffsetOnAxis(ap=aux_i[:, s, ID - D:ID - D + 1], axis=0),
                        ysc[:, s, :], None, compute_op=ALU.add, bounds_check=NT - 1, oob_is_err=False) \
                        .then_inc(added, 16)
                wait_alone(pool, (added, 32 * g + 32))
                pool.sem_inc(y_free, 1)

            def expert(e, half, later):
                lo, hi, base = tile_range(pool, e)
                if later:
                    wait(pool, m2_done, lo)
                    split_rest(e + 1, 1 - half)
                with pool.Fori(lo, hi) as g:
                    row = nc.s_assert_within(pool.snap(g * TT + base), 0, E * CAP - TT,
                                             skip_runtime_bounds_check_because="a list's tiles lie within it")
                    add_rows(g)
                    pool.dma_start(aux[:, :, :], lists[bass.ds(row, TT), D:ROW]
                                   .rearrange("(s p) d -> p s d", p=P)).then_inc(aux_in, 16)

            over_experts(pool, expert)
            total = pool.value_load(tab[0:1, E:E + 1], min_val=E, max_val=TILES)
            add_rows(total)

        @block.scalar
        def _(act):
            start(act, xn_ready, h_hi, h_full, q_hi, v_hi, p_exp, pt_hi, g_full, el_done, l1_act, l2_act, x_hi, g_act, y_act)
            act.preload_act_table_set("natural_log_exp_and_others")
            wait(act, setup_dve, 1)
            act.activation(ecT[:, :, :], cT[:, :, :], ACT.Exp, scale=-1.0).then_inc(setup_act, 1)

            def seed(b, sem_in, per, buf, sem_out):
                wait(act, sem_in, per * (b.val + 1))
                act.activation(buf[:, 1, :], buf[:, 0, :], ACT.Ln, bias=0.0).then_inc(sem_out, 1)
                wait(act, sem_out, 2 * b.val + 1)
                act.activation(buf[:, 2, :], buf[:, 1, :], ACT.Exp, scale=-0.5).then_inc(sem_out, 1)

            def normalise(b):
                wait(act, l1b, L1B * (b.val + 1))
                act.wait_ge(xa_in[b.half], 16 * (b.pair + 1))
                wait(act, t_done, b.val - 1)
                for i in range(NB):
                    act.activation(xn[b.half][:, i, :], xa[b.half][:, i, :], ACT.Identity,
                                   bias=mean1[:, i:i + 1], scale=r1[:, i:i + 1]).then_inc(xn_ready, 1)

            def hT(b):
                wait(act, mt_ready, b.val + 1)
                wait(act, t_done, b.val + 1)
                wait(act, h_lo, b.val)
                wait(act, s_done, NB * (b.val - 1))
                for j in range(KD):
                    sa, ca = mt[b.half][:, j:j + 1], mt[b.half][:, KD + j:KD + j + 1]
                    act.activation(hh[b.half][:, j, :], ps[:, BANK_T + j, :], ACT.Identity, bias=sa, scale=ca) \
                       .then_inc(h_hi, 1)
                    act.activation(hf[:, j, :], ps[:, BANK_T + j, :], ACT.Identity, bias=sa, scale=ca) \
                       .then_inc(h_full, 1)

            def exps(b, i):
                wait(act, neg_max, NB * b.val + i + 1)
                wait(act, pt_done, NB * b.val + i - 1)
                act.activation(pr[i % 2][:, 0:(i + 1) * P], ps[:, BANK_S + i % 2, 0:(i + 1) * P], ACT.Exp,
                               bias=nmax[:, i:i + 1], accum_out=rsum[:, i:i + 1]).then_inc(p_exp, 1)

            def probs_hi(b, i):
                wait(act, pt_done, NB * b.val + i + 1)
                wait(act, o_done, NB * b.val + i - 1)
                act.activation(pth[i % 2][:, 0:i + 1, :],
                               ps[:, BANK_P, 0:(i + 1) * P].rearrange("p (j q) -> p j q", q=P),
                               ACT.Copy).then_inc(pt_hi, 1)

            def queries_hi(b, m):
                wait(act, q_done, KD * b.val + m + 1)
                wait(act, s_done, NB * (b.val - 1))
                act.activation(qh[b.half][:, m, :], ps[:, BANK_QA + m, :], ACT.Copy).then_inc(q_hi, 1)

            def values_hi(b, p):
                wait(act, v_done, 2 * b.val + p + 1)
                wait(act, o_done, NB * (b.val - 1))
                act.activation(vh[b.half][:, 2 * p:2 * p + 2, :],
                               ps[:, BANK_QA + p, :].rearrange("p (i d) -> p i d", i=2), ACT.Copy).then_inc(v_hi, 1)

            def h2T(b):
                wait(act, gt_done, b.val + 1)
                wait(act, lg_done, b.val)
                for j in range(KD):
                    act.activation(h2f[:, j, :], ps[:, BANK_T + j, :], ACT.Copy).then_inc(g_full, 1)

            def exp_gap(b):
                wait(act, ra_s, RA * (b.val + 1))
                wait(act, rb_s, RB * b.val)
                act.activation(el[:, :], dl[:, :], ACT.Exp).then_inc(el_done, 1)

            def iteration(k, a, b, g):
                if k is None:
                    seed(a, l1a, L1A, ln1, l1_act)
                    normalise(a)
                    seed(a.next(), l1a, L1A, ln1, l1_act)
                    hT(a)
                    normalise(a.next())
                    for m in range(KD):
                        queries_hi(a, m)
                    for p in range(2):
                        values_hi(a, p)
                    return
                if b is not None:
                    exps(b, 0)
                    exps(b, 1)
                    probs_hi(b, 0)
                if g is not None:
                    seed(g, l2a, L2A, ln2, l2_act)
                if a is not None:
                    hT(a)
                if b is not None:
                    exps(b, 2)
                    probs_hi(b, 1)
                    exps(b, 3)
                if a is not None:
                    queries_hi(a, 0)
                if b is not None:
                    probs_hi(b, 2)
                if there(a, 1):
                    seed(a.next(), l1a, L1A, ln1, l1_act)
                if g is not None:
                    h2T(g)
                if a is not None:
                    queries_hi(a, 1)
                if there(a, 1):
                    normalise(a.next())
                if b is not None:
                    probs_hi(b, 3)
                if a is not None:
                    values_hi(a, 0)
                    values_hi(a, 1)
                if g is not None:
                    exp_gap(g)

            over_batches(act, iteration)
            act.preload_act_table_set("gelu_and_others")
            wait(act, el_done, B)
            act.sem_inc(over, 1)
            phase_over(act)

            def tokens_hi(n):
                wait(act, x_done, n)
                act.activation(xth[:, :, :], ps[:, BANK_X, :].rearrange("p (j t) -> p j t", j=KD), ACT.Copy) \
                   .then_inc(x_hi, 1)

            tokens_hi(1)

            def expert(e, half, later):
                lo, hi, base = tile_range(act, e)
                wait(act, b_cur, e + 1)
                with act.Fori(lo, hi) as g:
                    for j in range(KF):
                        wait(act, m1_done, KF * g + j + 1)
                        act.activation(gf[:, j, :], ps[:, BANK_H + j % 4, 0:TT], ACT.Gelu,
                                       bias=bcur[half][:, j:j + 1]).then_inc(g_act, 1)
                    tokens_hi(g + 2)
                    wait(act, m2_done, g + 1)
                    wait(act, yt_done, g + 1)
                    for j in range(KD):
                        act.activation(yT[:, j, :], ps[:, BANK_Y + j, 0:TT], ACT.Identity,
                                       bias=bcur[half][:, KF + j:KF + j + 1]).then_inc(y_act, 1)

            over_experts(act, expert)

        @block.vector
        def _(dve):
            start(dve, setup_dve, tab_s, mt_ready, l1a, l1b, l2a, l2b, q_lo, v_lo, neg_max, pt_lo, r_inv, o_scaled,
                       h2_mid, h2_ready, lg_read, ra_s, rb_s, rc_s, ps_read, w_hi, b_cur, w_cur, x_lo, g_hi,
                       g_lo, y_sc)
            ch = Chain(dve, setup_dve, 64, 0)
            dve.wait_ge(consts, 9)
            dve.wait_ge(setup_pe, 1)
            ch.step(dve.tensor_copy(cT[:, :, :], ps[:, 0, 0:KD * B].rearrange("p (j b) -> p j b", j=KD)))
            dve.wait_ge(setup_act, 1)
            ch.step(dve.tensor_scalar(ecT[:, :, :], ecT[:, :, :], 1.0, None, ALU.add))
            ch.done()
            ch.step(dve.reciprocal(ecT[:, :, :], ecT[:, :, :]))
            ch.done()
            ch.step(dve.tensor_tensor(cT[:, :, :], cT[:, :, :], ecT[:, :, :], ALU.mult))
            assert ch.n == SETUP_SILU
            dve.wait_ge(setup_pe, 2)
            ch.step(dve.tensor_copy(mods[:, :, :].rearrange("b m d -> b (m d)"),
                                    ps[0:B, 3:6, :].rearrange("b m d -> b (m d)")))
            for n in (1, 4):
                ch.done()
                ch.step(dve.tensor_scalar(mods[:, n, :], mods[:, n, :], 1.0, None, ALU.add))
            for n in (2, 5):
                gate = mods[:, n, :]
                ch.done()
                ch.step(dve.scalar_tensor_tensor(mtmp[:, :], gate, -1.0, gate, ALU.mult, ALU.max))
                ch.done()
                ch.step(dve.tensor_scalar(mtmp[:, :], mtmp[:, :], 0.25, None, ALU.max))
                ch.step(dve.tensor_scalar(mtmp2[:, :], gate, 0.0, 2.0, ALU.is_ge, ALU.mult))
                ch.done()
                ch.step(dve.scalar_tensor_tensor(gate, mtmp2[:, :], -1.0, mtmp[:, :], ALU.add, ALU.mult))
            assert ch.n == SETUP_MODS, ch.n
            dve.wait_ge(setup_pe, 3)
            ch.step(dve.tensor_copy(modT[:, :, :], ps[:, 6, 0:4 * B].rearrange("p (m b) -> p m b", b=B)))
            dve.wait_ge(setup_pe, 4)
            m_ps = ps[:, 2, :].rearrange("p (j h) -> p j h", j=KD)
            ch.step(dve.tensor_scalar(mh[:, :, :], m_ps, 1.0 / 16, None, ALU.mult))
            ch.done()
            ch.step(dve.scalar_tensor_tensor(ml[:, :, :], m_ps, 1.0 / 16, mh[:, :, :].bitcast(F32),
                                             ALU.mult, ALU.subtract))
            wv_ps = ps[:, 1, :].rearrange("p (j o) -> p j o", j=KD)
            ch.step(dve.tensor_copy(wvh[:, :, :], wv_ps))
            ch.done()
            ch.step(dve.tensor_tensor(wvl[:, :, :], wv_ps, wvh[:, :, :].bitcast(F32), ALU.subtract))
            ch.step(dve.tensor_copy(biasT[:, :], ps[:, 0, 16:16 + E * (KF + KD)]))
            ch.step(dve.memset(before[:, NB, :], 0.0))
            ch.step(dve.memset(unit[:, :], 1.0))
            ch.done()
            assert ch.n == SETUP_ALL, ch.n
            dve.wait_ge(iotas, 9)

            def prepare(e, half):
                dve.tensor_scalar(bcur[half][:, 0:KF], biasT[:, bass.ds(e * KF, KF)], 0.0, None, ALU.add)
                dve.tensor_scalar(bcur[half][:, KF:KF + KD], biasT[:, bass.ds(e * KD + E * KF, KD)], 0.0, None,
                                  ALU.add).then_inc(b_cur, 1)
                dve.wait_ge(st_in, 32 * (e + 1))
                dve.tensor_copy(w1h[half][:, :, :], stage1[:, :, :]).then_inc(w_hi, 1)
                dve.tensor_copy(w2h[half][:, :, :], stage2[:, :, :]).then_inc(w_hi, 1)

            def spread(b, xin, st, mv, ln, chain):
                for i in range(NB):
                    chain.step(dve.bn_stats(st[:, i, :], xin[b.half][:, i, :]))
                wait_alone(dve, chain.so_far())
                for i in range(NB):
                    chain.step(dve.bn_aggr(mv[:, i, :], st[:, i, :]))
                chain.done()
                chain.step(dve.tensor_scalar(ln[:, 0, :], mv[:, :, 1], EPS, None, ALU.add))

            def refine(ln, r, chain):
                chain.step(dve.tensor_tensor(ln[:, 3, :], ln[:, 2, :], ln[:, 2, :], ALU.mult))
                chain.done()
                chain.step(dve.scalar_tensor_tensor(ln[:, 3, :], ln[:, 3, :], -0.5, ln[:, 0, :], ALU.mult, ALU.mult))
                chain.done()
                chain.step(dve.scalar_tensor_tensor(r[:, :], ln[:, 3, :], 1.5, ln[:, 2, :], ALU.add, ALU.mult))

            def norm1_a(b):
                wait(dve, xn_ready, NB * b.val)
                dve.wait_ge(xa_in[b.half], 16 * (b.pair + 1))
                spread(b, xa, st1, mv1, ln1, Chain(dve, l1a, L1A, b.val))

            def norm1_b(b):
                wait(dve, l1_act, 2 * b.val + 2)
                chain = Chain(dve, l1b, L1B, b.val)
                refine(ln1, r1, chain)
                chain.done()
                chain.step(dve.scalar_tensor_tensor(mean1[:, :], mv1[:, :, 0], -1.0, r1[:, :], ALU.mult, ALU.mult))

            def mod_columns(b):
                wait(dve, h_full, KD * (b.val - 1))
                src = modT[:, :, b.val:b.val + 1] if isinstance(b.val, int) else modT[:, :, bass.ds(b.val, 1)]
                dve.tensor_scalar(mt[b.half][:, :].unsqueeze(2), src, 0.0, None, ALU.add).then_inc(mt_ready, 1)

            def queries_lo(b, m):
                wait(dve, q_hi, KD * b.val + m + 1)
                dve.tensor_tensor(ql[b.half][:, m, :], ps[:, BANK_QA + m, :], qh[b.half][:, m, :].bitcast(F32),
                                  ALU.subtract).then_inc(q_lo, 1)

            def values_lo(b, p):
                wait(dve, v_hi, 2 * b.val + p + 1)
                dve.tensor_tensor(vl[b.half][:, 2 * p:2 * p + 2, :],
                                  ps[:, BANK_QA + p, :].rearrange("p (i d) -> p i d", i=2),
                                  vh[b.half][:, 2 * p:2 * p + 2, :].bitcast(F32), ALU.subtract).then_inc(v_lo, 1)

            def row_max(b, i):
                wait(dve, s_done, NB * b.val + i + 1)
                dve.tensor_reduce(nmax[:, i:i + 1], ps[:, BANK_S + i % 2, 0:(i + 1) * P], AX.X, ALU.max,
                                  negate=True).then_inc(neg_max, 1)

            def probs_lo(b, i):
                wait(dve, pt_hi, NB * b.val + i + 1)
                dve.tensor_tensor(ptl[i % 2][:, 0:i + 1, :],
                                  ps[:, BANK_P, 0:(i + 1) * P].rearrange("p (j q) -> p j q", q=P),
                                  pth[i % 2][:, 0:i + 1, :].bitcast(F32), ALU.subtract).then_inc(pt_lo, 1)

            def scale_out(b, i):
                wait(dve, o_done, NB * b.val + i + 1)
                if i == 0:
                    dve.wait_ge(mb_in[b.half], 16 * (b.pair + 1))
                dve.reciprocal(rinv[:, i:i + 1], rsum[:, i:i + 1]).then_inc(r_inv, 1)
                wait(dve, r_inv, NB * b.val + i + 1)
                wait(dve, x1_ready, NB * (b.val - 1) + i + 1)
                dve.scalar_tensor_tensor(ob[:, i, :], ps[:, BANK_O, (i % 2) * D:(i % 2 + 1) * D], rinv[:, i:i + 1],
                                         mb[b.half][:, 0, :], ALU.mult, ALU.mult).then_inc(o_scaled, 1)

            def norm2_a(b):
                wait(dve, x1_ready, NB * (b.val + 1))
                spread(b, xr, st2, mv2, ln2, Chain(dve, l2a, L2A, b.val))

            def norm2_b(b):
                wait(dve, l2_act, 2 * b.val + 2)
                chain = Chain(dve, l2b, L2B, b.val)
                refine(ln2, r2, chain)
                chain.done()
                wait(dve, rows_free, b.val)
                for i in range(NB):
                    row = rows[:, b.half * NB + i, 0:D]
                    dve.scalar_tensor_tensor(row, xr[b.half][:, i, :], mv2[:, i, 0:1], mb[b.half][:, 2, :],
                                             ALU.subtract, ALU.mult).then_inc(h2_mid, 1)
                for i in range(NB):
                    row = rows[:, b.half * NB + i, 0:D]
                    wait(dve, h2_mid, NB * b.val + i + 1)
                    dve.scalar_tensor_tensor(row, row, r2[:, i:i + 1], mb[b.half][:, 1, :],
                                             ALU.mult, ALU.add).then_inc(h2_ready, 1)

            def route_a(b):
                wait(dve, lg_done, b.val + 1)
                chain = Chain(dve, ra_s, RA, b.val)
                dve.tensor_tensor(lg[:, :, :], ps[:, BANK_QB, 0:NB * E].rearrange("p (i e) -> p i e", e=E),
                                  gbias[:, :, :], ALU.add).then_inc(lg_read, 1)
                wait_alone(dve, (lg_read, b.val + 1))
                for i in range(NB):
                    chain.step(dve.max(mx[:, i, :], lg[:, i, :]))
                wait_alone(dve, chain.so_far())
                for i in range(NB):
                    chain.step(dve.max_index(mxi[:, i, :], mx[:, i, :], lg[:, i, :]))
                chain.done()
                chain.step(dve.tensor_copy(idxf[:, :, :], mxi[:, :, 0:2]))
                chain.step(dve.tensor_tensor(dl[:, :], mx[:, :, 1], mx[:, :, 0], ALU.subtract))
                chain.done()
                chain.step(dve.tensor_tensor(o1[:, :, :], iota8[:, :, :],
                                             idxf[:, :, 0:1].to_broadcast([P, NB, E]), ALU.is_equal))
                chain.step(dve.tensor_tensor(o2[:, :, :], iota8[:, :, :],
                                             idxf[:, :, 1:2].to_broadcast([P, NB, E]), ALU.is_equal))
                chain.done()
                wait(dve, ps_done, b.val)
                chain.step(dve.tensor_tensor(picks[:, :, :], o1[:, :, :], o2[:, :, :], ALU.add))
                chain.step(dve.tensor_copy(before[:, 0, :], before[:, NB, :]))
                for i in range(NB):
                    chain.done()
                    chain.step(dve.tensor_tensor(before[:, i + 1, :], before[:, i, :], picks[:, i, :], ALU.add))

            def route_b(b):
                chain = Chain(dve, rb_s, RB, b.val)
                wait(dve, el_done, b.val + 1)
                chain.step(dve.tensor_scalar(wt[:, 0, :], el[:, :], 1.0, None, ALU.add))
                chain.done()
                chain.step(dve.reciprocal(wt[:, 1, :], wt[:, 0, :]))
                chain.done()
                chain.step(dve.tensor_tensor(wt[:, 2, :], wt[:, 1, :], el[:, :], ALU.mult))
                chain.done()
                chain.step(dve.tensor_tensor(ra[:, :, :], o1[:, :, :],
                                             wt[:, 1, :].unsqueeze(2).to_broadcast([P, NB, E]), ALU.mult))
                chain.step(dve.tensor_tensor(rb[:, :, :], o2[:, :, :],
                                             wt[:, 2, :].unsqueeze(2).to_broadcast([P, NB, E]), ALU.mult))
                chain.done()
                chain.step(dve.tensor_tensor(rows[:, b.half * NB:(b.half + 1) * NB, RW:RW + E],
                                             ra[:, :, :], rb[:, :, :], ALU.add))

            def route_c(b):
                chain = Chain(dve, rc_s, RC, b.val)
                wait(dve, ps_done, b.val + 1)
                dve.tensor_tensor(pos[:, :, :], ps[:, BANK_QA, 0:NB * E].rearrange("p (i e) -> p i e", e=E),
                                  ecap[:, :, :], ALU.add).then_inc(ps_read, 1)
                wait(dve, ps_read, b.val + 1)
                chain.step(dve.tensor_tensor(pt1[:, 0, :, :], pos[:, :, :], o1[:, :, :], ALU.mult))
                chain.step(dve.tensor_tensor(pt1[:, 1, :, :], pos[:, :, :], o2[:, :, :], ALU.mult))
                chain.done()
                chain.step(dve.tensor_reduce(slotf[:, :, :], pt1[:, :, :, :], AX.X, ALU.add))
                chain.done()
                chain.step(dve.tensor_copy(slots[b.half][:, :, :], slotf[:, :, :]))
                own = slice(b.half * NB, (b.half + 1) * NB)
                chain.step(dve.tensor_scalar(numbers[:, own], numbers[:, own], float(2 * S), None, ALU.add))
                chain.done()
                chain.step(dve.tensor_copy(rows_i[:, own, ID], numbers[:, own]))

            def iteration(k, a, b, g):
                more = there(a, 1)
                if k is None:
                    norm1_a(a)
                    mod_columns(a)
                    norm1_b(a)
                    norm1_a(a.next())
                    norm1_b(a.next())
                    for m in range(KD):
                        queries_lo(a, m)
                    for p in range(2):
                        values_lo(a, p)
                    prepare(0, 0)
                    return
                if a is not None:
                    mod_columns(a)
                if b is not None:
                    row_max(b, 0)
                    row_max(b, 1)
                if g is not None:
                    norm2_a(g)
                if b is not None:
                    probs_lo(b, 0)
                    row_max(b, 2)
                    probs_lo(b, 1)
                    scale_out(b, 0)
                if g is not None:
                    norm2_b(g)
                if b is not None:
                    row_max(b, 3)
                    scale_out(b, 1)
                if more:
                    norm1_a(a.next())
                if a is not None:
                    queries_lo(a, 0)
                if b is not None:
                    probs_lo(b, 2)
                if more:
                    norm1_b(a.next())
                if a is not None:
                    queries_lo(a, 1)
                if b is not None:
                    scale_out(b, 2)
                    probs_lo(b, 3)
                if a is not None:
                    values_lo(a, 0)
                if g is not None:
                    route_a(g)
                if a is not None:
                    values_lo(a, 1)
                if b is not None:
                    scale_out(b, 3)
                if g is not None:
                    route_b(g)
                    route_c(g)

            over_batches(dve, iteration)

            tc = Chain(dve, tab_s, N_TAB, 0)
            dve.wait_ge(cnt_done, 1)
            tc.step(dve.tensor_copy(cnt[:, 0, :], ps[0:1, BANK_S, 0:E]))
            tc.done()
            tc.step(dve.tensor_scalar(cnti[:, 0, :], cnt[:, 0, :], float(TT - 1), None, ALU.add))
            tc.step(dve.tensor_tensor(tab[:, 17:17 + E], cnt[:, 0, :], ecap[0:1, 0, :], ALU.add))
            tc.done()
            tc.step(dve.tensor_scalar(cnti[:, 1, :], cnti[:, 0, :], TT.bit_length() - 1, None, ALU.logical_shift_right))
            tc.done()
            tc.step(dve.tensor_scalar(cnt[:, 1, :], cnti[:, 1, :], 1.0, None, ALU.max))
            tc.done()
            tc.step(dve.tensor_tensor_scan(cnt[:, 2, :], unit[:, :], cnt[:, 1, :], 0.0, ALU.mult, ALU.add))
            tc.step(dve.memset(tab[:, 0:1], 0))
            tc.done()
            tc.step(dve.tensor_copy(tab[:, 1:1 + E], cnt[:, 2, :]))
            tc.step(dve.tensor_tensor(cnt[:, 3, :], cnt[:, 2, :], cnt[:, 1, :], ALU.subtract))
            tc.done()
            tc.step(dve.scalar_tensor_tensor(tab[:, 9:9 + E], cnt[:, 3, :], -float(TT), ecap[0:1, 0, :],
                                             ALU.mult, ALU.add))
            tc.done()
            dve.sem_inc(over, 1)
            phase_over(dve)
            dve.memset(yT[:, :, :], 0.0).then_inc(clear, 1)
            dve.memset(aux[:, :, :], 0.0).then_inc(clear, 1)
            dve.memset(wcur[:, :, :], 0.0).then_inc(clear, 1)
            dve.wait_ge(clear, 3)
            for s in range(TB):
                dve.memset(aux_i[:, s, ID - D:ID - D + 1], FAR).then_inc(clear, 1)
            dve.wait_ge(clear, 5)

            def tokens_lo(n):
                wait(dve, x_hi, n)
                dve.tensor_tensor(xtl[:, :, :], ps[:, BANK_X, :].rearrange("p (j t) -> p j t", j=KD),
                                  xth[:, :, :].bitcast(F32), ALU.subtract).then_inc(x_lo, 1)

            tokens_lo(1)

            def weigh_before(g):
                wait(dve, yt_done, g + 1)
                wait(dve, w_cur, g)
                wait(dve, y_free, g)
                for s in range(TB):
                    dve.scalar_tensor_tensor(ysc[:, s, :], ps[:, BANK_YT, s * D:(s + 1) * D], wcur[:, s, :],
                                             aux[:, s, 0:D], ALU.mult, ALU.mult).then_inc(y_sc, 1)

            def expert(e, half, later):
                lo, hi, base = tile_range(dve, e)
                if later:
                    wait(dve, y_act, KD * lo)
                    prepare(e + 1, 1 - half)
                with dve.Fori(lo, hi) as g:
                    for j in range(KF):
                        wait(dve, g_act, KF * g + j + 1)
                        dve.tensor_copy(gh[:, j, :], gf[:, j, :]).then_inc(g_hi, 1)
                        wait(dve, g_hi, KF * g + j + 1)
                        dve.tensor_tensor(gl[:, j, :], gf[:, j, :], gh[:, j, :].bitcast(F32), ALU.subtract) \
                           .then_inc(g_lo, 1)
                        if j == 2:
                            weigh_before(g)
                    tokens_lo(g + 2)
                    dve.wait_ge(aux_in, 16 * g + 16)
                    dve.tensor_scalar(wcur[:, :, :], aux[:, :, bass.ds(e + (RW - D), 1)], 0.0, None, ALU.add) \
                       .then_inc(w_cur, 1)

            over_experts(dve, expert)
            total = dve.value_load(tab[0:1, E:E + 1], min_val=E, max_val=TILES)
            weigh_before(total)

        @block.tensor
        def _(pe):
            start(pe, t_done, q_done, v_done, s_done, pt_done, o_done, gt_done, lg_done, ps_done, x_done,
                      m1_done, m2_done, yt_done)
            def three(out_, wh, wl, xh, xl, start, stop):
                pe.matmul(out_, wh, xh, start=start, stop=False)
                pe.matmul(out_, wh, xl, start=False, stop=False)
                return pe.matmul(out_, wl, xh, start=False, stop=stop)

            pe.wait_ge(consts, 9)
            pe.wait_ge(w_in, 16 * (8 + NB))
            for j in range(KD):
                pe.transpose(ps[:, 0, j * B:(j + 1) * B], c_s[:, j * P:(j + 1) * P], ident[0:B, 0:B])
            rb80 = E * (KF + KD)
            pe.transpose(ps[:, 0, 16:16 + rb80], rows80[:, :], ident[0:rb80, 0:rb80]).then_inc(setup_pe, 1)
            wait(pe, setup_dve, SETUP_SILU)
            for n in range(3):
                for j in range(KD):
                    mm = pe.matmul(ps[0:B, 3 + n, :], cT[:, j, :], wmod_s[:, j, n * 512:(n + 1) * 512],
                                   start=(j == 0), stop=(j == KD - 1))
            mm.then_inc(setup_pe, 1)
            for oj in range(KD):
                for hj in range(KD):
                    pe.transpose(ps[:, 1, hj * D + oj * P:hj * D + (oj + 1) * P], wv_s[:, oj, hj * P:(hj + 1) * P],
                                 ident[:, :])
            for hj in range(KD):
                for oj in range(KD):
                    pe.matmul(ps[:, 2, hj * D:(hj + 1) * D], wq_s[:, oj, hj * P:(hj + 1) * P], wk_s[:, oj, :],
                              start=(oj == 0), stop=(oj == KD - 1))
            wait(pe, setup_dve, SETUP_MODS)
            for n in range(2):
                for j in range(KD):
                    mm = pe.transpose(ps[:, 6, (n * KD + j) * B:(n * KD + j + 1) * B],
                                      mods[:, n, j * P:(j + 1) * P], ident[0:B, 0:B])
            mm.then_inc(setup_pe, 2)
            wait(pe, setup_dve, SETUP_ALL)

            def tokens_T(b):
                wait(pe, xn_ready, NB * (b.val + 1))
                wait(pe, g_full, KD * (b.val - 2))
                for i in range(NB):
                    for j in range(KD):
                        mm = pe.transpose(ps[:, BANK_T + j, i * P:(i + 1) * P],
                                          xn[b.half][:, i, j * P:(j + 1) * P], ident[:, :])
                mm.then_inc(t_done, 1)

            def queries(b, m):
                wait(pe, h_lo, b.val + 1)
                if m == 0:
                    wait(pe, ps_read, b.val - 2)
                    wait(pe, v_lo, 2 * b.val - 1)
                else:
                    wait(pe, v_lo, 2 * b.val)
                    wait(pe, lg_read, b.val - 2)
                for j in range(KD):
                    mm = three(ps[:, BANK_QA + m, :], mh[:, j, m * P:(m + 1) * P], ml[:, j, m * P:(m + 1) * P],
                               hh[b.half][:, j, :], hl[b.half][:, j, :], j == 0, j == KD - 1)
                mm.then_inc(q_done, 1)

            def values(b, p):
                if p == 0:
                    wait(pe, q_lo, KD * b.val + 1)
                else:
                    wait(pe, q_lo, KD * b.val + 2)
                    wait(pe, lg_read, b.val - 1)
                for i in (2 * p, 2 * p + 1):
                    tok = slice(i * P, (i + 1) * P)
                    for j in range(KD):
                        o = ps[:, BANK_QA + p, (i % 2) * D:(i % 2 + 1) * D]
                        pe.matmul(o, hh[b.half][:, j, tok], wvh[:, j, :], start=(j == 0), stop=False)
                        pe.matmul(o, hh[b.half][:, j, tok], wvl[:, j, :], start=False, stop=False)
                        mm = pe.matmul(o, hl[b.half][:, j, tok], wvh[:, j, :], start=False, stop=(j == KD - 1))
                mm.then_inc(v_done, 1)

            def scores(b, i):
                if i == 0:
                    wait(pe, q_lo, KD * (b.val + 1))
                wait(pe, p_exp, NB * b.val + i - 1)
                n = max(2, i + 1) * P
                tok = slice(i * P, (i + 1) * P)
                bank = ps[:, BANK_S + i % 2, :]
                for j in range(KD):
                    q_hi_, q_lo_ = qh[b.half][:, j, tok], ql[b.half][:, j, tok]
                    pe.matmul(bank[:, 0:n], q_hi_, hh[b.half][:, j, 0:n], start=(j == 0), stop=False)
                    if j == 0:
                        pe.matmul(bank[:, tok], identb[:, :], maskb[:, :], start=False, stop=False)
                    pe.matmul(bank[:, 0:n], q_hi_, hl[b.half][:, j, 0:n], start=False, stop=False)
                    mm = pe.matmul(bank[:, 0:n], q_lo_, hh[b.half][:, j, 0:n], start=False, stop=(j == KD - 1))
                mm.then_inc(s_done, 1)

            def probs_T(b, i):
                wait(pe, p_exp, NB * b.val + i + 1)
                wait(pe, pt_lo, NB * b.val + i)
                for j in range(i + 1):
                    mm = pe.transpose(ps[:, BANK_P, j * P:(j + 1) * P], pr[i % 2][:, j * P:(j + 1) * P], ident[:, :])
                mm.then_inc(pt_done, 1)

            def attend(b, i):
                wait(pe, pt_lo, NB * b.val + i + 1)
                if i == 0:
                    wait(pe, v_lo, 2 * (b.val + 1))
                wait(pe, o_scaled, NB * b.val + i)
                o = ps[:, BANK_O, (i % 2) * D:(i % 2 + 1) * D]
                for j in range(i + 1):
                    pe.matmul(o, pth[i % 2][:, j, :], vh[b.half][:, j, :], start=(j == 0), stop=False)
                    pe.matmul(o, pth[i % 2][:, j, :], vl[b.half][:, j, :], start=False, stop=False)
                    mm = pe.matmul(o, ptl[i % 2][:, j, :], vh[b.half][:, j, :], start=False, stop=(j == i))
                mm.then_inc(o_done, 1)

            def h2_T(b):
                wait(pe, h2_ready, NB * (b.val + 1))
                n = b.val + 3
                wait(pe, h_full, KD * (min(n, B) if isinstance(n, int) else n))
                for i in range(NB):
                    for j in range(KD):
                        mm = pe.transpose(ps[:, BANK_T + j, i * P:(i + 1) * P],
                                          rows[:, b.half * NB + i, j * P:(j + 1) * P], ident[:, :])
                mm.then_inc(gt_done, 1)

            def logits(b):
                wait(pe, g_full, KD * (b.val + 1))
                n = b.val + 3
                wait(pe, q_lo, KD * (min(n, B) if isinstance(n, int) else n))
                for i in range(NB):
                    for j in range(KD):
                        mm = pe.matmul(ps[:, BANK_QB, i * E:(i + 1) * E], h2f[:, j, i * P:(i + 1) * P], gw[:, j, :],
                                       start=(j == 0), stop=(j == KD - 1))
                mm.then_inc(lg_done, 1)

            def places(b):
                wait(pe, ra_s, RA * (b.val + 1))
                n = b.val + 3
                wait(pe, v_lo, 2 * (min(n, B) if isinstance(n, int) else n) - 1)
                o = ps[:, BANK_QA, 0:NB * E]
                pe.matmul(o, trib[:, :], picks[:, :, :].rearrange("p i e -> p (i e)"), start=True, stop=False)
                pe.matmul(o, onesb[:, :], before[:, 0:NB, :].rearrange("p i e -> p (i e)"), start=False, stop=True) \
                  .then_inc(ps_done, 1)

            def iteration(k, a, b, g):
                if k is None:
                    tokens_T(a)
                    for m in range(KD):
                        queries(a, m)
                    for p in range(2):
                        values(a, p)
                    return
                if b is not None:
                    scores(b, 0)
                    scores(b, 1)
                if a is not None:
                    tokens_T(a)
                if b is not None:
                    probs_T(b, 0)
                    scores(b, 2)
                    probs_T(b, 1)
                    attend(b, 0)
                    scores(b, 3)
                    attend(b, 1)
                if a is not None:
                    queries(a, 0)
                if b is not None:
                    probs_T(b, 2)
                if g is not None:
                    h2_T(g)
                if a is not None:
                    queries(a, 1)
                if b is not None:
                    attend(b, 2)
                    probs_T(b, 3)
                if a is not None:
                    values(a, 0)
                if g is not None:
                    logits(g)
                if a is not None:
                    values(a, 1)
                if b is not None:
                    attend(b, 3)
                if g is not None:
                    places(g)

            over_batches(pe, iteration)
            pe.matmul(ps[:, BANK_S, 0:E], onesb[:, :], before[:, NB, :], start=True, stop=True).then_inc(cnt_done, 1)
            pe.wait_ge(cnt_done, 1)
            pe.sem_inc(over, 1)
            phase_over(pe)

            def tile_T(n):
                pe.wait_ge(xt_in, 16 * n + 16)
                for s in range(TB):
                    for j in range(KD):
                        mm = pe.transpose(ps[:, BANK_X, j * TT + s * P:j * TT + (s + 1) * P],
                                          xt[:, s, j * P:(j + 1) * P], ident[:, :])
                mm.then_inc(x_done, 1)

            def result_T(g):
                wait(pe, y_act, KD * g)
                wait(pe, y_sc, TB * g)
                for s in range(TB):
                    for j in range(KD):
                        mm = pe.transpose(ps[:, BANK_YT, s * D + j * P:s * D + (j + 1) * P],
                                          yT[:, j, s * P:(s + 1) * P], ident[:, :])
                mm.then_inc(yt_done, 1)

            def up(g, j, half):
                cols = slice(j * P, (j + 1) * P)
                if j == 0:
                    wait(pe, x_lo, g + 1)
                if j >= 4:
                    wait(pe, g_act, KF * g + j - 3)
                for n in range(KD):
                    mm = three(ps[:, BANK_H + j % 4, 0:TT], w1h[half][:, n, cols], w1l[half][:, n, cols],
                               xth[:, n, :], xtl[:, n, :], n == 0, n == KD - 1)
                mm.then_inc(m1_done, 1)

            def down(g, j, half):
                wait(pe, g_lo, KF * g + j + 1)
                for n in range(KD):
                    cols = slice(n * P, (n + 1) * P)
                    mm = three(ps[:, BANK_Y + n, 0:TT], w2h[half][:, j, cols], w2l[half][:, j, cols],
                               gh[:, j, :], gl[:, j, :], j == 0, j == KF - 1)
                if j == KF - 1:
                    mm.then_inc(m2_done, 1)

            tile_T(0)

            def expert(e, half, later):
                lo, hi, base = tile_range(pe, e)
                wait_alone(pe, (w_lo, 2 * e + 2))
                with pe.Fori(lo, hi) as g:
                    for j in range(KF):
                        up(g, j, half)
                        if j == 1:
                            result_T(g)
                        if j >= LAG:
                            down(g, j - LAG, half)
                    tile_T(g + 1)
                    for j in range(KF - LAG, KF):
                        down(g, j, half)

            over_experts(pe, expert)
            total = pe.value_load(tab[0:1, E:E + 1], min_val=E, max_val=TILES)
            result_T(total)


SETUP_SILU = 4
SETUP_MODS = SETUP_SILU + 3 + 8
SETUP_ALL = SETUP_MODS + 8


_INS = ["L0_attn_x", "L0_attn_Wq", "L0_attn_Wk", "L0_attn_Wv", "L0_ffn_gate_w", "L0_ffn_gate_b",
        "L0_ffn_w1", "L0_ffn_b1", "L0_ffn_w2", "L0_ffn_b2", "L0_c", "L0_wmod"]


def kernel(**inputs):
    import numpy as np
    import concourse.bacc as bacc
    from concourse.bass_utils import run_bass_kernel_spmd

    nc = bacc.Bacc("TRN2", target_bir_lowering=False, num_devices=1)
    arrays, args = {}, []
    for name in _INS:
        a = np.ascontiguousarray(inputs[name])
        arrays[f"in_{name}"] = a
        args.append(nc.dram_tensor(f"in_{name}", a.shape, mybir.dt.from_np(a.dtype), kind="ExternalInput").ap())
    args.append(nc.dram_tensor("out_0", (B, S, D), F32, kind="ExternalOutput").ap())
    layer(nc, *args)
    r = run_bass_kernel_spmd(nc, [arrays], core_ids=[0])
    return r.results[0]["out_0"]
```

```python
from contextlib import ExitStack

import concourse.bass as bass
from concourse import mybir
from concourse.alu_op_type import AluOpType as ALU

F32 = mybir.dt.float32
F32R = mybir.dt.float32r
BF16 = mybir.dt.bfloat16
I32 = mybir.dt.int32
U32 = mybir.dt.uint32
ACT = mybir.ActivationFunctionType
AX = mybir.AxisListType

P = 128
B, S, D = 8, 512, 256
NB = S // P
KD = D // P
E, F = 8, 1024
KF = F // P
NT = B * S
TT = 256
TB = TT // P
CAP = NT + TT
TILES = 2 * NT // TT + E
GB, RW, ID, ROW = D, 2 * D, 2 * D + E, 2 * D + 2 * E
AUX = ROW - D
FAR = 1 << 20
EPS = 1e-5
MASKED = -3.0e38
CHUNKS = 4
LAG = 4


class Batch:

    def __init__(self, val, half, pair):
        self.val, self.half, self.pair = val, half, pair

    def next(self):
        return Batch(self.val + 1, 1 - self.half, self.pair + self.half)

    def prev(self):
        return Batch(self.val - 1, 1 - self.half, self.pair - (1 - self.half))


def wait(eng, sem, count):
    if isinstance(count, int) and count <= 0:
        return
    eng.wait_ge(sem, count + 1)


def start(eng, *sems):
    for sem in sems:
        eng.sem_inc(sem, 1)


class Chain:

    def __init__(self, eng, sem, per, times):
        self.eng, self.sem, self.per, self.base, self.n = eng, sem, per, times * per, 0

    def so_far(self):
        return self.sem, self.base + self.n

    def step(self, ins):
        self.n += 1
        assert self.n <= self.per
        ins.then_inc(self.sem, 1)

    def done(self):
        wait(self.eng, *self.so_far())


def over_batches(eng, iteration):
    first = Batch(0, 0, 0)
    iteration(None, first, None, None)
    iteration(first, first.next(), first, None)
    with eng.Fori(0, (B - 4) // 2) as m:
        for k in (Batch(2 * m + 1, 1, m), Batch(2 * m + 2, 0, m + 1)):
            iteration(k, k.next(), k, k.prev())
    for n in range(B - 3, B + 1):
        k = Batch(n, n % 2, n // 2)
        iteration(k, k.next() if n + 1 < B else None, k if n < B else None, k.prev())


def there(b, more=0):
    return b is not None and not (isinstance(b.val, int) and b.val + more >= B)


def over_experts(eng, expert):
    with eng.Fori(0, (E - 2) // 2) as m:
        expert(2 * m, 0, 2)
        expert(2 * m + 1, 1, 2)
    expert(E - 2, 0, 1)
    expert(E - 1, 1, 0)


def layer(nc, x, Wq, Wk, Wv, gate_w, gate_b, w1, b1, w2, b2, c, wmod, out):
    ctx = ExitStack()
    with ctx:
        def sb(name, shape, dt=F32, where=ctx):
            return where.enter_context(nc.sbuf_tensor(name, shape, dt))

        def sem(name):
            return ctx.enter_context(nc.semaphore(name))

        lists = nc.dram_tensor("lists", [E * CAP, ROW], F32).ap()
        modd = nc.dram_tensor("modd", [B, 6 * D], F32).ap()
        xb = x.rearrange("b (i p) d -> b p i d", p=P)
        outb = out.rearrange("b (i p) d -> b p i d", p=P)
        out_rows = out.rearrange("b s d -> (b s) d")

        ident = sb("ident", [P, P])
        pad = sb("pad", [P, TB, ROW])
        rows64 = sb("rows64", [E * KF, P])
        biasT = sb("biasT", [P, E * KF])
        tab = sb("tab", [1, 32], I32)
        stage1 = sb("stage1", [P, KD, F])
        stage2 = sb("stage2", [P, KF, D])
        w1h, w1l, w2h, w2l = [], [], [], []

        def expert_weights(n, where):
            w1h.append(sb(f"w1h{n}", [P, KD, F], F32R, where))
            w1l.append(sb(f"w1l{n}", [P, KD, F], F32R, where))
            w2h.append(sb(f"w2h{n}", [P, KF, D], F32R, where))
            w2l.append(sb(f"w2l{n}", [P, KF, D], F32R, where))

        expert_weights(0, ctx)
        bcur = [sb(f"bcur{n}", [P, KF]) for n in range(2)]
        b2row = [sb(f"b2row{n}", [P, D]) for n in range(2)]

        one = ExitStack()

        def s1(name, shape, dt=F32):
            return sb(name, shape, dt, one)

        with ExitStack() as zero:
            wmod_s = sb("wmod_s", [P, KD, 6 * D], F32, zero)
            wq_s = sb("wq_s", [P, KD, D], F32, zero)
            wk_s = sb("wk_s", [P, KD, D], F32, zero)
            wv_s = sb("wv_s", [P, KD, D], F32, zero)
        batch1 = [s1(f"{name}1", shape, F32R) for name, shape in (
            ("hh", [P, KD, S]), ("hl", [P, KD, S]), ("qh", [P, KD, S]), ("ql", [P, KD, S]),
            ("vh", [P, NB, D]), ("vl", [P, NB, D]))]
        maskb = s1("maskb", [P, P], BF16)
        identb = s1("identb", [P, P], BF16)
        trib = s1("trib", [P, P], BF16)
        onesb = s1("onesb", [P, P], BF16)
        mh = s1("mh", [P, KD, D], F32R)
        ml = s1("ml", [P, KD, D], F32R)
        wvh = s1("wvh", [P, KD, D], F32R)
        wvl = s1("wvl", [P, KD, D], F32R)
        gw = s1("gw", [P, KD, E])
        gbias = s1("gbias", [P, NB, E])
        iota8 = s1("iota8", [P, NB, E])
        ecap = s1("ecap", [P, NB, E])
        c_s = s1("c_s", [B, D])
        cT = s1("cT", [P, KD, B])
        ecT = s1("ecT", [P, KD, B])
        mods = s1("mods", [B, 6, D])
        mtmp = s1("mtmp", [B, D])
        mtmp2 = s1("mtmp2", [B, D])
        modT = s1("modT", [P, 8, B])
        xa = [s1(f"xa{n}", [P, NB, D]) for n in range(2)]
        xr = [s1(f"xr{n}", [P, NB, D]) for n in range(2)]
        mb = [s1(f"mb{n}", [P, 3, D]) for n in range(2)]
        mt = [s1(f"mt{n}", [P, 4]) for n in range(2)]
        mt2 = s1("mt2", [P, 4])
        xn2 = s1("xn2", [P, NB, D])
        mean2 = s1("mean2", [P, NB])
        xn = [s1(f"xn{n}", [P, NB, D]) for n in range(2)]
        st1 = s1("st1", [P, NB, 6])
        mv1 = s1("mv1", [P, NB, 2])
        ln1 = s1("ln1", [P, 4, NB])
        r1 = s1("r1", [P, NB])
        mean1 = s1("mean1", [P, NB])
        st2 = s1("st2", [P, NB, 6])
        mv2 = s1("mv2", [P, NB, 2])
        ln2 = s1("ln2", [P, 4, NB])
        r2 = s1("r2", [P, NB])
        hf = s1("hf", [P, KD, S])
        hh = [s1("hh0", [P, KD, S], F32R), batch1[0]]
        hl = [s1("hl0", [P, KD, S], F32R), batch1[1]]
        qh = [s1("qh0", [P, KD, S], F32R), batch1[2]]
        ql = [s1("ql0", [P, KD, S], F32R), batch1[3]]
        vh = [s1("vh0", [P, NB, D], F32R), batch1[4]]
        vl = [s1("vl0", [P, NB, D], F32R), batch1[5]]
        nmax = s1("nmax", [P, NB])
        rsum = s1("rsum", [P, NB])
        rinv = s1("rinv", [P, NB])
        pr = [s1(f"pr{n}", [P, S]) for n in range(2)]
        pth = [s1(f"pth{n}", [P, NB, P], F32R) for n in range(2)]
        ptl = [s1(f"ptl{n}", [P, NB, P], F32R) for n in range(2)]
        ob = s1("ob", [P, NB, D])
        rows = s1("rows", [P, 2 * NB, ROW])
        rows_i = rows[:, :, :].bitcast(I32)
        h2f = s1("h2f", [P, KD, S])
        lg = s1("lg", [P, NB, E])
        mx = s1("mx", [P, NB, E])
        mxi = s1("mxi", [P, NB, E], U32)
        idxf = s1("idxf", [P, NB, 2])
        o1 = s1("o1", [P, NB, E])
        o2 = s1("o2", [P, NB, E])
        picks = s1("picks", [P, NB, E], BF16)
        before = s1("before", [P, NB + 1, E], BF16)
        dl = s1("dl", [P, NB])
        el = s1("el", [P, NB])
        wt = s1("wt", [P, 3, NB])
        ra = s1("ra", [P, NB, E])
        rb = s1("rb", [P, NB, E])
        pos = s1("pos", [P, NB, E])
        pt1 = s1("pt1", [P, 2, NB, E])
        numbers = s1("numbers", [P, 2 * NB], I32)
        slotf = s1("slotf", [P, 2, NB])
        slots = [s1(f"slots{n}", [P, 2, NB], I32) for n in range(2)]
        cnt = s1("cnt", [1, 4, E])
        cnti = s1("cnti", [1, 2, E], I32)
        unit = s1("unit", [1, E])
        one.close()

        expert_weights(1, ctx)
        xt = sb("xt", [P, TB, D])
        aux = sb("aux", [P, TB, AUX])
        aux_i = aux[:, :, :].bitcast(I32)
        xth = sb("xth", [P, KD, TT], F32R)
        xtl = sb("xtl", [P, KD, TT], F32R)
        gf = sb("gf", [P, KF, TT])
        gh = sb("gh", [P, KF, TT], F32R)
        gl = sb("gl", [P, KF, TT], F32R)
        ysc = sb("ysc", [P, TB, D])
        gcur = sb("gcur", [P, TB, D])
        num = [sb(f"num{n}", [P, TB], I32) for n in range(2)]

        ps = ctx.enter_context(nc.psum_tensor("ps", [P, 8, 512], F32))
        BANK_T, BANK_QA, BANK_QB, BANK_S, BANK_P, BANK_O = 0, 2, 3, 4, 6, 7
        BANK_H, BANK_Y, BANK_X = 0, 4, 6

        c_in = sem("c_in")
        w_in = sem("w_in")
        consts = sem("consts")
        iotas = sem("iotas")
        setup_pe = sem("setup_pe")
        setup_act = sem("setup_act")
        setup_dve = sem("setup_dve")
        mod_out = sem("mod_out")
        xa_in = [sem(f"xa_in{n}") for n in range(2)]
        xr_in = [sem(f"xr_in{n}") for n in range(2)]
        mb_in = [sem(f"mb_in{n}") for n in range(2)]
        gb_in = [sem(f"gb_in{n}") for n in range(2)]
        x1_out = [sem(f"x1_out{n}") for n in range(2)]
        scattered = [sem(f"scattered{n}") for n in range(2)]
        rows_free = sem("rows_free")
        mt_ready, mt2_ready = sem("mt_ready"), sem("mt2_ready")
        l1a, l1b, l2a, l2b = sem("l1a"), sem("l1b"), sem("l2a"), sem("l2b")
        l1_act, l2_act = sem("l1_act"), sem("l2_act")
        xn_ready = sem("xn_ready")
        t_done = sem("t_done")
        h_full = sem("h_full")
        h_hi, h_lo = sem("h_hi"), sem("h_lo")
        q_done, q_hi, q_lo = sem("q_done"), sem("q_hi"), sem("q_lo")
        v_done, v_hi, v_lo = sem("v_done"), sem("v_hi"), sem("v_lo")
        s_done, neg_max, p_exp = sem("s_done"), sem("neg_max"), sem("p_exp")
        pt_done, pt_hi, pt_lo = sem("pt_done"), sem("pt_hi"), sem("pt_lo")
        o_done, r_inv, o_scaled = sem("o_done"), sem("r_inv"), sem("o_scaled")
        x1_ready = sem("x1_ready")
        xn2_ready = sem("xn2_ready")
        h2_mid, h2_ready = sem("h2_mid"), sem("h2_ready")
        gt_done, g_full = sem("gt_done"), sem("g_full")
        lg_done, lg_read = sem("lg_done"), sem("lg_read")
        ra_s, rb_s, rc_s = sem("ra_s"), sem("rb_s"), sem("rc_s")
        el_done = sem("el_done")
        ps_done, ps_read = sem("ps_done"), sem("ps_read")
        cnt_done, tab_s = sem("cnt_done"), sem("tab_s")
        passed = sem("passed")
        over = sem("over")
        pad_out = sem("pad_out")
        st_in = sem("st_in")
        w_hi = sem("w_hi")
        w1_lo, w2_lo = sem("w1_lo"), sem("w2_lo")
        b_cur, b2_in = sem("b_cur"), sem("b2_in")
        xt_in, aux_in = sem("xt_in"), sem("aux_in")
        x_done = sem("x_done")
        x_hi, x_lo = sem("x_hi"), sem("x_lo")
        m1_done, g_act, g_hi, g_lo = sem("m1_done"), sem("g_act"), sem("g_hi"), sem("g_lo")
        m2_done, y_sum, y_sc = sem("m2_done"), sem("y_sum"), sem("y_sc")
        aux_read = sem("aux_read")
        added = sem("added")
        y_free = sem("y_free")
        dma_sems = [*xa_in, *xr_in, *mb_in, *gb_in, *x1_out, *scattered, added, aux_in, xt_in, st_in, b2_in]
        clear = sem("clear")

        L1A, L1B, L2A, L2B, RA, RB, RC = 9, 4, 9, 4, 18, 6, 6
        N_TAB = 10

        block = ctx.enter_context(nc.Block())

        def phase_over(eng):
            eng.wait_ge(over, 4)

        def tile_range(eng, e):
            def load(col, low, high):
                at = tab[0:1, col:col + 1] if isinstance(col, int) else tab[0:1, bass.ds(col, 1)]
                return eng.value_load(at, min_val=low, max_val=high)
            return load(e + 0, 0, TILES - 1), load(e + 1, 1, TILES), load(e + 9, 0, E * CAP)

        def at(ap, v):
            return ap[bass.ds(v, 1)]

        def load_stage(eng, e):
            eng.dma_start(stage1[:, :, :], at(w1, e).rearrange("a (j p) f -> p (a j) f", p=P)).then_inc(st_in, 16)
            eng.dma_start(stage2[:, :, :], at(w2, e).rearrange("a (j p) d -> p (a j) d", p=P)).then_inc(st_in, 16)

        def load_b2(eng, e, half):
            eng.dma_start(b2row[half][:, :], at(b2, e).rearrange("a d -> (a d)").partition_broadcast(P)) \
               .then_inc(b2_in, 16)

        def chunk1(half, c):
            return half[:, :, c * F // CHUNKS:(c + 1) * F // CHUNKS]

        def chunk2(half, c):
            return half[:, c * KF // CHUNKS:(c + 1) * KF // CHUNKS, :]

        def wait_alone(eng, *waits):
            for sm, n in waits:
                (eng.wait_ge if any(sm is d for d in dma_sems) else lambda *w: wait(eng, *w))(sm, n)
            eng.sem_inc(passed, 1)

        @block.sync
        def _(sp):
            def load_xa(b):
                sp.dma_start(xa[b.half][:, :, :], at(xb, b.val).rearrange("a p i d -> p (a i) d")) \
                  .then_inc(xa_in[b.half], 16)

            sp.dma_start(c_s[:, :], c).then_inc(c_in, 16)
            sp.dma_start(rows64[:, :], b1.rearrange("e (j p) -> (e j) p", p=P)).then_inc(c_in, 16)
            first = Batch(0, 0, 0)
            load_xa(first)
            for dst, src in (
                (wmod_s[:, :, :], wmod.rearrange("(j p) n -> p j n", p=P)),
                (wq_s[:, :, :], Wq.rearrange("(j p) h -> p j h", p=P)),
                (wk_s[:, :, :], Wk.rearrange("(j p) h -> p j h", p=P)),
                (wv_s[:, :, :], Wv.rearrange("(j p) h -> p j h", p=P)),
                (gw[:, :, :], gate_w.rearrange("(j p) e -> p j e", p=P)),
            ):
                sp.dma_start(dst, src).then_inc(w_in, 16)
            for i in range(NB):
                sp.dma_start(gbias[:, i, :], gate_b.partition_broadcast(P)).then_inc(w_in, 16)

            load_xa(first.next())
            wait(sp, setup_dve, SETUP_MODS)
            sp.dma_start(modd, mods[:, :, :].rearrange("b m d -> b (m d)")).then_inc(mod_out, 16)
            load_stage(sp, 0)
            load_b2(sp, 0, 0)
            sp.wait_ge(mod_out, 16)

            def load_batch(b):
                sp.dma_start(xr[b.half][:, :, :], at(xb, b.val).rearrange("a p i d -> p (a i) d")) \
                  .then_inc(xr_in[b.half], 16)
                sp.dma_start(mb[b.half][:, :, :].rearrange("p m d -> p (m d)"),
                             at(modd, b.val)[:, 2 * D:5 * D].rearrange("a d -> (a d)").partition_broadcast(P)).then_inc(mb_in[b.half], 16)

            def load_gb(b):
                sp.dma_start(rows[:, b.half * NB:(b.half + 1) * NB, GB:GB + D],
                             at(modd, b.val)[:, 5 * D:6 * D].rearrange("a d -> (a d)").partition_broadcast(P)
                             .unsqueeze(1).to_broadcast([P, NB, D])).then_inc(gb_in[b.half], 16)

            def iteration(k, a, b, g):
                if k is None:
                    load_batch(a)
                    load_gb(a.next())
                    wait(sp, xn_ready, NB)
                    load_xa(a.next().next())
                    return
                if there(k, 3):
                    wait(sp, xn_ready, NB * (k.val + 2))
                    load_xa(k.next().next().next())
                if g is not None:
                    wait(sp, rows_free, g.val)
                    load_gb(g)
                if a is not None:
                    if g is not None:
                        wait(sp, h2_ready, NB * (g.val + 1))
                        sp.wait_ge(x1_out[g.half], 16 * (g.pair + 1))
                    load_batch(a)
                if b is not None:
                    wait(sp, x1_ready, NB * (b.val + 1))
                    sp.dma_start(at(outb, b.val).rearrange("a p i d -> p (a i) d"), xr[b.half][:, :, :]) \
                      .then_inc(x1_out[b.half], 16)

            over_batches(sp, iteration)
            wait(sp, w1_lo, CHUNKS)
            wait(sp, w2_lo, CHUNKS)
            load_stage(sp, 1)
            wait(sp, tab_s, N_TAB)
            with sp.Fori(0, E) as e:
                end = sp.value_load(tab[0:1, bass.ds(e + 17, 1)], min_val=0, max_val=E * CAP - TT)
                sp.dma_start(lists[bass.ds(end, TT), :].rearrange("(s p) c -> p s c", p=P), pad[:, :, :]) \
                  .then_inc(pad_out, 16)
            phase_over(sp)
            for half in range(2):
                sp.wait_ge(x1_out[half], 16 * (B // 2))
                sp.wait_ge(scattered[half], 16 * 2 * NB * (B // 2 + half))
            sp.wait_ge(pad_out, 16 * E)

            def load_xt(row):
                sp.dma_start(xt[:, :, :], lists[bass.ds(row, TT), 0:D].rearrange("(s p) d -> p s d", p=P)) \
                  .then_inc(xt_in, 16)

            def load_tile(g, base):
                row = nc.s_assert_within(sp.snap(g * TT + base), 0, E * CAP - TT,
                                         skip_runtime_bounds_check_because="a list's tiles lie within it")
                wait(sp, x_done, g)
                load_xt(row)
                wait(sp, aux_read, (TB + 1) * g)
                sp.dma_start(aux[:, :, :], lists[bass.ds(row, TT), D:ROW].rearrange("(s p) d -> p s d", p=P)) \
                  .then_inc(aux_in, 16)

            def expert(e, half, later):
                lo, hi, base = tile_range(sp, e)
                load_tile(lo, base)
                with sp.If(lo + 1 < hi):
                    with sp.Fori(lo + 1, hi) as g:
                        load_tile(g, base)

            over_experts(sp, expert)
            total = sp.value_load(tab[0:1, E:E + 1], min_val=E, max_val=TILES)
            wait(sp, x_done, total)
            load_xt(0)

        @block.gpsimd
        def _(pool):
            start(pool, h_lo, x1_ready, h2_mid, h2_ready, w2_lo, rows_free, y_free)
            pool.memset(ident[:, :], 0.0).then_inc(consts, 1)
            pool.memset(maskb[:, :], 0.0).then_inc(consts, 1)
            pool.memset(identb[:, :], 0.0).then_inc(consts, 1)
            pool.memset(trib[:, :], 0.0).then_inc(consts, 1)
            pool.memset(onesb[:, :], 1.0).then_inc(consts, 1)
            pool.wait_ge(consts, 5)
            pool.affine_select(out=ident[:, :], in_=ident[:, :], compare_op=ALU.not_equal, fill=1.0,
                               base=0, pattern=[[-1, P]], channel_multiplier=1).then_inc(consts, 1)
            pool.affine_select(out=identb[:, :], in_=identb[:, :], compare_op=ALU.not_equal, fill=1.0,
                               base=0, pattern=[[-1, P]], channel_multiplier=1).then_inc(consts, 1)
            pool.affine_select(out=maskb[:, :], in_=maskb[:, :], compare_op=ALU.is_ge, fill=MASKED,
                               base=0, pattern=[[-1, P]], channel_multiplier=1).then_inc(consts, 1)
            pool.affine_select(out=trib[:, :], in_=trib[:, :], compare_op=ALU.is_ge, fill=1.0,
                               base=0, pattern=[[-1, P]], channel_multiplier=1).then_inc(consts, 1)
            pool.iota(iota8[:, :, :], [[0, NB], [1, E]], base=0, channel_multiplier=0,
                      allow_small_or_imprecise_dtypes=True).then_inc(iotas, 1)
            pool.iota(ecap[:, :, :], [[0, NB], [1, E]], base=0, channel_multiplier=0,
                      allow_small_or_imprecise_dtypes=True).then_inc(iotas, 1)
            pool.memset(rows[:, :, RW:ROW], 0.0).then_inc(iotas, 1)
            pool.memset(pad[:, :, :], 0.0).then_inc(iotas, 1)
            pool.memset(rows[:, NB:2 * NB, 0:D], 0.0).then_inc(iotas, 1)
            pool.memset(slots[1][:, :, :], E * CAP).then_inc(iotas, 1)
            pool.wait_ge(iotas, 6)
            pool.iota(numbers[:, :], [[P, 2 * NB]], base=-2 * S, channel_multiplier=1).then_inc(iotas, 1)
            pool.iota(pad[:, :, :].bitcast(I32)[:, :, ID], [[0, TB]], base=FAR, channel_multiplier=0).then_inc(iotas, 1)
            pool.tensor_scalar(ecap[:, :, :], ecap[:, :, :], float(CAP), 0.0, ALU.mult, ALU.add).then_inc(iotas, 1)

            def split_rest(e, half, c):
                wait(pool, w_hi, 2 * CHUNKS * e + CHUNKS + c + 1)
                pool.tensor_tensor(chunk2(w2l[half], c), chunk2(stage2, c), chunk2(w2h[half], c).bitcast(F32),
                                   ALU.subtract).then_inc(w2_lo, 1)

            def hT_rest(b):
                wait(pool, h_hi, KD * (b.val + 1))
                wait(pool, h_full, KD * (b.val + 1))
                wait(pool, s_done, NB * (b.val - 1))
                pool.tensor_tensor(hl[b.half][:, :, :], hf[:, :, :], hh[b.half][:, :, :].bitcast(F32),
                                   ALU.subtract).then_inc(h_lo, 1)

            def residual(b, i):
                wait(pool, o_scaled, NB * b.val + i + 1)
                if i == 0:
                    pool.wait_ge(xr_in[b.half], 16 * (b.pair + 1))
                pool.tensor_tensor(xr[b.half][:, i, :], xr[b.half][:, i, :], ob[:, i, :], ALU.add) \
                    .then_inc(x1_ready, 1)

            def modulate2(b):
                for i in range(NB):
                    if i == 0:
                        wait(pool, rows_free, b.val)
                    wait(pool, xn2_ready, NB * b.val + i + 1)
                    pool.tensor_tensor(rows[:, b.half * NB + i, 0:D], xn2[:, i, :], mb[b.half][:, 2, :], ALU.mult) \
                        .then_inc(h2_mid, 1)
                for i in range(NB):
                    row = rows[:, b.half * NB + i, 0:D]
                    wait(pool, h2_mid, NB * b.val + i + 1)
                    pool.tensor_tensor(row, row, mb[b.half][:, 1, :], ALU.add).then_inc(h2_ready, 1)

            def scatter_begin(b):
                wait_alone(pool, (rc_s, RC * (b.val + 1)), (rb_s, RB * (b.val + 1)),
                           (h2_ready, NB * (b.val + 1)))
                wait_alone(pool, (gb_in[b.half], 16 * (b.pair + 1 + b.half)))

            def scatter(b, i):
                for pick in range(2):
                    pool.indirect_dma_start(
                        lists, bass.IndirectOffsetOnAxis(ap=slots[b.half][:, pick, i:i + 1], axis=0),
                        rows[:, b.half * NB + i, :], None, bounds_check=E * CAP - 1, oob_is_err=False) \
                        .then_inc(scattered[b.half], 16)

            def iteration(k, a, b, g):
                more = there(a, 1)
                if k is None:
                    hT_rest(a)
                    hT_rest(a.next())
                    return
                gone = g.prev() if g is not None else None
                if gone is not None:
                    scatter_begin(gone)
                    scatter(gone, 0)
                    scatter(gone, 1)
                if b is not None:
                    residual(b, 0)
                if gone is not None:
                    scatter(gone, 2)
                if g is not None:
                    modulate2(g)
                if b is not None:
                    residual(b, 1)
                if gone is not None:
                    scatter(gone, 3)
                if b is not None:
                    residual(b, 2)
                if more:
                    hT_rest(a.next())
                if gone is not None:
                    wait_alone(pool, (scattered[gone.half], 16 * 2 * NB * (gone.pair + 1 + gone.half)))
                    pool.sem_inc(rows_free, 1)
                if b is not None:
                    residual(b, 3)
                if a is None and b is not None:
                    for c in range(CHUNKS):
                        split_rest(0, 0, c)

            over_batches(pool, iteration)
            last = Batch(B - 1, (B - 1) % 2, (B - 1) // 2)
            scatter_begin(last)
            for i in range(NB):
                scatter(last, i)
            for half in range(2):
                pool.wait_ge(scattered[half], 16 * 2 * NB * (B // 2 + half))
            pool.engine_nop().then_inc(over, 1)
            phase_over(pool)
            pool.wait_ge(clear, 3)
            for half in range(2):
                pool.wait_ge(x1_out[half], 16 * (B // 2))

            def add_rows(g):
                wait_alone(pool, (y_sc, 2 * g + 2))
                for s in range(TB):
                    pool.indirect_dma_start(
                        out_rows, bass.IndirectOffsetOnAxis(ap=num[1][:, s:s + 1], axis=0),
                        ysc[:, s, :], None, compute_op=ALU.add, bounds_check=NT - 1, oob_is_err=False) \
                        .then_inc(added, 16)

            def rows_added(g):
                wait_alone(pool, (added, 32 * g + 32))
                pool.sem_inc(y_free, 1)

            def expert(e, half, later):
                lo, hi, base = tile_range(pool, e)
                add_rows(lo)
                if later:
                    split_rest(e + 1, 1 - half, 0)
                    split_rest(e + 1, 1 - half, 1)
                rows_added(lo)
                if later:
                    split_rest(e + 1, 1 - half, 2)
                    split_rest(e + 1, 1 - half, 3)
                with pool.If(lo + 1 < hi):
                    with pool.Fori(lo + 1, hi) as g:
                        add_rows(g)
                        rows_added(g)

            over_experts(pool, expert)
            total = pool.value_load(tab[0:1, E:E + 1], min_val=E, max_val=TILES)
            add_rows(total)
            rows_added(total)

        @block.scalar
        def _(act):
            start(act, xn_ready, xn2_ready, h_hi, h_full, q_hi, v_hi, p_exp, pt_hi, g_full, el_done, l1_act, l2_act, w_hi,
                  x_hi, g_act)
            act.preload_act_table_set("natural_log_exp_and_others")
            wait(act, setup_dve, 1)
            act.activation(ecT[:, :, :], cT[:, :, :], ACT.Exp, scale=-1.0).then_inc(setup_act, 1)

            def seed(b, sem_in, per, buf, sem_out):
                wait(act, sem_in, per * (b.val + 1))
                act.activation(buf[:, 1, :], buf[:, 0, :], ACT.Ln, bias=0.0).then_inc(sem_out, 1)
                wait(act, sem_out, 2 * b.val + 1)
                act.activation(buf[:, 2, :], buf[:, 1, :], ACT.Exp, scale=-0.5).then_inc(sem_out, 1)

            def normalise(b):
                wait(act, l1b, L1B * (b.val + 1))
                act.wait_ge(xa_in[b.half], 16 * (b.pair + 1))
                wait(act, t_done, b.val - 1)
                for i in range(NB):
                    act.activation(xn[b.half][:, i, :], xa[b.half][:, i, :], ACT.Identity,
                                   bias=mean1[:, i:i + 1], scale=r1[:, i:i + 1]).then_inc(xn_ready, 1)

            def normalise2(b):
                wait(act, l2b, L2B * (b.val + 1))
                wait(act, gt_done, b.val)
                wait(act, h2_mid, NB * b.val)
                for i in range(NB):
                    act.activation(xn2[:, i, :], xr[b.half][:, i, :], ACT.Identity,
                                   bias=mean2[:, i:i + 1], scale=r2[:, i:i + 1]).then_inc(xn2_ready, 1)

            def hT(b):
                wait(act, mt_ready, b.val + 1)
                wait(act, t_done, b.val + 1)
                wait(act, h_lo, b.val)
                wait(act, s_done, NB * (b.val - 1))
                for j in range(KD):
                    sa, ca = mt[b.half][:, j:j + 1], mt[b.half][:, KD + j:KD + j + 1]
                    act.activation(hh[b.half][:, j, :], ps[:, BANK_T + j, :], ACT.Identity, bias=sa, scale=ca) \
                       .then_inc(h_hi, 1)
                    act.activation(hf[:, j, :], ps[:, BANK_T + j, :], ACT.Identity, bias=sa, scale=ca) \
                       .then_inc(h_full, 1)

            def exps(b, i):
                wait(act, neg_max, NB * b.val + i + 1)
                wait(act, pt_done, NB * b.val + i - 1)
                act.activation(pr[i % 2][:, 0:(i + 1) * P], ps[:, BANK_S + i % 2, 0:(i + 1) * P], ACT.Exp,
                               bias=nmax[:, i:i + 1], accum_out=rsum[:, i:i + 1]).then_inc(p_exp, 1)

            def probs_hi(b, i):
                wait(act, pt_done, NB * b.val + i + 1)
                wait(act, o_done, NB * b.val + i - 1)
                act.activation(pth[i % 2][:, 0:i + 1, :],
                               ps[:, BANK_P, 0:(i + 1) * P].rearrange("p (j q) -> p j q", q=P),
                               ACT.Copy).then_inc(pt_hi, 1)

            def queries_hi(b, m):
                wait(act, q_done, KD * b.val + m + 1)
                wait(act, s_done, NB * (b.val - 1))
                act.activation(qh[b.half][:, m, :], ps[:, BANK_QA + m, :], ACT.Copy).then_inc(q_hi, 1)

            def values_hi(b, p):
                wait(act, v_done, 2 * b.val + p + 1)
                wait(act, o_done, NB * (b.val - 1))
                act.activation(vh[b.half][:, 2 * p:2 * p + 2, :],
                               ps[:, BANK_QA + p, :].rearrange("p (i d) -> p i d", i=2), ACT.Copy).then_inc(v_hi, 1)

            def h2T(b):
                wait(act, gt_done, b.val + 1)
                wait(act, lg_done, b.val)
                wait(act, mt2_ready, b.val + 1)
                for j in range(KD):
                    act.activation(h2f[:, j, :], ps[:, BANK_T + j, :], ACT.Identity, bias=mt2[:, j:j + 1],
                                   scale=mt2[:, KD + j:KD + j + 1]).then_inc(g_full, 1)

            def exp_gap(b):
                wait(act, ra_s, RA * (b.val + 1))
                wait(act, rb_s, RB * b.val)
                act.activation(el[:, :], dl[:, :], ACT.Exp).then_inc(el_done, 1)

            def round_weights(e, half, c):
                chunk, stage, hi = (chunk1, stage1, w1h[half]) if c < CHUNKS else (chunk2, stage2, w2h[half])
                act.activation(chunk(hi, c % CHUNKS), chunk(stage, c % CHUNKS), ACT.Copy).then_inc(w_hi, 1)

            def iteration(k, a, b, g):
                more = there(a, 1)
                if k is None:
                    seed(a, l1a, L1A, ln1, l1_act)
                    normalise(a)
                    seed(a.next(), l1a, L1A, ln1, l1_act)
                    normalise(a.next())
                    hT(a)
                    for m in range(KD):
                        queries_hi(a, m)
                    hT(a.next())
                    for p in range(2):
                        values_hi(a, p)
                    return
                if b is not None:
                    exps(b, 0)
                    exps(b, 1)
                    probs_hi(b, 0)
                if a is not None:
                    queries_hi(a, 0)
                if g is not None:
                    seed(g, l2a, L2A, ln2, l2_act)
                if b is not None:
                    exps(b, 2)
                    probs_hi(b, 1)
                if g is not None:
                    normalise2(g)
                if a is not None:
                    queries_hi(a, 1)
                if b is not None:
                    exps(b, 3)
                    probs_hi(b, 2)
                if more:
                    seed(a.next(), l1a, L1A, ln1, l1_act)
                if g is not None:
                    h2T(g)
                if a is not None:
                    values_hi(a, 0)
                if more:
                    normalise(a.next())
                if b is not None:
                    probs_hi(b, 3)
                if more:
                    hT(a.next())
                if a is not None:
                    values_hi(a, 1)
                if g is not None:
                    exp_gap(g)
                if a is None and b is not None:
                    act.wait_ge(st_in, 32)
                    for c in range(2 * CHUNKS):
                        round_weights(0, 0, c)

            over_batches(act, iteration)
            act.preload_act_table_set("gelu_and_others")
            wait(act, el_done, B)
            act.sem_inc(over, 1)
            phase_over(act)

            def tokens_hi(n):
                wait(act, x_done, n)
                act.activation(xth[:, :, :], ps[:, BANK_X, :].rearrange("p (j t) -> p j t", j=KD), ACT.Copy) \
                   .then_inc(x_hi, 1)

            tokens_hi(1)

            def tile(g, half, more):
                for j in range(KF):
                    wait(act, m1_done, KF * g + j + 1)
                    act.activation(gf[:, j, :], ps[:, BANK_H + j % 4, 0:TT], ACT.Gelu,
                                   bias=bcur[half][:, j:j + 1]).then_inc(g_act, 1)
                    more(j)
                tokens_hi(g + 2)

            def expert(e, half, later):
                lo, hi, base = tile_range(act, e)
                wait(act, b_cur, e + 1)

                def split(j):
                    if later:
                        if j == 0:
                            act.wait_ge(st_in, 32 * (e + 2))
                            wait(act, m2_done, lo)
                        round_weights(e + 1, 1 - half, j)

                tile(lo, half, split)
                if later:
                    wait(act, y_sum, lo + 1)
                    load_b2(act, e + 1, 1 - half)
                if later == 2:
                    wait(act, w1_lo, CHUNKS * (e + 2))
                    wait(act, w2_lo, CHUNKS * (e + 2))
                    load_stage(act, e + 2)
                with act.If(lo + 1 < hi):
                    with act.Fori(lo + 1, hi) as g:
                        tile(g, half, lambda j: None)

            over_experts(act, expert)

        @block.vector
        def _(dve):
            start(dve, setup_dve, tab_s, mt_ready, l1a, l1b, l2a, l2b, q_lo, v_lo, neg_max, pt_lo, r_inv, o_scaled,
                       mt2_ready, lg_read, ra_s, rb_s, rc_s, ps_read, w1_lo, b_cur, x_lo, g_hi,
                       g_lo, y_sum, y_sc, aux_read)
            def spread(b, xin, st, mv, ln, chain):
                for i in range(NB):
                    chain.step(dve.bn_stats(st[:, i, :], xin[b.half][:, i, :]))
                wait_alone(dve, chain.so_far())
                for i in range(NB):
                    chain.step(dve.bn_aggr(mv[:, i, :], st[:, i, :]))
                chain.done()
                chain.step(dve.tensor_scalar(ln[:, 0, :], mv[:, :, 1], EPS, None, ALU.add))

            def refine(ln, r, chain):
                chain.step(dve.tensor_tensor(ln[:, 3, :], ln[:, 2, :], ln[:, 2, :], ALU.mult))
                chain.done()
                chain.step(dve.scalar_tensor_tensor(ln[:, 3, :], ln[:, 3, :], -0.5, ln[:, 0, :], ALU.mult, ALU.mult))
                chain.done()
                chain.step(dve.scalar_tensor_tensor(r[:, :], ln[:, 3, :], 1.5, ln[:, 2, :], ALU.add, ALU.mult))

            def norm1_a(b):
                wait(dve, xn_ready, NB * b.val)
                dve.wait_ge(xa_in[b.half], 16 * (b.pair + 1))
                spread(b, xa, st1, mv1, ln1, Chain(dve, l1a, L1A, b.val))

            def norm1_b(b):
                wait(dve, l1_act, 2 * b.val + 2)
                chain = Chain(dve, l1b, L1B, b.val)
                refine(ln1, r1, chain)
                chain.done()
                chain.step(dve.scalar_tensor_tensor(mean1[:, :], mv1[:, :, 0], -1.0, r1[:, :], ALU.mult, ALU.mult))

            ch = Chain(dve, setup_dve, 64, 0)
            dve.wait_ge(consts, 9)
            dve.wait_ge(setup_pe, 1)
            ch.step(dve.tensor_copy(cT[:, :, :], ps[:, 6, 0:KD * B].rearrange("p (j b) -> p j b", j=KD)))
            ch.step(dve.tensor_copy(biasT[:, :], ps[:, 6, 16:16 + E * KF]))
            dve.wait_ge(setup_act, 1)
            ch.step(dve.tensor_scalar(ecT[:, :, :], ecT[:, :, :], 1.0, None, ALU.add))
            ch.done()
            ch.step(dve.reciprocal(ecT[:, :, :], ecT[:, :, :]))
            ch.done()
            ch.step(dve.tensor_tensor(cT[:, :, :], cT[:, :, :], ecT[:, :, :], ALU.mult))
            assert ch.n == SETUP_SILU
            norm1_a(Batch(0, 0, 0))
            norm1_b(Batch(0, 0, 0))
            norm1_a(Batch(1, 1, 0))
            norm1_b(Batch(1, 1, 0))
            dve.wait_ge(setup_pe, 2)
            ch.step(dve.tensor_copy(mods[:, :, :].rearrange("b m d -> b (m d)"),
                                    ps[0:B, 3:6, :].rearrange("b m d -> b (m d)")))
            for n in (1, 4):
                ch.done()
                ch.step(dve.tensor_scalar(mods[:, n, :], mods[:, n, :], 1.0, None, ALU.add))
            for n in (2, 5):
                gate = mods[:, n, :]
                ch.done()
                ch.step(dve.scalar_tensor_tensor(mtmp[:, :], gate, -1.0, gate, ALU.mult, ALU.max))
                ch.done()
                ch.step(dve.tensor_scalar(mtmp[:, :], mtmp[:, :], 0.25, None, ALU.max))
                ch.step(dve.tensor_scalar(mtmp2[:, :], gate, 0.0, 2.0, ALU.is_ge, ALU.mult))
                ch.done()
                ch.step(dve.scalar_tensor_tensor(gate, mtmp2[:, :], -1.0, mtmp[:, :], ALU.add, ALU.mult))
            assert ch.n == SETUP_MODS, ch.n
            dve.wait_ge(setup_pe, 3)
            ch.step(dve.tensor_copy(modT[:, :, :], ps[:, 6, 0:8 * B].rearrange("p (m b) -> p m b", b=B)))
            dve.wait_ge(setup_pe, 4)
            m_ps = ps[:, 2, :].rearrange("p (j h) -> p j h", j=KD)
            ch.step(dve.tensor_scalar(mh[:, :, :], m_ps, 1.0 / 16, None, ALU.mult))
            ch.done()
            ch.step(dve.scalar_tensor_tensor(ml[:, :, :], m_ps, 1.0 / 16, mh[:, :, :].bitcast(F32),
                                             ALU.mult, ALU.subtract))
            wv_ps = ps[:, 7, :].rearrange("p (j o) -> p j o", j=KD)
            ch.step(dve.tensor_copy(wvh[:, :, :], wv_ps))
            ch.done()
            ch.step(dve.tensor_tensor(wvl[:, :, :], wv_ps, wvh[:, :, :].bitcast(F32), ALU.subtract))
            ch.step(dve.memset(before[:, NB, :], 0.0))
            ch.step(dve.memset(unit[:, :], 1.0))
            ch.done()
            assert ch.n == SETUP_ALL, ch.n
            dve.wait_ge(iotas, 9)

            def biases(e, half):
                dve.tensor_scalar(bcur[half][:, :], biasT[:, bass.ds(e * KF, KF)], 0.0, None, ALU.add) \
                   .then_inc(b_cur, 1)

            def split_rest(e, half, c):
                wait(dve, w_hi, 2 * CHUNKS * e + c + 1)
                dve.tensor_tensor(chunk1(w1l[half], c), chunk1(stage1, c), chunk1(w1h[half], c).bitcast(F32),
                                  ALU.subtract).then_inc(w1_lo, 1)

            def mod_columns(b):
                wait(dve, h_full, KD * (b.val - 1))
                src = modT[:, 0:4, b.val:b.val + 1] if isinstance(b.val, int) else modT[:, 0:4, bass.ds(b.val, 1)]
                dve.tensor_scalar(mt[b.half][:, :].unsqueeze(2), src, 0.0, None, ALU.add).then_inc(mt_ready, 1)

            def mod_columns2(b):
                wait(dve, g_full, KD * b.val)
                src = modT[:, 4:8, b.val:b.val + 1] if isinstance(b.val, int) else modT[:, 4:8, bass.ds(b.val, 1)]
                dve.tensor_scalar(mt2[:, :].unsqueeze(2), src, 0.0, None, ALU.add).then_inc(mt2_ready, 1)

            def queries_lo(b, m):
                wait(dve, q_hi, KD * b.val + m + 1)
                dve.tensor_tensor(ql[b.half][:, m, :], ps[:, BANK_QA + m, :], qh[b.half][:, m, :].bitcast(F32),
                                  ALU.subtract).then_inc(q_lo, 1)

            def values_lo(b, p):
                wait(dve, v_hi, 2 * b.val + p + 1)
                dve.tensor_tensor(vl[b.half][:, 2 * p:2 * p + 2, :],
                                  ps[:, BANK_QA + p, :].rearrange("p (i d) -> p i d", i=2),
                                  vh[b.half][:, 2 * p:2 * p + 2, :].bitcast(F32), ALU.subtract).then_inc(v_lo, 1)

            def row_max(b, i):
                wait(dve, s_done, NB * b.val + i + 1)
                dve.tensor_reduce(nmax[:, i:i + 1], ps[:, BANK_S + i % 2, 0:(i + 1) * P], AX.X, ALU.max,
                                  negate=True).then_inc(neg_max, 1)

            def probs_lo(b, i):
                wait(dve, pt_hi, NB * b.val + i + 1)
                dve.tensor_tensor(ptl[i % 2][:, 0:i + 1, :],
                                  ps[:, BANK_P, 0:(i + 1) * P].rearrange("p (j q) -> p j q", q=P),
                                  pth[i % 2][:, 0:i + 1, :].bitcast(F32), ALU.subtract).then_inc(pt_lo, 1)

            def scale_out(b, i):
                wait(dve, o_done, NB * b.val + i + 1)
                if i == 0:
                    dve.wait_ge(mb_in[b.half], 16 * (b.pair + 1))
                dve.reciprocal(rinv[:, i:i + 1], rsum[:, i:i + 1]).then_inc(r_inv, 1)
                wait(dve, r_inv, NB * b.val + i + 1)
                wait(dve, x1_ready, NB * (b.val - 1) + i + 1)
                dve.scalar_tensor_tensor(ob[:, i, :], ps[:, BANK_O, (i % 2) * D:(i % 2 + 1) * D], rinv[:, i:i + 1],
                                         mb[b.half][:, 0, :], ALU.mult, ALU.mult).then_inc(o_scaled, 1)

            def norm2_a(b):
                wait(dve, x1_ready, NB * (b.val + 1))
                spread(b, xr, st2, mv2, ln2, Chain(dve, l2a, L2A, b.val))

            def norm2_b(b):
                wait(dve, l2_act, 2 * b.val + 2)
                wait(dve, xn2_ready, NB * b.val)
                chain = Chain(dve, l2b, L2B, b.val)
                refine(ln2, r2, chain)
                chain.done()
                chain.step(dve.scalar_tensor_tensor(mean2[:, :], mv2[:, :, 0], -1.0, r2[:, :], ALU.mult, ALU.mult))

            def route_a(b):
                wait(dve, lg_done, b.val + 1)
                chain = Chain(dve, ra_s, RA, b.val)
                dve.tensor_tensor(lg[:, :, :], ps[:, BANK_QB, 0:NB * E].rearrange("p (i e) -> p i e", e=E),
                                  gbias[:, :, :], ALU.add).then_inc(lg_read, 1)
                wait_alone(dve, (lg_read, b.val + 1))
                for i in range(NB):
                    chain.step(dve.max(mx[:, i, :], lg[:, i, :]))
                wait_alone(dve, chain.so_far())
                for i in range(NB):
                    chain.step(dve.max_index(mxi[:, i, :], mx[:, i, :], lg[:, i, :]))
                chain.done()
                chain.step(dve.tensor_copy(idxf[:, :, :], mxi[:, :, 0:2]))
                chain.step(dve.tensor_tensor(dl[:, :], mx[:, :, 1], mx[:, :, 0], ALU.subtract))
                chain.done()
                chain.step(dve.tensor_tensor(o1[:, :, :], iota8[:, :, :],
                                             idxf[:, :, 0:1].to_broadcast([P, NB, E]), ALU.is_equal))
                chain.step(dve.tensor_tensor(o2[:, :, :], iota8[:, :, :],
                                             idxf[:, :, 1:2].to_broadcast([P, NB, E]), ALU.is_equal))
                chain.done()
                wait(dve, ps_done, b.val)
                chain.step(dve.tensor_tensor(picks[:, :, :], o1[:, :, :], o2[:, :, :], ALU.add))
                chain.step(dve.tensor_copy(before[:, 0, :], before[:, NB, :]))
                for i in range(NB):
                    chain.done()
                    chain.step(dve.tensor_tensor(before[:, i + 1, :], before[:, i, :], picks[:, i, :], ALU.add))

            def route_b(b):
                chain = Chain(dve, rb_s, RB, b.val)
                wait(dve, rows_free, b.val)
                wait(dve, el_done, b.val + 1)
                chain.step(dve.tensor_scalar(wt[:, 0, :], el[:, :], 1.0, None, ALU.add))
                chain.done()
                chain.step(dve.reciprocal(wt[:, 1, :], wt[:, 0, :]))
                chain.done()
                chain.step(dve.tensor_tensor(wt[:, 2, :], wt[:, 1, :], el[:, :], ALU.mult))
                chain.done()
                chain.step(dve.tensor_tensor(ra[:, :, :], o1[:, :, :],
                                             wt[:, 1, :].unsqueeze(2).to_broadcast([P, NB, E]), ALU.mult))
                chain.step(dve.tensor_tensor(rb[:, :, :], o2[:, :, :],
                                             wt[:, 2, :].unsqueeze(2).to_broadcast([P, NB, E]), ALU.mult))
                chain.done()
                chain.step(dve.tensor_tensor(rows[:, b.half * NB:(b.half + 1) * NB, RW:RW + E],
                                             ra[:, :, :], rb[:, :, :], ALU.add))

            def route_c(b):
                chain = Chain(dve, rc_s, RC, b.val)
                wait(dve, ps_done, b.val + 1)
                dve.tensor_tensor(pos[:, :, :], ps[:, BANK_QA, 0:NB * E].rearrange("p (i e) -> p i e", e=E),
                                  ecap[:, :, :], ALU.add).then_inc(ps_read, 1)
                wait(dve, ps_read, b.val + 1)
                chain.step(dve.tensor_tensor(pt1[:, 0, :, :], pos[:, :, :], o1[:, :, :], ALU.mult))
                chain.step(dve.tensor_tensor(pt1[:, 1, :, :], pos[:, :, :], o2[:, :, :], ALU.mult))
                chain.done()
                chain.step(dve.tensor_reduce(slotf[:, :, :], pt1[:, :, :, :], AX.X, ALU.add))
                chain.done()
                chain.step(dve.tensor_copy(slots[b.half][:, :, :], slotf[:, :, :]))
                own = slice(b.half * NB, (b.half + 1) * NB)
                chain.step(dve.tensor_scalar(numbers[:, own], numbers[:, own], float(2 * S), None, ALU.add))
                chain.done()
                chain.step(dve.tensor_copy(rows_i[:, own, ID], numbers[:, own]))

            def iteration(k, a, b, g):
                more = there(a, 1)
                if k is None:
                    mod_columns(a)
                    mod_columns(a.next())
                    for m in range(KD):
                        queries_lo(a, m)
                    for p in range(2):
                        values_lo(a, p)
                    biases(0, 0)
                    return
                if b is not None:
                    row_max(b, 0)
                    row_max(b, 1)
                if g is not None:
                    norm2_a(g)
                if b is not None:
                    probs_lo(b, 0)
                    row_max(b, 2)
                if a is not None:
                    queries_lo(a, 0)
                if g is not None:
                    norm2_b(g)
                    mod_columns2(g)
                if b is not None:
                    probs_lo(b, 1)
                    scale_out(b, 0)
                    row_max(b, 3)
                if a is not None:
                    queries_lo(a, 1)
                if more:
                    norm1_a(a.next())
                    mod_columns(a.next())
                if b is not None:
                    scale_out(b, 1)
                    probs_lo(b, 2)
                if more:
                    norm1_b(a.next())
                if a is not None:
                    values_lo(a, 0)
                if b is not None:
                    scale_out(b, 2)
                    probs_lo(b, 3)
                if g is not None:
                    route_a(g)
                if a is not None:
                    values_lo(a, 1)
                if b is not None:
                    scale_out(b, 3)
                if g is not None:
                    route_b(g)
                    route_c(g)
                if a is None and b is not None:
                    for c in range(CHUNKS):
                        split_rest(0, 0, c)

            over_batches(dve, iteration)

            tc = Chain(dve, tab_s, N_TAB, 0)
            dve.wait_ge(cnt_done, 1)
            tc.step(dve.tensor_copy(cnt[:, 0, :], ps[0:1, BANK_S, 0:E]))
            tc.done()
            tc.step(dve.tensor_scalar(cnti[:, 0, :], cnt[:, 0, :], float(TT - 1), None, ALU.add))
            tc.step(dve.tensor_tensor(tab[:, 17:17 + E], cnt[:, 0, :], ecap[0:1, 0, :], ALU.add))
            tc.done()
            tc.step(dve.tensor_scalar(cnti[:, 1, :], cnti[:, 0, :], TT.bit_length() - 1, None, ALU.logical_shift_right))
            tc.done()
            tc.step(dve.tensor_scalar(cnt[:, 1, :], cnti[:, 1, :], 1.0, None, ALU.max))
            tc.done()
            tc.step(dve.tensor_tensor_scan(cnt[:, 2, :], unit[:, :], cnt[:, 1, :], 0.0, ALU.mult, ALU.add))
            tc.step(dve.memset(tab[:, 0:1], 0))
            tc.done()
            tc.step(dve.tensor_copy(tab[:, 1:1 + E], cnt[:, 2, :]))
            tc.step(dve.tensor_tensor(cnt[:, 3, :], cnt[:, 2, :], cnt[:, 1, :], ALU.subtract))
            tc.done()
            tc.step(dve.scalar_tensor_tensor(tab[:, 9:9 + E], cnt[:, 3, :], -float(TT), ecap[0:1, 0, :],
                                             ALU.mult, ALU.add))
            tc.done()
            dve.sem_inc(over, 1)
            phase_over(dve)
            dve.memset(gcur[:, :, :], 0.0).then_inc(clear, 1)
            dve.memset(b2row[1][:, :], 0.0).then_inc(clear, 1)
            dve.memset(num[0][:, :], FAR).then_inc(clear, 1)
            dve.wait_ge(clear, 3)

            def tokens_lo(n):
                wait(dve, x_hi, n)
                dve.tensor_tensor(xtl[:, :, :], ps[:, BANK_X, :].rearrange("p (j t) -> p j t", j=KD),
                                  xth[:, :, :].bitcast(F32), ALU.subtract).then_inc(x_lo, 1)

            tokens_lo(1)

            def weigh_before(g, half):
                wait(dve, m2_done, g)
                wait(dve, y_free, g)
                y = ps[:, BANK_Y:BANK_Y + TB, 0:D]
                dve.tensor_tensor(ysc[:, :, :], y, b2row[half][:, :].unsqueeze(1).to_broadcast([P, TB, D]), ALU.add) \
                   .then_inc(y_sum, 1)
                dve.tensor_copy(num[1][:, :], num[0][:, :]).then_inc(y_sc, 1)
                wait(dve, y_sum, g + 1)
                dve.tensor_tensor(ysc[:, :, :], ysc[:, :, :], gcur[:, :, :], ALU.mult).then_inc(y_sc, 1)

            def weights_of(g, e):
                dve.wait_ge(aux_in, 16 * g + 16)
                for s in range(TB):
                    dve.tensor_scalar(gcur[:, s, :], aux[:, s, 0:D], aux[:, s, bass.ds(e + (RW - D), 1)], None,
                                      ALU.mult).then_inc(aux_read, 1)
                dve.tensor_copy(num[0][:, :], aux_i[:, :, ID - D]).then_inc(aux_read, 1)

            def tile(g, e, more):
                for j in range(KF):
                    wait(dve, g_act, KF * g + j + 1)
                    dve.tensor_copy(gh[:, j, :], gf[:, j, :]).then_inc(g_hi, 1)
                    wait(dve, g_hi, KF * g + j + 1)
                    dve.tensor_tensor(gl[:, j, :], gf[:, j, :], gh[:, j, :].bitcast(F32), ALU.subtract) \
                       .then_inc(g_lo, 1)
                    if j == 0:
                        weights_of(g, e)
                    else:
                        more(j)
                tokens_lo(g + 2)

            def expert(e, half, later):
                lo, hi, base = tile_range(dve, e)
                dve.wait_ge(b2_in, 16 * (e + 1))
                weigh_before(lo, 1 - half)

                def split(j):
                    if later and j == 1:
                        biases(e + 1, 1 - half)
                    if later and 2 <= j < 2 + CHUNKS:
                        split_rest(e + 1, 1 - half, j - 2)

                tile(lo, e, split)
                with dve.If(lo + 1 < hi):
                    with dve.Fori(lo + 1, hi) as g:
                        weigh_before(g, half)
                        tile(g, e, lambda j: None)

            over_experts(dve, expert)
            total = dve.value_load(tab[0:1, E:E + 1], min_val=E, max_val=TILES)
            weigh_before(total, 1)

        @block.tensor
        def _(pe):
            start(pe, t_done, q_done, v_done, s_done, pt_done, o_done, gt_done, lg_done, ps_done, x_done,
                  m1_done, m2_done)
            def three(out_, wh, wl, xh, xl, start, stop):
                pe.matmul(out_, wh, xh, start=start, stop=False)
                pe.matmul(out_, wh, xl, start=False, stop=False)
                return pe.matmul(out_, wl, xh, start=False, stop=stop)

            def tokens_T(b):
                wait(pe, xn_ready, NB * (b.val + 1))
                wait(pe, g_full, KD * (b.val - 2))
                for i in range(NB):
                    for j in range(KD):
                        mm = pe.transpose(ps[:, BANK_T + j, i * P:(i + 1) * P],
                                          xn[b.half][:, i, j * P:(j + 1) * P], ident[:, :])
                mm.then_inc(t_done, 1)

            pe.wait_ge(consts, 9)
            pe.wait_ge(c_in, 32)
            for j in range(KD):
                pe.transpose(ps[:, 6, j * B:(j + 1) * B], c_s[:, j * P:(j + 1) * P], ident[0:B, 0:B])
            pe.transpose(ps[:, 6, 16:16 + E * KF], rows64[:, :], ident[0:E * KF, 0:E * KF]).then_inc(setup_pe, 1)
            wait(pe, setup_dve, SETUP_SILU)
            pe.wait_ge(w_in, 16 * (5 + NB))
            for n in range(3):
                for j in range(KD):
                    mm = pe.matmul(ps[0:B, 3 + n, :], cT[:, j, :], wmod_s[:, j, n * 512:(n + 1) * 512],
                                   start=(j == 0), stop=(j == KD - 1))
            mm.then_inc(setup_pe, 1)
            tokens_T(Batch(0, 0, 0))
            for oj in range(KD):
                for hj in range(KD):
                    pe.transpose(ps[:, 7, hj * D + oj * P:hj * D + (oj + 1) * P], wv_s[:, oj, hj * P:(hj + 1) * P],
                                 ident[:, :])
            for hj in range(KD):
                for oj in range(KD):
                    pe.matmul(ps[:, 2, hj * D:(hj + 1) * D], wq_s[:, oj, hj * P:(hj + 1) * P], wk_s[:, oj, :],
                              start=(oj == 0), stop=(oj == KD - 1))
            wait(pe, setup_dve, SETUP_MODS)
            for n, m in enumerate((0, 1, 3, 4)):
                for j in range(KD):
                    mm = pe.transpose(ps[:, 6, (n * KD + j) * B:(n * KD + j + 1) * B],
                                      mods[:, m, j * P:(j + 1) * P], ident[0:B, 0:B])
            mm.then_inc(setup_pe, 2)
            wait(pe, setup_dve, SETUP_ALL)

            def queries(b, m):
                wait(pe, h_lo, b.val + 1)
                if m == 0:
                    wait(pe, ps_read, b.val - 2)
                    wait(pe, v_lo, 2 * b.val - 1)
                else:
                    wait(pe, v_lo, 2 * b.val)
                    wait(pe, lg_read, b.val - 2)
                for j in range(KD):
                    mm = three(ps[:, BANK_QA + m, :], mh[:, j, m * P:(m + 1) * P], ml[:, j, m * P:(m + 1) * P],
                               hh[b.half][:, j, :], hl[b.half][:, j, :], j == 0, j == KD - 1)
                mm.then_inc(q_done, 1)

            def values(b, p):
                if p == 0:
                    wait(pe, q_lo, KD * b.val + 1)
                else:
                    wait(pe, q_lo, KD * b.val + 2)
                    wait(pe, lg_read, b.val - 1)
                for i in (2 * p, 2 * p + 1):
                    tok = slice(i * P, (i + 1) * P)
                    for j in range(KD):
                        o = ps[:, BANK_QA + p, (i % 2) * D:(i % 2 + 1) * D]
                        pe.matmul(o, hh[b.half][:, j, tok], wvh[:, j, :], start=(j == 0), stop=False)
                        pe.matmul(o, hh[b.half][:, j, tok], wvl[:, j, :], start=False, stop=False)
                        mm = pe.matmul(o, hl[b.half][:, j, tok], wvh[:, j, :], start=False, stop=(j == KD - 1))
                mm.then_inc(v_done, 1)

            def scores(b, i):
                if i == 0:
                    wait(pe, q_lo, KD * (b.val + 1))
                wait(pe, p_exp, NB * b.val + i - 1)
                n = max(2, i + 1) * P
                tok = slice(i * P, (i + 1) * P)
                bank = ps[:, BANK_S + i % 2, :]
                for j in range(KD):
                    q_hi_, q_lo_ = qh[b.half][:, j, tok], ql[b.half][:, j, tok]
                    pe.matmul(bank[:, 0:n], q_hi_, hh[b.half][:, j, 0:n], start=(j == 0), stop=False)
                    if j == 0:
                        pe.matmul(bank[:, tok], identb[:, :], maskb[:, :], start=False, stop=False)
                    pe.matmul(bank[:, 0:n], q_hi_, hl[b.half][:, j, 0:n], start=False, stop=False)
                    mm = pe.matmul(bank[:, 0:n], q_lo_, hh[b.half][:, j, 0:n], start=False, stop=(j == KD - 1))
                mm.then_inc(s_done, 1)

            def probs_T(b, i):
                wait(pe, p_exp, NB * b.val + i + 1)
                wait(pe, pt_lo, NB * b.val + i)
                for j in range(i + 1):
                    mm = pe.transpose(ps[:, BANK_P, j * P:(j + 1) * P], pr[i % 2][:, j * P:(j + 1) * P], ident[:, :])
                mm.then_inc(pt_done, 1)

            def attend(b, i):
                wait(pe, pt_lo, NB * b.val + i + 1)
                if i == 0:
                    wait(pe, v_lo, 2 * (b.val + 1))
                wait(pe, o_scaled, NB * b.val + i)
                o = ps[:, BANK_O, (i % 2) * D:(i % 2 + 1) * D]
                for j in range(i + 1):
                    pe.matmul(o, pth[i % 2][:, j, :], vh[b.half][:, j, :], start=(j == 0), stop=False)
                    pe.matmul(o, pth[i % 2][:, j, :], vl[b.half][:, j, :], start=False, stop=False)
                    mm = pe.matmul(o, ptl[i % 2][:, j, :], vh[b.half][:, j, :], start=False, stop=(j == i))
                mm.then_inc(o_done, 1)

            def h2_T(b):
                wait(pe, xn2_ready, NB * (b.val + 1))
                n = b.val + 3
                wait(pe, h_full, KD * (min(n, B) if isinstance(n, int) else n))
                for i in range(NB):
                    for j in range(KD):
                        mm = pe.transpose(ps[:, BANK_T + j, i * P:(i + 1) * P],
                                          xn2[:, i, j * P:(j + 1) * P], ident[:, :])
                mm.then_inc(gt_done, 1)

            def logits(b):
                wait(pe, g_full, KD * (b.val + 1))
                n = b.val + 3
                wait(pe, q_lo, KD * (min(n, B) if isinstance(n, int) else n))
                for i in range(NB):
                    for j in range(KD):
                        mm = pe.matmul(ps[:, BANK_QB, i * E:(i + 1) * E], h2f[:, j, i * P:(i + 1) * P], gw[:, j, :],
                                       start=(j == 0), stop=(j == KD - 1))
                mm.then_inc(lg_done, 1)

            def places(b):
                wait(pe, ra_s, RA * (b.val + 1))
                n = b.val + 3
                wait(pe, v_lo, 2 * (min(n, B) if isinstance(n, int) else n) - 1)
                o = ps[:, BANK_QA, 0:NB * E]
                pe.matmul(o, trib[:, :], picks[:, :, :].rearrange("p i e -> p (i e)"), start=True, stop=False)
                pe.matmul(o, onesb[:, :], before[:, 0:NB, :].rearrange("p i e -> p (i e)"), start=False, stop=True) \
                  .then_inc(ps_done, 1)

            def iteration(k, a, b, g):
                more = there(a, 1)
                if k is None:
                    for m in range(KD):
                        queries(a, m)
                    tokens_T(a.next())
                    for p in range(2):
                        values(a, p)
                    return
                if b is not None:
                    scores(b, 0)
                    scores(b, 1)
                if a is not None:
                    queries(a, 0)
                if b is not None:
                    probs_T(b, 0)
                    scores(b, 2)
                    attend(b, 0)
                    probs_T(b, 1)
                if a is not None:
                    queries(a, 1)
                if b is not None:
                    scores(b, 3)
                    attend(b, 1)
                if g is not None:
                    h2_T(g)
                if b is not None:
                    probs_T(b, 2)
                if a is not None:
                    values(a, 0)
                if b is not None:
                    attend(b, 2)
                    probs_T(b, 3)
                if g is not None:
                    logits(g)
                if more:
                    tokens_T(a.next())
                if a is not None:
                    values(a, 1)
                if b is not None:
                    attend(b, 3)
                if g is not None:
                    places(g)

            over_batches(pe, iteration)
            pe.matmul(ps[:, BANK_S, 0:E], onesb[:, :], before[:, NB, :], start=True, stop=True).then_inc(cnt_done, 1)
            pe.wait_ge(cnt_done, 1)
            pe.sem_inc(over, 1)
            phase_over(pe)

            def tile_T(n):
                pe.wait_ge(xt_in, 16 * n + 16)
                for s in range(TB):
                    for j in range(KD):
                        mm = pe.transpose(ps[:, BANK_X, j * TT + s * P:j * TT + (s + 1) * P],
                                          xt[:, s, j * P:(j + 1) * P], ident[:, :])
                mm.then_inc(x_done, 1)

            def up(g, j, half):
                cols = slice(j * P, (j + 1) * P)
                if j == 0:
                    wait(pe, x_lo, g + 1)
                if j >= 4:
                    wait(pe, g_act, KF * g + j - 3)
                for n in range(KD):
                    mm = three(ps[:, BANK_H + j % 4, 0:TT], w1h[half][:, n, cols], w1l[half][:, n, cols],
                               xth[:, n, :], xtl[:, n, :], n == 0, n == KD - 1)
                mm.then_inc(m1_done, 1)

            def down(g, j, half):
                wait(pe, g_lo, KF * g + j + 1)
                if j == 0:
                    wait(pe, y_sum, g + 1)
                for s in range(TB):
                    y, tok = ps[:, BANK_Y + s, 0:D], slice(s * P, (s + 1) * P)
                    pe.matmul(y, gh[:, j, tok], w2h[half][:, j, :], start=(j == 0), stop=False)
                    pe.matmul(y, gh[:, j, tok], w2l[half][:, j, :], start=False, stop=False)
                    mm = pe.matmul(y, gl[:, j, tok], w2h[half][:, j, :], start=False, stop=(j == KF - 1))
                if j == KF - 1:
                    mm.then_inc(m2_done, 1)

            tile_T(0)

            def expert(e, half, later):
                lo, hi, base = tile_range(pe, e)
                wait_alone(pe, (w1_lo, CHUNKS * (e + 1)), (w2_lo, CHUNKS * (e + 1)))
                with pe.Fori(lo, hi) as g:
                    for j in range(KF):
                        up(g, j, half)
                        if j >= LAG:
                            down(g, j - LAG, half)
                    tile_T(g + 1)
                    for j in range(KF - LAG, KF):
                        down(g, j, half)

            over_experts(pe, expert)


SETUP_SILU = 5
SETUP_MODS = SETUP_SILU + 3 + 8
SETUP_ALL = SETUP_MODS + 7


_INS = ["L0_attn_x", "L0_attn_Wq", "L0_attn_Wk", "L0_attn_Wv", "L0_ffn_gate_w", "L0_ffn_gate_b",
        "L0_ffn_w1", "L0_ffn_b1", "L0_ffn_w2", "L0_ffn_b2", "L0_c", "L0_wmod"]


def kernel(**inputs):
    import numpy as np
    import concourse.bacc as bacc
    from concourse.bass_utils import run_bass_kernel_spmd

    nc = bacc.Bacc("TRN2", target_bir_lowering=False, num_devices=1)
    arrays, args = {}, []
    for name in _INS:
        a = np.ascontiguousarray(inputs[name])
        arrays[f"in_{name}"] = a
        args.append(nc.dram_tensor(f"in_{name}", a.shape, mybir.dt.from_np(a.dtype), kind="ExternalInput").ap())
    args.append(nc.dram_tensor("out_0", (B, S, D), F32, kind="ExternalOutput").ap())
    layer(nc, *args)
    r = run_bass_kernel_spmd(nc, [arrays], core_ids=[0])
    return r.results[0]["out_0"]
```

```python
from contextlib import ExitStack

import concourse.bass as bass
from concourse import mybir
from concourse.alu_op_type import AluOpType as ALU

F32 = mybir.dt.float32
F32R = mybir.dt.float32r
BF16 = mybir.dt.bfloat16
I32 = mybir.dt.int32
U32 = mybir.dt.uint32
ACT = mybir.ActivationFunctionType
AX = mybir.AxisListType

P = 128
B, S, D = 8, 512, 256
NB = S // P
KD = D // P
E, F = 8, 1024
KF = F // P
NT = B * S
TT = 256
TB = TT // P
CAP = NT + TT
TILES = 2 * NT // TT + E
GB, RW, ID, ROW = D, 2 * D, 2 * D + E, 2 * D + 2 * E
AUX = ROW - D
EPS = 1e-5
MASKED = -3.0e38
CHUNKS = 4
SHORT = ROW - RW
LAG = 4


class Batch:

    def __init__(self, val, half, pair):
        self.val, self.half, self.pair = val, half, pair

    def next(self):
        return Batch(self.val + 1, 1 - self.half, self.pair + self.half)

    def prev(self):
        return Batch(self.val - 1, 1 - self.half, self.pair - (1 - self.half))


def wait(eng, sem, count):
    if isinstance(count, int) and count <= 0:
        return
    eng.wait_ge(sem, count + 1)


def start(eng, *sems):
    for sem in sems:
        eng.sem_inc(sem, 1)


class Chain:

    def __init__(self, eng, sem, per, times, n=0):
        self.eng, self.sem, self.per, self.base, self.n = eng, sem, per, times * per, n

    def so_far(self):
        return self.sem, self.base + self.n

    def step(self, ins):
        self.n += 1
        assert self.n <= self.per
        ins.then_inc(self.sem, 1)

    def done(self):
        wait(self.eng, *self.so_far())


def over_batches(eng, iteration):
    first = Batch(0, 0, 0)
    iteration(None, first, None, None)
    iteration(first, first.next(), first, None)
    with eng.Fori(0, (B - 4) // 2) as m:
        for k in (Batch(2 * m + 1, 1, m), Batch(2 * m + 2, 0, m + 1)):
            iteration(k, k.next(), k, k.prev())
    for n in range(B - 3, B + 1):
        k = Batch(n, n % 2, n // 2)
        iteration(k, k.next() if n + 1 < B else None, k if n < B else None, k.prev())


def there(b, more=0):
    return b is not None and not (isinstance(b.val, int) and b.val + more >= B)


def over_experts(eng, expert):
    with eng.Fori(0, (E - 4) // 2) as m:
        expert(2 * m, 0, 3)
        expert(2 * m + 1, 1, 3)
    for e in range(E - 4, E):
        expert(e, e % 2, E - 1 - e)


def layer(nc, x, Wq, Wk, Wv, gate_w, gate_b, w1, b1, w2, b2, c, wmod, out):
    ctx = ExitStack()
    with ctx:
        def sb(name, shape, dt=F32, where=ctx):
            return where.enter_context(nc.sbuf_tensor(name, shape, dt))

        def sem(name):
            return ctx.enter_context(nc.semaphore(name))

        lists = nc.dram_tensor("lists", [E * CAP, ROW], F32).ap()
        modd = nc.dram_tensor("modd", [B, 6 * D], F32).ap()
        xb = x.rearrange("b (i p) d -> b p i d", p=P)
        lists_short = lists.rearrange("r (n c) -> (r n) c", c=SHORT)
        out_rows = out.rearrange("b s d -> (b s) d")
        outb = out.rearrange("b (i p) d -> b p i d", p=P)

        ident = sb("ident", [P, P])
        pad = sb("pad", [P, TB, ROW])
        rows64 = sb("rows64", [E * KF, P])
        biasT = sb("biasT", [P, E * KF])
        tab = sb("tab", [1, 32], I32)
        padslots = sb("padslots", [P, E], I32)
        padcur = sb("padcur", [P, 1], I32)
        others = sb("others", [P, SHORT])
        stage1 = [sb("stage1", [P, KD, F])]
        stage2 = [sb("stage2", [P, KF, D])]
        w1h, w1l, w2h, w2l = [], [], [], []

        def expert_weights(n, where):
            w1h.append(sb(f"w1h{n}", [P, KD, F], F32R, where))
            w1l.append(sb(f"w1l{n}", [P, KD, F], F32R, where))
            w2h.append(sb(f"w2h{n}", [P, KF, D], F32R, where))
            w2l.append(sb(f"w2l{n}", [P, KF, D], F32R, where))

        expert_weights(0, ctx)
        bcur = [sb(f"bcur{n}", [P, KF]) for n in range(2)]
        b2row = [sb(f"b2row{n}", [P, D]) for n in range(2)]

        one = ExitStack()

        def s1(name, shape, dt=F32):
            return sb(name, shape, dt, one)

        with ExitStack() as zero:
            wmod_s = sb("wmod_s", [P, KD, 6 * D], F32, zero)
            wq_s = sb("wq_s", [P, KD, D], F32, zero)
            wk_s = sb("wk_s", [P, KD, D], F32, zero)
            wv_s = sb("wv_s", [P, KD, D], F32, zero)
        batch1 = [s1(f"{name}1", shape, F32R) for name, shape in (
            ("hh", [P, KD, S]), ("hl", [P, KD, S]), ("qh", [P, KD, S]), ("ql", [P, KD, S]),
            ("vh", [P, NB, D]), ("vl", [P, NB, D]))]
        maskb = s1("maskb", [P, P], BF16)
        identb = s1("identb", [P, P], BF16)
        trib = s1("trib", [P, P], BF16)
        onesb = s1("onesb", [P, P], BF16)
        mh = s1("mh", [P, KD, D], F32R)
        ml = s1("ml", [P, KD, D], F32R)
        wvh = s1("wvh", [P, KD, D], F32R)
        wvl = s1("wvl", [P, KD, D], F32R)
        gw = s1("gw", [P, KD, E])
        gbias = s1("gbias", [P, NB, E])
        iota8 = s1("iota8", [P, NB, E])
        ecap = s1("ecap", [P, NB, E])
        c_s = s1("c_s", [B, D])
        cT = s1("cT", [P, KD, B])
        ecT = s1("ecT", [P, KD, B])
        mods = s1("mods", [B, 6, D])
        mtmp = s1("mtmp", [B, D])
        mtmp2 = s1("mtmp2", [B, D])
        modT = s1("modT", [P, 8, B])
        xa = [s1(f"xa{n}", [P, NB, D]) for n in range(2)]
        xr = [s1(f"xr{n}", [P, NB, D]) for n in range(2)]
        mb = [s1(f"mb{n}", [P, 3, D]) for n in range(2)]
        mt = [s1(f"mt{n}", [P, 4]) for n in range(2)]
        mt2 = s1("mt2", [P, 4])
        xn2 = s1("xn2", [P, NB, D])
        mean2 = s1("mean2", [P, NB])
        xn = [s1(f"xn{n}", [P, NB, D]) for n in range(2)]
        st1 = s1("st1", [P, NB, 6])
        mv1 = s1("mv1", [P, NB, 2])
        ln1 = s1("ln1", [P, 4, NB])
        r1 = s1("r1", [P, NB])
        mean1 = s1("mean1", [P, NB])
        st2 = s1("st2", [P, NB, 6])
        mv2 = s1("mv2", [P, NB, 2])
        ln2 = s1("ln2", [P, 4, NB])
        r2 = s1("r2", [P, NB])
        hf = s1("hf", [P, KD, S])
        hh = [s1("hh0", [P, KD, S], F32R), batch1[0]]
        hl = [s1("hl0", [P, KD, S], F32R), batch1[1]]
        qh = [s1("qh0", [P, KD, S], F32R), batch1[2]]
        ql = [s1("ql0", [P, KD, S], F32R), batch1[3]]
        vh = [s1("vh0", [P, NB, D], F32R), batch1[4]]
        vl = [s1("vl0", [P, NB, D], F32R), batch1[5]]
        nmax = s1("nmax", [P, NB])
        rsum = s1("rsum", [P, NB])
        rinv = s1("rinv", [P, NB])
        pr = [s1(f"pr{n}", [P, S]) for n in range(2)]
        pth = [s1(f"pth{n}", [P, NB, P], F32R) for n in range(2)]
        ptl = [s1(f"ptl{n}", [P, NB, P], F32R) for n in range(2)]
        ob = s1("ob", [P, NB, D])
        rows = s1("rows", [P, 2 * NB, ROW])
        rows_i = rows[:, :, :].bitcast(I32)
        h2f = s1("h2f", [P, KD, S])
        lg = s1("lg", [P, NB, E])
        mx = s1("mx", [P, NB, E])
        mxi = s1("mxi", [P, NB, E], U32)
        idxf = s1("idxf", [P, NB, 2])
        o1 = s1("o1", [P, NB, E])
        o2 = s1("o2", [P, NB, E])
        picks = s1("picks", [P, NB, E], BF16)
        before = s1("before", [P, NB + 1, E], BF16)
        dl = s1("dl", [P, NB])
        el = s1("el", [P, NB])
        wt = s1("wt", [P, 3, NB])
        ra = s1("ra", [P, NB, E])
        rb = s1("rb", [P, NB, E])
        pos = s1("pos", [P, NB, E])
        pt1 = s1("pt1", [P, 2, NB, E])
        numbers = s1("numbers", [P, 2 * NB], I32)
        slotf = s1("slotf", [P, 2, NB])
        slots = [s1(f"slots{n}", [P, 2, NB], I32) for n in range(2)]
        cnt = s1("cnt", [1, 4, E])
        cnti = s1("cnti", [1, 2, E], I32)
        unit = s1("unit", [1, E])
        padf = s1("padf", [P, 3, E])
        ownp = s1("ownp", [P, E])
        one.close()

        expert_weights(1, ctx)
        stage1.append(sb("stage1b", [P, KD, F]))
        stage2.append(sb("stage2b", [P, KF, D]))
        xt = sb("xt", [P, TB, D])
        aux = sb("aux", [P, TB, AUX])
        aux_i = aux[:, :, :].bitcast(I32)
        xth = sb("xth", [P, KD, TT], F32R)
        xtl = sb("xtl", [P, KD, TT], F32R)
        gf = sb("gf", [P, KF, TT])
        gh = sb("gh", [P, KF, TT], F32R)
        gl = sb("gl", [P, KF, TT], F32R)
        ysc = sb("ysc", [P, TB, D])
        gcur = sb("gcur", [P, TB, D])
        num = [sb(f"num{n}", [P, TB], I32) for n in range(2)]

        ps = ctx.enter_context(nc.psum_tensor("ps", [P, 8, 512], F32))
        BANK_T, BANK_QA, BANK_QB, BANK_S, BANK_P, BANK_O = 0, 2, 3, 4, 6, 7
        BANK_H, BANK_Y, BANK_X = 0, 4, 6

        c_in = sem("c_in")
        w_in = sem("w_in")
        m_in = [sem(f"m_in{n}") for n in range(2)]
        r_in = sem("r_in")
        consts = sem("consts")
        iotas = sem("iotas")
        setup_pe = sem("setup_pe")
        setup_act = sem("setup_act")
        setup_dve = sem("setup_dve")
        mod_out = sem("mod_out")
        xa_in = [sem(f"xa_in{n}") for n in range(2)]
        xr_in = [sem(f"xr_in{n}") for n in range(2)]
        mb_in = [sem(f"mb_in{n}") for n in range(2)]
        gb_in = [sem(f"gb_in{n}") for n in range(2)]
        x1_out = [sem(f"x1_out{n}") for n in range(2)]
        scattered = [sem(f"scattered{n}") for n in range(2)]
        rows_free = sem("rows_free")
        mt_ready, mt2_ready = sem("mt_ready"), sem("mt2_ready")
        l1a, l1b, l2a, l2b = sem("l1a"), sem("l1b"), sem("l2a"), sem("l2b")
        l1_act, l2_act = sem("l1_act"), sem("l2_act")
        xn_ready = sem("xn_ready")
        t_done = sem("t_done")
        h_full = sem("h_full")
        h_hi, h_lo = sem("h_hi"), sem("h_lo")
        q_done, q_hi, q_lo = sem("q_done"), sem("q_hi"), sem("q_lo")
        v_done, v_hi, v_lo = sem("v_done"), sem("v_hi"), sem("v_lo")
        s_done, neg_max, p_exp = sem("s_done"), sem("neg_max"), sem("p_exp")
        pt_done, pt_hi, pt_lo = sem("pt_done"), sem("pt_hi"), sem("pt_lo")
        o_done, r_inv, o_scaled = sem("o_done"), sem("r_inv"), sem("o_scaled")
        x1_ready = sem("x1_ready")
        xn2_ready = sem("xn2_ready")
        h2_mid, h2_ready = sem("h2_mid"), sem("h2_ready")
        gt_done, g_full = sem("gt_done"), sem("g_full")
        lg_done, lg_read = sem("lg_done"), sem("lg_read")
        ra_s, rb_s, rc_s = sem("ra_s"), sem("rb_s"), sem("rc_s")
        el_done = sem("el_done")
        ps_done, ps_read = sem("ps_done"), sem("ps_read")
        cnt_done, tab_s = sem("cnt_done"), sem("tab_s")
        passed = sem("passed")
        over = sem("over")
        pad_out = sem("pad_out")
        pad_cur = sem("pad_cur")
        renumbered = sem("renumbered")
        st_in = [sem(f"st_in{n}") for n in range(2)]
        w_hi = sem("w_hi")
        w1_lo, w2_lo = sem("w1_lo"), sem("w2_lo")
        b_cur, b2_in = sem("b_cur"), sem("b2_in")
        xt_in, aux_in = sem("xt_in"), sem("aux_in")
        x_done = sem("x_done")
        x_hi, x_lo = sem("x_hi"), sem("x_lo")
        m1_done, g_act, g_hi, g_lo = sem("m1_done"), sem("g_act"), sem("g_hi"), sem("g_lo")
        m2_done, y_sum, y_sc = sem("m2_done"), sem("y_sum"), sem("y_sc")
        aux_read = sem("aux_read")
        added = sem("added")
        y_free = sem("y_free")
        dma_sems = [pad_out, renumbered, *xa_in, *xr_in, *mb_in, *gb_in, *x1_out, *scattered, added, aux_in, xt_in, *st_in, b2_in]
        clear = sem("clear")

        L1A, L1B, L2A, L2B, RA, RB, RC = 9, 4, 9, 4, 18, 8, 4
        RA_MAX, RA_GAP, RA_PICKS = NB, 2 * NB + 1, 2 * NB + 4
        N_TAB = 17

        block = ctx.enter_context(nc.Block())

        def phase_over(eng):
            eng.wait_ge(over, 4)

        def tile_range(eng, e):
            def load(col, low, high):
                at = tab[0:1, col:col + 1] if isinstance(col, int) else tab[0:1, bass.ds(col, 1)]
                return eng.value_load(at, min_val=low, max_val=high)
            return load(e + 0, 0, TILES - 1), load(e + 1, 1, TILES), load(e + 9, 0, E * CAP)

        def at(ap, v):
            return ap[bass.ds(v, 1)]

        def load_stage(eng, e, n):
            eng.dma_start(stage1[n][:, :, :], at(w1, e).rearrange("a (j p) f -> p (a j) f", p=P)).then_inc(st_in[n], 16)
            eng.dma_start(stage2[n][:, :, :], at(w2, e).rearrange("a (j p) d -> p (a j) d", p=P)).then_inc(st_in[n], 16)

        def load_b2(eng, e, half):
            eng.dma_start(b2row[half][:, :], at(b2, e).rearrange("a d -> (a d)").partition_broadcast(P)) \
               .then_inc(b2_in, 16)

        def chunk1(half, c):
            return half[:, :, c * F // CHUNKS:(c + 1) * F // CHUNKS]

        def chunk2(half, c):
            return half[:, c * KF // CHUNKS:(c + 1) * KF // CHUNKS, :]

        def wait_alone(eng, *waits):
            for sm, n in waits:
                (eng.wait_ge if any(sm is d for d in dma_sems) else lambda *w: wait(eng, *w))(sm, n)
            eng.sem_inc(passed, 1)

        @block.sync
        def _(sp):
            def load_xa(b):
                sp.dma_start(xa[b.half][:, :, :], at(xb, b.val).rearrange("a p i d -> p (a i) d")) \
                  .then_inc(xa_in[b.half], 16)

            sp.dma_start(c_s[:, :], c).then_inc(c_in, 16)
            sp.dma_start(rows64[:, :], b1.rearrange("e (j p) -> (e j) p", p=P)).then_inc(c_in, 16)
            first = Batch(0, 0, 0)
            for n, cols in enumerate((slice(0, 2 * D), slice(2 * D, 6 * D))):
                if n == 1:
                    load_xa(first)
                    for dst, src in ((wq_s, Wq), (wk_s, Wk), (wv_s, Wv)):
                        sp.dma_start(dst[:, :, :], src.rearrange("(j p) h -> p j h", p=P)).then_inc(w_in, 16)
                sp.dma_start(wmod_s[:, :, cols], wmod[:, cols].rearrange("(j p) n -> p j n", p=P)).then_inc(m_in[n], 16)
            load_xa(first.next())
            sp.dma_start(gw[:, :, :], gate_w.rearrange("(j p) e -> p j e", p=P)).then_inc(r_in, 16)
            for i in range(NB):
                sp.dma_start(gbias[:, i, :], gate_b.partition_broadcast(P)).then_inc(r_in, 16)

            wait(sp, setup_dve, SETUP_MODS)
            sp.dma_start(modd, mods[:, :, :].rearrange("b m d -> b (m d)")).then_inc(mod_out, 16)
            load_stage(sp, 0, 0)
            load_b2(sp, 0, 0)
            sp.wait_ge(mod_out, 16)

            def load_batch(b):
                sp.dma_start(xr[b.half][:, :, :], at(xb, b.val).rearrange("a p i d -> p (a i) d")) \
                  .then_inc(xr_in[b.half], 16)
                sp.dma_start(mb[b.half][:, :, :].rearrange("p m d -> p (m d)"),
                             at(modd, b.val)[:, 2 * D:5 * D].rearrange("a d -> (a d)").partition_broadcast(P)).then_inc(mb_in[b.half], 16)

            def load_gb(b):
                sp.dma_start(rows[:, b.half * NB:(b.half + 1) * NB, GB:GB + D],
                             at(modd, b.val)[:, 5 * D:6 * D].rearrange("a d -> (a d)").partition_broadcast(P)
                             .unsqueeze(1).to_broadcast([P, NB, D])).then_inc(gb_in[b.half], 16)

            def iteration(k, a, b, g):
                if k is None:
                    load_batch(a)
                    load_gb(a.next())
                    wait(sp, xn_ready, NB)
                    load_xa(a.next().next())
                    return
                if there(k, 3):
                    wait(sp, xn_ready, NB * (k.val + 2))
                    load_xa(k.next().next().next())
                if g is not None:
                    wait(sp, rows_free, g.val)
                    load_gb(g)
                if a is not None:
                    if g is not None:
                        wait(sp, h2_ready, NB * (g.val + 1))
                        sp.wait_ge(x1_out[g.half], 16 * (g.pair + 1))
                    load_batch(a)
                if b is not None:
                    wait(sp, x1_ready, NB * (b.val + 1))
                    sp.dma_start(at(outb, b.val).rearrange("a p i d -> p (a i) d"), xr[b.half][:, :, :]) \
                      .then_inc(x1_out[b.half], 16)

            over_batches(sp, iteration)
            wait(sp, w1_lo, CHUNKS)
            wait(sp, w2_lo, CHUNKS)
            load_stage(sp, 1, 0)
            wait(sp, tab_s, N_TAB)

            def pad_list(e):
                end = sp.value_load(tab[0:1, bass.ds(e + 17, 1)], min_val=0, max_val=E * CAP - TT)
                sp.dma_start(lists[bass.ds(end, TT), :].rearrange("(s p) c -> p s c", p=P), pad[:, :, :]) \
                  .then_inc(pad_out, 16)

            for e in range(2):
                pad_list(e)
            phase_over(sp)
            for half in range(2):
                sp.wait_ge(x1_out[half], 16 * (B // 2))
                sp.wait_ge(scattered[half], 16 * 2 * NB * (B // 2 + half))

            def load_xt(row):
                sp.dma_start(xt[:, :, :], lists[bass.ds(row, TT), 0:D].rearrange("(s p) d -> p s d", p=P)) \
                  .then_inc(xt_in, 16)

            def load_tile(g, base):
                row = nc.s_assert_within(sp.snap(g * TT + base), 0, E * CAP - TT,
                                         skip_runtime_bounds_check_because="a list's tiles lie within it")
                wait(sp, x_done, g)
                load_xt(row)
                wait(sp, aux_read, (TB + 1) * g)
                sp.dma_start(aux[:, :, :], lists[bass.ds(row, TT), D:ROW].rearrange("(s p) d -> p s d", p=P)) \
                  .then_inc(aux_in, 16)

            def expert(e, half, later):
                lo, hi, base = tile_range(sp, e)
                wait_alone(sp, (renumbered, 16 * (e + 1)))
                load_tile(lo, base)
                if later >= 2:
                    wait_alone(sp, (renumbered, 16 * (e + 2)))
                    pad_list(e + 2)
                with sp.If(lo + 1 < hi):
                    with sp.Fori(lo + 1, hi) as g:
                        load_tile(g, base)

            over_experts(sp, expert)
            total = sp.value_load(tab[0:1, E:E + 1], min_val=E, max_val=TILES)
            wait(sp, x_done, total)
            load_xt(0)

        @block.gpsimd
        def _(pool):
            start(pool, h_lo, x1_ready, h2_mid, h2_ready, w2_lo, rows_free, y_free)
            pool.memset(ident[:, :], 0.0).then_inc(consts, 1)
            pool.memset(maskb[:, :], 0.0).then_inc(consts, 1)
            pool.memset(identb[:, :], 0.0).then_inc(consts, 1)
            pool.memset(trib[:, :], 0.0).then_inc(consts, 1)
            pool.memset(onesb[:, :], 1.0).then_inc(consts, 1)
            pool.wait_ge(consts, 5)
            pool.affine_select(out=ident[:, :], in_=ident[:, :], compare_op=ALU.not_equal, fill=1.0,
                               base=0, pattern=[[-1, P]], channel_multiplier=1).then_inc(consts, 1)
            pool.affine_select(out=identb[:, :], in_=identb[:, :], compare_op=ALU.not_equal, fill=1.0,
                               base=0, pattern=[[-1, P]], channel_multiplier=1).then_inc(consts, 1)
            pool.affine_select(out=maskb[:, :], in_=maskb[:, :], compare_op=ALU.is_ge, fill=MASKED,
                               base=0, pattern=[[-1, P]], channel_multiplier=1).then_inc(consts, 1)
            pool.affine_select(out=trib[:, :], in_=trib[:, :], compare_op=ALU.is_ge, fill=1.0,
                               base=0, pattern=[[-1, P]], channel_multiplier=1).then_inc(consts, 1)
            pool.iota(iota8[:, :, :], [[0, NB], [1, E]], base=0, channel_multiplier=0,
                      allow_small_or_imprecise_dtypes=True).then_inc(iotas, 1)
            pool.iota(ecap[:, :, :], [[0, NB], [1, E]], base=0, channel_multiplier=0,
                      allow_small_or_imprecise_dtypes=True).then_inc(iotas, 1)
            pool.memset(rows[:, :, RW:ROW], 0.0).then_inc(iotas, 1)
            pool.memset(pad[:, :, :], 0.0).then_inc(iotas, 1)
            pool.memset(rows[:, NB:2 * NB, 0:D], 0.0).then_inc(iotas, 1)
            pool.memset(slots[1][:, :, :], E * CAP).then_inc(iotas, 1)
            pool.memset(others[:, :], 0.0).then_inc(iotas, 1)
            pool.iota(ownp[:, :], [[0, E]], base=0, channel_multiplier=1,
                      allow_small_or_imprecise_dtypes=True).then_inc(iotas, 1)
            pool.wait_ge(iotas, 8)
            pool.iota(others[:, :].bitcast(I32)[:, ID - RW:ID - RW + 1], [[0, 1]], base=NT - P, channel_multiplier=1) \
                .then_inc(iotas, 1)
            pool.iota(numbers[:, :], [[P, 2 * NB]], base=-2 * S, channel_multiplier=1).then_inc(iotas, 1)
            pool.iota(pad[:, :, :].bitcast(I32)[:, :, ID], [[0, TB]], base=0, channel_multiplier=1).then_inc(iotas, 1)
            pool.tensor_scalar(ecap[:, :, :], ecap[:, :, :], float(CAP), 0.0, ALU.mult, ALU.add).then_inc(iotas, 1)

            def split_rest(e, half, c, n):
                wait(pool, w_hi, 2 * CHUNKS * e + CHUNKS + c + 1)
                pool.tensor_tensor(chunk2(w2l[half], c), chunk2(stage2[n], c), chunk2(w2h[half], c).bitcast(F32),
                                   ALU.subtract).then_inc(w2_lo, 1)

            def hT_rest(b, j):
                wait(pool, h_hi, KD * b.val + j + 1)
                wait(pool, h_full, KD * b.val + j + 1)
                wait(pool, s_done, NB * (b.val - 1))
                pool.tensor_tensor(hl[b.half][:, j, :], hf[:, j, :], hh[b.half][:, j, :].bitcast(F32),
                                   ALU.subtract).then_inc(h_lo, 1)

            def residual(b, i):
                wait(pool, o_scaled, NB * b.val + i + 1)
                if i == 0:
                    pool.wait_ge(xr_in[b.half], 16 * (b.pair + 1))
                pool.tensor_tensor(xr[b.half][:, i, :], xr[b.half][:, i, :], ob[:, i, :], ALU.add) \
                    .then_inc(x1_ready, 1)

            def scale2(b, i):
                if i == 0:
                    wait(pool, rows_free, b.val)
                wait(pool, xn2_ready, NB * b.val + i + 1)
                pool.tensor_tensor(rows[:, b.half * NB + i, 0:D], xn2[:, i, :], mb[b.half][:, 2, :], ALU.mult) \
                    .then_inc(h2_mid, 1)

            def shift2(b, i):
                row = rows[:, b.half * NB + i, 0:D]
                wait(pool, h2_mid, NB * b.val + i + 1)
                pool.tensor_tensor(row, row, mb[b.half][:, 1, :], ALU.add).then_inc(h2_ready, 1)

            def scattered_all(b):
                wait_alone(pool, (scattered[b.half], 16 * 2 * NB * (b.pair + 1 + b.half)))
                pool.sem_inc(rows_free, 1)

            def scatter_begin(b):
                wait_alone(pool, (rc_s, RC * (b.val + 1)), (rb_s, RB * (b.val + 1)),
                           (h2_ready, NB * (b.val + 1)))
                wait_alone(pool, (gb_in[b.half], 16 * (b.pair + 1 + b.half)))

            def scatter(b, i):
                for pick in range(2):
                    pool.indirect_dma_start(
                        lists, bass.IndirectOffsetOnAxis(ap=slots[b.half][:, pick, i:i + 1], axis=0),
                        rows[:, b.half * NB + i, :], None, bounds_check=E * CAP - 1, oob_is_err=False) \
                        .then_inc(scattered[b.half], 16)

            def iteration(k, a, b, g):
                more = there(a, 1)
                if k is None:
                    for n in (a, a.next()):
                        for j in range(KD):
                            hT_rest(n, j)
                    return
                gone = g.prev() if g is not None else None
                if gone is not None:
                    scatter_begin(gone)
                    scatter(gone, 0)
                    scatter(gone, 1)
                if g is not None:
                    scale2(g, 0)
                if gone is not None:
                    scatter(gone, 2)
                if b is not None:
                    residual(b, 0)
                if g is not None:
                    scale2(g, 1)
                    shift2(g, 0)
                    scale2(g, 2)
                if b is not None:
                    residual(b, 1)
                if g is not None:
                    shift2(g, 1)
                if gone is not None:
                    scatter(gone, 3)
                if g is not None:
                    scale2(g, 3)
                    shift2(g, 2)
                if more:
                    hT_rest(a.next(), 0)
                if g is not None:
                    shift2(g, 3)
                if b is not None:
                    residual(b, 2)
                if more:
                    hT_rest(a.next(), 1)
                if b is not None:
                    residual(b, 3)
                if gone is not None:
                    scattered_all(gone)

            over_batches(pool, iteration)
            last = Batch(B - 1, (B - 1) % 2, (B - 1) // 2)
            scatter_begin(last)
            for i in range(NB):
                scatter(last, i)
            def renumber(column):
                pool.indirect_dma_start(
                    lists_short, bass.IndirectOffsetOnAxis(ap=column, axis=0), others[:, :], None,
                    bounds_check=E * CAP * ROW // SHORT - 1, oob_is_err=False).then_inc(renumbered, 16)

            wait(pool, tab_s, N_TAB)
            pool.wait_ge(pad_out, 32)
            renumber(padslots[:, 0:1])
            for half in range(2):
                pool.wait_ge(scattered[half], 16 * 2 * NB * (B // 2 + half))
            pool.wait_ge(renumbered, 16)
            pool.engine_nop().then_inc(over, 1)
            phase_over(pool)
            renumber(padslots[:, 1:2])
            pool.wait_ge(clear, 4)
            for half in range(2):
                pool.wait_ge(x1_out[half], 16 * (B // 2))

            def add_rows(g, n):
                wait_alone(pool, (y_sc, 2 * g + 2))
                pool.indirect_dma_start(
                    out_rows, bass.IndirectOffsetOnAxis(ap=num[1][:, n:n + 1], axis=0),
                    ysc[:, n, :], None, compute_op=ALU.add).then_inc(added, 16)

            def rows_added(g, n):
                wait_alone(pool, (added, 32 * g + 16 * (n + 1)))
                if n == TB - 1:
                    pool.sem_inc(y_free, 1)

            def expert(e, half, later):
                lo, hi, base = tile_range(pool, e)
                for n in range(TB):
                    add_rows(lo, n)
                    if later:
                        split_rest(e + 1, 1 - half, 2 * n, half)
                        split_rest(e + 1, 1 - half, 2 * n + 1, half)
                    rows_added(lo, n)
                if later >= 2:
                    wait_alone(pool, (pad_cur, e + 1), (pad_out, 16 * (e + 3)))
                    renumber(padcur[:, :])
                with pool.If(lo + 1 < hi):
                    with pool.Fori(lo + 1, hi) as g:
                        for n in range(TB):
                            add_rows(g, n)
                            rows_added(g, n)

            over_experts(pool, expert)
            total = pool.value_load(tab[0:1, E:E + 1], min_val=E, max_val=TILES)
            for n in range(TB):
                add_rows(total, n)
                rows_added(total, n)

        @block.scalar
        def _(act):
            start(act, xn_ready, xn2_ready, h_hi, h_full, q_hi, v_hi, p_exp, pt_hi, g_full, el_done, l1_act, l2_act, w_hi,
                  x_hi, g_act)
            act.preload_act_table_set("natural_log_exp_and_others")
            wait(act, setup_dve, 1)
            act.activation(ecT[:, :, :], cT[:, :, :], ACT.Exp, scale=-1.0).then_inc(setup_act, 1)

            def seed(b, sem_in, per, buf, sem_out):
                wait(act, sem_in, per * (b.val + 1))
                act.activation(buf[:, 1, :], buf[:, 0, :], ACT.Ln, bias=0.0).then_inc(sem_out, 1)
                wait(act, sem_out, 2 * b.val + 1)
                act.activation(buf[:, 2, :], buf[:, 1, :], ACT.Exp, scale=-0.5).then_inc(sem_out, 1)

            def normalise(b, blocks=range(NB)):
                if 0 in blocks:
                    wait(act, l1b, L1B * (b.val + 1))
                    act.wait_ge(xa_in[b.half], 16 * (b.pair + 1))
                    wait(act, t_done, b.val - 1)
                for i in blocks:
                    act.activation(xn[b.half][:, i, :], xa[b.half][:, i, :], ACT.Identity,
                                   bias=mean1[:, i:i + 1], scale=r1[:, i:i + 1]).then_inc(xn_ready, 1)

            def normalise2(b, blocks):
                if 0 in blocks:
                    wait(act, l2b, L2B * (b.val + 1))
                    wait(act, gt_done, b.val)
                    wait(act, h2_mid, NB * b.val)
                for i in blocks:
                    act.activation(xn2[:, i, :], xr[b.half][:, i, :], ACT.Identity,
                                   bias=mean2[:, i:i + 1], scale=r2[:, i:i + 1]).then_inc(xn2_ready, 1)

            def hT(b, blocks=range(KD)):
                if 0 in blocks:
                    wait(act, mt_ready, b.val + 1)
                    wait(act, t_done, b.val + 1)
                    wait(act, h_lo, KD * b.val)
                    wait(act, s_done, NB * (b.val - 1))
                for j in blocks:
                    sa, ca = mt[b.half][:, j:j + 1], mt[b.half][:, KD + j:KD + j + 1]
                    act.activation(hh[b.half][:, j, :], ps[:, BANK_T + j, :], ACT.Identity, bias=sa, scale=ca) \
                       .then_inc(h_hi, 1)
                    act.activation(hf[:, j, :], ps[:, BANK_T + j, :], ACT.Identity, bias=sa, scale=ca) \
                       .then_inc(h_full, 1)

            def exps(b, i):
                wait(act, neg_max, NB * b.val + i + 1)
                wait(act, pt_done, NB * b.val + i - 1)
                act.activation(pr[i % 2][:, 0:(i + 1) * P], ps[:, BANK_S + i % 2, 0:(i + 1) * P], ACT.Exp,
                               bias=nmax[:, i:i + 1], accum_out=rsum[:, i:i + 1]).then_inc(p_exp, 1)

            def probs_hi(b, i):
                wait(act, pt_done, NB * b.val + i + 1)
                wait(act, o_done, NB * b.val + i - 1)
                act.activation(pth[i % 2][:, 0:i + 1, :],
                               ps[:, BANK_P, 0:(i + 1) * P].rearrange("p (j q) -> p j q", q=P),
                               ACT.Copy).then_inc(pt_hi, 1)

            def queries_hi(b, m):
                wait(act, q_done, KD * b.val + m + 1)
                wait(act, s_done, NB * (b.val - 1))
                act.activation(qh[b.half][:, m, :], ps[:, BANK_QA + m, :], ACT.Copy).then_inc(q_hi, 1)

            def values_hi(b, p):
                wait(act, v_done, 2 * b.val + p + 1)
                wait(act, o_done, NB * (b.val - 1))
                act.activation(vh[b.half][:, 2 * p:2 * p + 2, :],
                               ps[:, BANK_QA + p, :].rearrange("p (i d) -> p i d", i=2), ACT.Copy).then_inc(v_hi, 1)

            def h2T(b):
                wait(act, gt_done, b.val + 1)
                wait(act, lg_done, b.val)
                wait(act, mt2_ready, b.val + 1)
                for j in range(KD):
                    act.activation(h2f[:, j, :], ps[:, BANK_T + j, :], ACT.Identity, bias=mt2[:, j:j + 1],
                                   scale=mt2[:, KD + j:KD + j + 1]).then_inc(g_full, 1)

            def exp_gap(b):
                wait(act, ra_s, RA * b.val + RA_GAP)
                wait(act, rb_s, RB * b.val)
                act.activation(el[:, :], dl[:, :], ACT.Exp).then_inc(el_done, 1)

            def round_weights(half, c, n):
                chunk, stage, hi = (chunk1, stage1[n], w1h[half]) if c < CHUNKS else (chunk2, stage2[n], w2h[half])
                act.activation(chunk(hi, c % CHUNKS), chunk(stage, c % CHUNKS), ACT.Copy).then_inc(w_hi, 1)

            def iteration(k, a, b, g):
                more = there(a, 1)
                if k is None:
                    seed(a, l1a, L1A, ln1, l1_act)
                    normalise(a)
                    hT(a)
                    seed(a.next(), l1a, L1A, ln1, l1_act)
                    normalise(a.next())
                    for m in range(KD):
                        queries_hi(a, m)
                    hT(a.next())
                    for p in range(2):
                        values_hi(a, p)
                    return
                if b is not None:
                    exps(b, 0)
                    exps(b, 1)
                    probs_hi(b, 0)
                if g is not None:
                    seed(g, l2a, L2A, ln2, l2_act)
                if b is not None:
                    probs_hi(b, 1)
                    exps(b, 2)
                if g is not None:
                    normalise2(g, (0, 1))
                if a is not None:
                    queries_hi(a, 0)
                if g is not None:
                    normalise2(g, (2, 3))
                if b is not None:
                    probs_hi(b, 2)
                if a is not None:
                    queries_hi(a, 1)
                if more:
                    seed(a.next(), l1a, L1A, ln1, l1_act)
                if b is not None:
                    exps(b, 3)
                if g is not None:
                    h2T(g)
                if more:
                    normalise(a.next(), (0, 1))
                    normalise(a.next(), (2, 3))
                if a is not None:
                    values_hi(a, 0)
                if b is not None:
                    probs_hi(b, 3)
                if more:
                    hT(a.next(), (0,))
                    hT(a.next(), (1,))
                if g is not None:
                    exp_gap(g)
                if a is not None:
                    values_hi(a, 1)
                if a is None and b is not None:
                    act.wait_ge(st_in[0], 32)
                    for c in range(2 * CHUNKS):
                        round_weights(0, c, 0)

            over_batches(act, iteration)
            act.preload_act_table_set("gelu_and_others")
            wait(act, el_done, B)
            act.sem_inc(over, 1)
            phase_over(act)

            def tokens_hi(n):
                wait(act, x_done, n)
                act.activation(xth[:, :, :], ps[:, BANK_X, :].rearrange("p (j t) -> p j t", j=KD), ACT.Copy) \
                   .then_inc(x_hi, 1)

            tokens_hi(1)
            load_stage(act, 2, 1)

            def tile(g, half, more):
                for j in range(KF):
                    more(j)
                    wait(act, m1_done, KF * g + j + 1)
                    act.activation(gf[:, j, :], ps[:, BANK_H + j % 4, 0:TT], ACT.Gelu,
                                   bias=bcur[half][:, j:j + 1]).then_inc(g_act, 1)
                tokens_hi(g + 2)

            def expert(e, half, later):
                lo, hi, base = tile_range(act, e)
                wait(act, b_cur, e + 1)

                def split(j):
                    if later:
                        if j == 0:
                            act.wait_ge(st_in[half], 16 * e + (64, 16)[half])
                            wait(act, m2_done, lo)
                        round_weights(1 - half, j, half)

                tile(lo, half, split)
                if later:
                    wait(act, y_sum, lo + 1)
                    load_b2(act, e + 1, 1 - half)
                if later == 3:
                    wait(act, w1_lo, CHUNKS * (e + 2))
                    wait(act, w2_lo, CHUNKS * (e + 2))
                    load_stage(act, e + 3, half)
                with act.If(lo + 1 < hi):
                    with act.Fori(lo + 1, hi) as g:
                        tile(g, half, lambda j: None)

            over_experts(act, expert)

        @block.vector
        def _(dve):
            start(dve, setup_dve, tab_s, mt_ready, l1a, l1b, l2a, l2b, q_lo, v_lo, neg_max, pt_lo, r_inv, o_scaled,
                       mt2_ready, lg_read, ra_s, rb_s, rc_s, ps_read, w1_lo, b_cur, pad_cur, x_lo, g_hi,
                       g_lo, y_sum, y_sc, aux_read)
            def moments(mv, st, ln, chain):
                wait_alone(dve, chain.so_far())
                for i in range(NB):
                    chain.step(dve.bn_aggr(mv[:, i, :], st[:, i, :]))
                chain.done()
                chain.step(dve.tensor_scalar(ln[:, 0, :], mv[:, :, 1], EPS, None, ALU.add))

            def refine(ln, r, chain):
                chain.step(dve.tensor_tensor(ln[:, 3, :], ln[:, 2, :], ln[:, 2, :], ALU.mult))
                chain.done()
                chain.step(dve.scalar_tensor_tensor(ln[:, 3, :], ln[:, 3, :], -0.5, ln[:, 0, :], ALU.mult, ALU.mult))
                chain.done()
                chain.step(dve.scalar_tensor_tensor(r[:, :], ln[:, 3, :], 1.5, ln[:, 2, :], ALU.add, ALU.mult))

            def norm1_a(b):
                wait(dve, xn_ready, NB * b.val)
                dve.wait_ge(xa_in[b.half], 16 * (b.pair + 1))
                chain = Chain(dve, l1a, L1A, b.val)
                for i in range(NB):
                    chain.step(dve.bn_stats(st1[:, i, :], xa[b.half][:, i, :]))
                moments(mv1, st1, ln1, chain)

            def norm1_b(b):
                wait(dve, l1_act, 2 * b.val + 2)
                chain = Chain(dve, l1b, L1B, b.val)
                refine(ln1, r1, chain)
                chain.done()
                chain.step(dve.scalar_tensor_tensor(mean1[:, :], mv1[:, :, 0], -1.0, r1[:, :], ALU.mult, ALU.mult))

            def mod_columns(b):
                wait(dve, h_full, KD * (b.val - 1))
                src = modT[:, 0:4, b.val:b.val + 1] if isinstance(b.val, int) else modT[:, 0:4, bass.ds(b.val, 1)]
                dve.tensor_scalar(mt[b.half][:, :].unsqueeze(2), src, 0.0, None, ALU.add).then_inc(mt_ready, 1)

            ch = Chain(dve, setup_dve, 64, 0)
            dve.wait_ge(consts, 9)
            dve.wait_ge(setup_pe, 1)
            ch.step(dve.tensor_copy(cT[:, :, :], ps[:, 6, 0:KD * B].rearrange("p (j b) -> p j b", j=KD)))
            ch.step(dve.tensor_copy(biasT[:, :], ps[:, 6, 16:16 + E * KF]))
            dve.wait_ge(setup_act, 1)
            ch.step(dve.tensor_scalar(ecT[:, :, :], ecT[:, :, :], 1.0, None, ALU.add))
            ch.done()
            ch.step(dve.reciprocal(ecT[:, :, :], ecT[:, :, :]))
            ch.done()
            ch.step(dve.tensor_tensor(cT[:, :, :], cT[:, :, :], ecT[:, :, :], ALU.mult))
            assert ch.n == SETUP_SILU
            norm1_a(Batch(0, 0, 0))
            dve.wait_ge(setup_pe, 2)
            ch.step(dve.tensor_copy(mods[:, 0:2, :].rearrange("b m d -> b (m d)"), ps[0:B, 3, :]))
            ch.done()
            ch.step(dve.tensor_scalar(mods[:, 1, :], mods[:, 1, :], 1.0, None, ALU.add))
            assert ch.n == SETUP_FIRST, ch.n
            norm1_b(Batch(0, 0, 0))
            dve.wait_ge(setup_pe, 3)
            ch.step(dve.tensor_copy(modT[:, 0:4, :], ps[:, 6, 0:4 * B].rearrange("p (m b) -> p m b", b=B)))
            ch.done()
            mod_columns(Batch(0, 0, 0))
            dve.wait_ge(setup_pe, 4)
            m_ps = ps[:, 2, :].rearrange("p (j h) -> p j h", j=KD)
            ch.step(dve.tensor_scalar(mh[:, :, :], m_ps, 1.0 / 16, None, ALU.mult))
            ch.done()
            ch.step(dve.scalar_tensor_tensor(ml[:, :, :], m_ps, 1.0 / 16, mh[:, :, :].bitcast(F32),
                                             ALU.mult, ALU.subtract))
            wv_ps = ps[:, 7, :].rearrange("p (j o) -> p j o", j=KD)
            ch.step(dve.tensor_copy(wvh[:, :, :], wv_ps))
            ch.done()
            ch.step(dve.tensor_tensor(wvl[:, :, :], wv_ps, wvh[:, :, :].bitcast(F32), ALU.subtract))
            norm1_a(Batch(1, 1, 0))
            norm1_b(Batch(1, 1, 0))
            mod_columns(Batch(1, 1, 0))
            dve.wait_ge(setup_pe, 5)
            ch.step(dve.tensor_copy(mods[:, 2:6, :].rearrange("b m d -> b (m d)"),
                                    ps[0:B, 4:6, :].rearrange("b m d -> b (m d)")))
            ch.done()
            ch.step(dve.tensor_scalar(mods[:, 4, :], mods[:, 4, :], 1.0, None, ALU.add))
            for n in (2, 5):
                gate = mods[:, n, :]
                ch.done()
                ch.step(dve.scalar_tensor_tensor(mtmp[:, :], gate, -1.0, gate, ALU.mult, ALU.max))
                ch.done()
                ch.step(dve.tensor_scalar(mtmp[:, :], mtmp[:, :], 0.25, None, ALU.max))
                ch.step(dve.tensor_scalar(mtmp2[:, :], gate, 0.0, 2.0, ALU.is_ge, ALU.mult))
                ch.done()
                ch.step(dve.scalar_tensor_tensor(gate, mtmp2[:, :], -1.0, mtmp[:, :], ALU.add, ALU.mult))
            assert ch.n == SETUP_MODS, ch.n
            ch.step(dve.memset(before[:, NB, :], 0.0))
            ch.step(dve.memset(unit[:, :], 1.0))
            ch.done()
            dve.wait_ge(iotas, 12)
            dve.wait_ge(r_in, 16 * (1 + NB))

            def biases(e, half):
                dve.tensor_scalar(bcur[half][:, :], biasT[:, bass.ds(e * KF, KF)], 0.0, None, ALU.add) \
                   .then_inc(b_cur, 1)

            def split_first():
                for c in range(CHUNKS):
                    split_rest(0, 0, c, 0)
                for c in range(CHUNKS):
                    wait(dve, w_hi, CHUNKS + c + 1)
                    dve.tensor_tensor(chunk2(w2l[0], c), chunk2(stage2[0], c), chunk2(w2h[0], c).bitcast(F32),
                                      ALU.subtract).then_inc(w2_lo, 1)

            def split_rest(e, half, c, n):
                wait(dve, w_hi, 2 * CHUNKS * e + c + 1)
                dve.tensor_tensor(chunk1(w1l[half], c), chunk1(stage1[n], c), chunk1(w1h[half], c).bitcast(F32),
                                  ALU.subtract).then_inc(w1_lo, 1)

            def mod_columns2(b):
                wait(dve, g_full, KD * b.val)
                src = modT[:, 4:8, b.val:b.val + 1] if isinstance(b.val, int) else modT[:, 4:8, bass.ds(b.val, 1)]
                dve.tensor_scalar(mt2[:, :].unsqueeze(2), src, 0.0, None, ALU.add).then_inc(mt2_ready, 1)

            def queries_lo(b, m):
                wait(dve, q_hi, KD * b.val + m + 1)
                dve.tensor_tensor(ql[b.half][:, m, :], ps[:, BANK_QA + m, :], qh[b.half][:, m, :].bitcast(F32),
                                  ALU.subtract).then_inc(q_lo, 1)

            def values_lo(b, p):
                wait(dve, v_hi, 2 * b.val + p + 1)
                dve.tensor_tensor(vl[b.half][:, 2 * p:2 * p + 2, :],
                                  ps[:, BANK_QA + p, :].rearrange("p (i d) -> p i d", i=2),
                                  vh[b.half][:, 2 * p:2 * p + 2, :].bitcast(F32), ALU.subtract).then_inc(v_lo, 1)

            def row_max(b, i):
                wait(dve, s_done, NB * b.val + i + 1)
                dve.tensor_reduce(nmax[:, i:i + 1], ps[:, BANK_S + i % 2, 0:(i + 1) * P], AX.X, ALU.max,
                                  negate=True).then_inc(neg_max, 1)

            def probs_lo(b, i):
                wait(dve, pt_hi, NB * b.val + i + 1)
                dve.tensor_tensor(ptl[i % 2][:, 0:i + 1, :],
                                  ps[:, BANK_P, 0:(i + 1) * P].rearrange("p (j q) -> p j q", q=P),
                                  pth[i % 2][:, 0:i + 1, :].bitcast(F32), ALU.subtract).then_inc(pt_lo, 1)

            def scale_out(b, i):
                wait(dve, o_done, NB * b.val + i + 1)
                if i == 0:
                    dve.wait_ge(mb_in[b.half], 16 * (b.pair + 1))
                dve.reciprocal(rinv[:, i:i + 1], rsum[:, i:i + 1]).then_inc(r_inv, 1)
                wait(dve, r_inv, NB * b.val + i + 1)
                wait(dve, x1_ready, NB * (b.val - 1) + i + 1)
                dve.scalar_tensor_tensor(ob[:, i, :], ps[:, BANK_O, (i % 2) * D:(i % 2 + 1) * D], rinv[:, i:i + 1],
                                         mb[b.half][:, 0, :], ALU.mult, ALU.mult).then_inc(o_scaled, 1)

            def stats2(b, i):
                wait(dve, x1_ready, NB * b.val + i + 1)
                Chain(dve, l2a, L2A, b.val, i).step(dve.bn_stats(st2[:, i, :], xr[b.half][:, i, :]))

            def norm2_a(b):
                moments(mv2, st2, ln2, Chain(dve, l2a, L2A, b.val, NB))

            def norm2_b(b):
                wait(dve, l2_act, 2 * b.val + 2)
                wait(dve, xn2_ready, NB * b.val)
                chain = Chain(dve, l2b, L2B, b.val)
                refine(ln2, r2, chain)
                chain.done()
                chain.step(dve.scalar_tensor_tensor(mean2[:, :], mv2[:, :, 0], -1.0, r2[:, :], ALU.mult, ALU.mult))

            def route_max(b):
                wait(dve, lg_done, b.val + 1)
                chain = Chain(dve, ra_s, RA, b.val)
                dve.tensor_tensor(lg[:, :, :], ps[:, BANK_QB, 0:NB * E].rearrange("p (i e) -> p i e", e=E),
                                  gbias[:, :, :], ALU.add).then_inc(lg_read, 1)
                wait_alone(dve, (lg_read, b.val + 1))
                for i in range(NB):
                    chain.step(dve.max(mx[:, i, :], lg[:, i, :]))
                assert chain.n == RA_MAX

            def route_index(b):
                chain = Chain(dve, ra_s, RA, b.val, RA_MAX)
                wait_alone(dve, chain.so_far())
                for i in range(NB):
                    chain.step(dve.max_index(mxi[:, i, :], mx[:, i, :], lg[:, i, :]))
                chain.step(dve.tensor_tensor(dl[:, :], mx[:, :, 1], mx[:, :, 0], ALU.subtract))
                assert chain.n == RA_GAP

            def route_number(b):
                chain = Chain(dve, ra_s, RA, b.val, RA_GAP)
                chain.done()
                chain.step(dve.tensor_copy(idxf[:, :, :], mxi[:, :, 0:2]))

            def route_picks(b):
                chain = Chain(dve, ra_s, RA, b.val, RA_GAP + 1)
                chain.done()
                for n, o in enumerate((o1, o2)):
                    chain.step(dve.tensor_tensor(o[:, :, :], iota8[:, :, :],
                                                 idxf[:, :, n:n + 1].to_broadcast([P, NB, E]), ALU.is_equal))
                assert chain.n == RA_PICKS

            def route_before(b, part):
                chain = Chain(dve, ra_s, RA, b.val, RA_PICKS + (0, 4)[part])
                chain.done()
                if part == 0:
                    wait(dve, ps_done, b.val)
                    chain.step(dve.tensor_tensor(picks[:, :, :], o1[:, :, :], o2[:, :, :], ALU.add))
                    chain.step(dve.tensor_copy(before[:, 0, :], before[:, NB, :]))
                for i in ((0, 1), (2, 3))[part]:
                    chain.done()
                    chain.step(dve.tensor_tensor(before[:, i + 1, :], before[:, i, :], picks[:, i, :], ALU.add))

            def route_b(b):
                own = slice(b.half * NB, (b.half + 1) * NB)
                chain = Chain(dve, rb_s, RB, b.val)
                wait(dve, rows_free, b.val)
                wait(dve, el_done, b.val + 1)
                chain.step(dve.tensor_scalar(wt[:, 0, :], el[:, :], 1.0, None, ALU.add))
                chain.step(dve.tensor_scalar(numbers[:, own], numbers[:, own], float(2 * S), None, ALU.add))
                chain.done()
                chain.step(dve.reciprocal(wt[:, 1, :], wt[:, 0, :]))
                chain.step(dve.tensor_copy(rows_i[:, own, ID], numbers[:, own]))
                chain.done()
                chain.step(dve.tensor_tensor(wt[:, 2, :], wt[:, 1, :], el[:, :], ALU.mult))
                chain.step(dve.tensor_tensor(ra[:, :, :], o1[:, :, :],
                                             wt[:, 1, :].unsqueeze(2).to_broadcast([P, NB, E]), ALU.mult))
                chain.done()
                chain.step(dve.tensor_tensor(rb[:, :, :], o2[:, :, :],
                                             wt[:, 2, :].unsqueeze(2).to_broadcast([P, NB, E]), ALU.mult))
                chain.done()
                chain.step(dve.tensor_tensor(rows[:, own, RW:RW + E], ra[:, :, :], rb[:, :, :], ALU.add))

            def route_c(b):
                chain = Chain(dve, rc_s, RC, b.val)
                wait(dve, ps_done, b.val + 1)
                dve.tensor_tensor(pos[:, :, :], ps[:, BANK_QA, 0:NB * E].rearrange("p (i e) -> p i e", e=E),
                                  ecap[:, :, :], ALU.add).then_inc(ps_read, 1)
                wait(dve, ps_read, b.val + 1)
                chain.step(dve.tensor_tensor(pt1[:, 0, :, :], pos[:, :, :], o1[:, :, :], ALU.mult))
                chain.step(dve.tensor_tensor(pt1[:, 1, :, :], pos[:, :, :], o2[:, :, :], ALU.mult))
                chain.done()
                chain.step(dve.tensor_reduce(slotf[:, :, :], pt1[:, :, :, :], AX.X, ALU.add))
                chain.done()
                chain.step(dve.tensor_copy(slots[b.half][:, :, :], slotf[:, :, :]))

            def iteration(k, a, b, g):
                more = there(a, 1)
                if k is None:
                    for m in range(KD):
                        queries_lo(a, m)
                    dve.wait_ge(setup_pe, 6)
                    ch.step(dve.tensor_copy(modT[:, 4:8, :], ps[:, 6, 4 * B:8 * B].rearrange("p (m b) -> p m b", b=B)))
                    ch.done()
                    for p in range(2):
                        values_lo(a, p)
                    biases(0, 0)
                    return
                if b is not None:
                    row_max(b, 0)
                    row_max(b, 1)
                if more:
                    mod_columns(a.next())
                if g is not None:
                    stats2(g, 3)
                    mod_columns2(g)
                    norm2_a(g)
                if b is not None:
                    probs_lo(b, 0)
                    row_max(b, 2)
                if g is not None:
                    norm2_b(g)
                if b is None:
                    split_first()
                if b is not None:
                    scale_out(b, 0)
                    probs_lo(b, 1)
                if more:
                    norm1_a(a.next())
                if b is not None:
                    row_max(b, 3)
                if a is not None:
                    queries_lo(a, 0)
                if b is not None:
                    probs_lo(b, 2)
                if more:
                    norm1_b(a.next())
                if b is not None:
                    scale_out(b, 1)
                if a is not None:
                    queries_lo(a, 1)
                if b is not None:
                    stats2(b, 0)
                if a is not None:
                    values_lo(a, 0)
                if g is not None:
                    route_max(g)
                if b is not None:
                    stats2(b, 1)
                if g is not None:
                    route_index(g)
                if b is not None:
                    scale_out(b, 2)
                if g is not None:
                    route_number(g)
                    route_picks(g)
                if b is not None:
                    probs_lo(b, 3)
                if g is not None:
                    route_before(g, 0)
                    route_b(g)
                    route_before(g, 1)
                if b is not None:
                    stats2(b, 2)
                    scale_out(b, 3)
                if g is not None:
                    route_c(g)
                if a is not None:
                    values_lo(a, 1)

            over_batches(dve, iteration)

            tc = Chain(dve, tab_s, N_TAB, 0)
            dve.wait_ge(cnt_done, 1)
            tc.step(dve.tensor_copy(cnt[:, 0, :], ps[0:1, BANK_S, 0:E]))
            tc.done()
            tc.step(dve.tensor_scalar(cnti[:, 0, :], cnt[:, 0, :], float(TT - 1), None, ALU.add))
            tc.step(dve.tensor_tensor(tab[:, 17:17 + E], cnt[:, 0, :], ecap[0:1, 0, :], ALU.add))
            tc.done()
            tc.step(dve.tensor_scalar(cnti[:, 1, :], cnti[:, 0, :], TT.bit_length() - 1, None, ALU.logical_shift_right))
            tc.done()
            tc.step(dve.tensor_scalar(cnt[:, 1, :], cnti[:, 1, :], 1.0, None, ALU.max))
            tc.done()
            tc.step(dve.tensor_tensor_scan(cnt[:, 2, :], unit[:, :], cnt[:, 1, :], 0.0, ALU.mult, ALU.add))
            tc.step(dve.memset(tab[:, 0:1], 0))
            tc.done()
            tc.step(dve.tensor_copy(tab[:, 1:1 + E], cnt[:, 2, :]))
            tc.step(dve.tensor_tensor(cnt[:, 3, :], cnt[:, 2, :], cnt[:, 1, :], ALU.subtract))
            tc.done()
            tc.step(dve.scalar_tensor_tensor(tab[:, 9:9 + E], cnt[:, 3, :], -float(TT), ecap[0:1, 0, :],
                                             ALU.mult, ALU.add))
            tc.step(dve.tensor_tensor(padf[:, 0, :], ps[:, BANK_S, 0:E], ownp[:, :], ALU.add))
            tc.done()
            tc.step(dve.tensor_tensor(padf[:, 1, :], padf[:, 0, :], ps[:, BANK_S, E:2 * E], ALU.subtract))
            tc.done()
            tc.step(dve.scalar_tensor_tensor(padf[:, 2, :], picks[:, NB - 1, :], float(P), padf[:, 1, :],
                                             ALU.mult, ALU.add))
            tc.done()
            tc.step(dve.tensor_scalar(padf[:, 0, :], padf[:, 2, :], float(P), float(E * CAP), ALU.is_ge, ALU.mult))
            tc.step(dve.tensor_tensor(padf[:, 1, :], padf[:, 2, :], ecap[:, 0, :], ALU.add))
            tc.done()
            tc.step(dve.tensor_tensor(padf[:, 2, :], padf[:, 0, :], padf[:, 1, :], ALU.add))
            tc.done()
            tc.step(dve.tensor_scalar(padslots[:, :], padf[:, 2, :], float(ROW // SHORT), float(ROW // SHORT - 1),
                                      ALU.mult, ALU.add))
            tc.done()
            dve.sem_inc(over, 1)
            phase_over(dve)
            dve.memset(gcur[:, :, :], 0.0).then_inc(clear, 1)
            dve.memset(ps[:, BANK_Y:BANK_Y + TB, 0:D], 0.0).then_inc(clear, 1)
            dve.memset(b2row[1][:, :], 0.0).then_inc(clear, 1)
            dve.tensor_copy(num[0][:, :], pad[:, :, :].bitcast(I32)[:, :, ID]).then_inc(clear, 1)
            dve.wait_ge(clear, 4)

            def tokens_lo(n):
                wait(dve, x_hi, n)
                dve.tensor_tensor(xtl[:, :, :], ps[:, BANK_X, :].rearrange("p (j t) -> p j t", j=KD),
                                  xth[:, :, :].bitcast(F32), ALU.subtract).then_inc(x_lo, 1)

            tokens_lo(1)

            def weigh_before(g, half):
                wait(dve, m2_done, g)
                wait(dve, y_free, g)
                y = ps[:, BANK_Y:BANK_Y + TB, 0:D]
                dve.tensor_tensor(ysc[:, :, :], y, b2row[half][:, :].unsqueeze(1).to_broadcast([P, TB, D]), ALU.add) \
                   .then_inc(y_sum, 1)
                dve.tensor_copy(num[1][:, :], num[0][:, :]).then_inc(y_sc, 1)
                wait(dve, y_sum, g + 1)
                dve.tensor_tensor(ysc[:, :, :], ysc[:, :, :], gcur[:, :, :], ALU.mult).then_inc(y_sc, 1)

            def weights_of(g, e):
                dve.wait_ge(aux_in, 16 * g + 16)
                for s in range(TB):
                    dve.tensor_scalar(gcur[:, s, :], aux[:, s, 0:D], aux[:, s, bass.ds(e + (RW - D), 1)], None,
                                      ALU.mult).then_inc(aux_read, 1)
                dve.tensor_copy(num[0][:, :], aux_i[:, :, ID - D]).then_inc(aux_read, 1)

            def tile(g, e, more):
                for j in range(KF):
                    wait(dve, g_act, KF * g + j + 1)
                    dve.tensor_copy(gh[:, j, :], gf[:, j, :]).then_inc(g_hi, 1)
                    wait(dve, g_hi, KF * g + j + 1)
                    dve.tensor_tensor(gl[:, j, :], gf[:, j, :], gh[:, j, :].bitcast(F32), ALU.subtract) \
                       .then_inc(g_lo, 1)
                    if j == 0:
                        weights_of(g, e)
                    else:
                        more(j)
                tokens_lo(g + 2)

            def expert(e, half, later):
                lo, hi, base = tile_range(dve, e)
                dve.wait_ge(b2_in, 16 * (e + 1))
                weigh_before(lo, 1 - half)

                def split(j):
                    if later and j == 1:
                        biases(e + 1, 1 - half)
                    if later >= 2 and j == 1:
                        dve.wait_ge(renumbered, 16 * (e + 2))
                        dve.tensor_scalar(padcur[:, :], padslots[:, bass.ds(e + 2, 1)], 0.0, None, ALU.add) \
                           .then_inc(pad_cur, 1)
                    if later and 2 <= j < 2 + CHUNKS:
                        split_rest(e + 1, 1 - half, j - 2, half)

                tile(lo, e, split)
                with dve.If(lo + 1 < hi):
                    with dve.Fori(lo + 1, hi) as g:
                        weigh_before(g, half)
                        tile(g, e, lambda j: None)

            over_experts(dve, expert)
            total = dve.value_load(tab[0:1, E:E + 1], min_val=E, max_val=TILES)
            weigh_before(total, 1)

        @block.tensor
        def _(pe):
            start(pe, t_done, q_done, v_done, s_done, pt_done, o_done, gt_done, lg_done, ps_done, x_done,
                  m1_done, m2_done)
            def three(out_, wh, wl, xh, xl, start, stop):
                pe.matmul(out_, wh, xh, start=start, stop=False)
                pe.matmul(out_, wh, xl, start=False, stop=False)
                return pe.matmul(out_, wl, xh, start=False, stop=stop)

            def tokens_T(b):
                wait(pe, g_full, KD * (b.val - 2))
                for i in range(NB):
                    wait(pe, xn_ready, NB * b.val + i + 1)
                    for j in range(KD):
                        mm = pe.transpose(ps[:, BANK_T + j, i * P:(i + 1) * P],
                                          xn[b.half][:, i, j * P:(j + 1) * P], ident[:, :])
                mm.then_inc(t_done, 1)

            pe.wait_ge(consts, 9)
            pe.wait_ge(c_in, 32)
            for j in range(KD):
                pe.transpose(ps[:, 6, j * B:(j + 1) * B], c_s[:, j * P:(j + 1) * P], ident[0:B, 0:B])
            pe.transpose(ps[:, 6, 16:16 + E * KF], rows64[:, :], ident[0:E * KF, 0:E * KF]).then_inc(setup_pe, 1)
            wait(pe, setup_dve, SETUP_SILU)
            def modulation(n):
                for j in range(KD):
                    mm = pe.matmul(ps[0:B, 3 + n, :], cT[:, j, :], wmod_s[:, j, n * 512:(n + 1) * 512],
                                   start=(j == 0), stop=(j == KD - 1))
                return mm

            def modulation_T(at_n, m):
                for j in range(KD):
                    mm = pe.transpose(ps[:, 6, (at_n * KD + j) * B:(at_n * KD + j + 1) * B],
                                      mods[:, m, j * P:(j + 1) * P], ident[0:B, 0:B])
                return mm

            pe.wait_ge(m_in[0], 16)
            modulation(0).then_inc(setup_pe, 1)
            wait(pe, setup_dve, SETUP_FIRST)
            modulation_T(0, 0)
            modulation_T(1, 1).then_inc(setup_pe, 1)
            pe.wait_ge(w_in, 48)
            for hj in range(KD):
                for oj in range(KD):
                    pe.matmul(ps[:, 2, hj * D:(hj + 1) * D], wq_s[:, oj, hj * P:(hj + 1) * P], wk_s[:, oj, :],
                              start=(oj == 0), stop=(oj == KD - 1))
            for oj in range(KD):
                for hj in range(KD):
                    mm = pe.transpose(ps[:, 7, hj * D + oj * P:hj * D + (oj + 1) * P],
                                      wv_s[:, oj, hj * P:(hj + 1) * P], ident[:, :])
            mm.then_inc(setup_pe, 1)
            tokens_T(Batch(0, 0, 0))
            pe.wait_ge(m_in[1], 16)
            modulation(1)
            modulation(2).then_inc(setup_pe, 1)
            pe.wait_ge(r_in, 16 * (1 + NB))
            wait(pe, setup_dve, SETUP_SPLIT)

            def queries(b, m):
                wait(pe, h_lo, KD * (b.val + 1))
                if m == 0:
                    wait(pe, ps_read, b.val - 2)
                    wait(pe, v_lo, 2 * b.val - 1)
                else:
                    wait(pe, v_lo, 2 * b.val)
                    wait(pe, lg_read, b.val - 2)
                for j in range(KD):
                    mm = three(ps[:, BANK_QA + m, :], mh[:, j, m * P:(m + 1) * P], ml[:, j, m * P:(m + 1) * P],
                               hh[b.half][:, j, :], hl[b.half][:, j, :], j == 0, j == KD - 1)
                mm.then_inc(q_done, 1)

            def values(b, p):
                if p == 0:
                    wait(pe, q_lo, KD * b.val + 1)
                else:
                    wait(pe, q_lo, KD * b.val + 2)
                    wait(pe, lg_read, b.val - 1)
                for i in (2 * p, 2 * p + 1):
                    tok = slice(i * P, (i + 1) * P)
                    for j in range(KD):
                        o = ps[:, BANK_QA + p, (i % 2) * D:(i % 2 + 1) * D]
                        pe.matmul(o, hh[b.half][:, j, tok], wvh[:, j, :], start=(j == 0), stop=False)
                        pe.matmul(o, hh[b.half][:, j, tok], wvl[:, j, :], start=False, stop=False)
                        mm = pe.matmul(o, hl[b.half][:, j, tok], wvh[:, j, :], start=False, stop=(j == KD - 1))
                mm.then_inc(v_done, 1)

            def scores(b, i):
                if i == 0:
                    wait(pe, q_lo, KD * (b.val + 1))
                wait(pe, p_exp, NB * b.val + i - 1)
                n = max(2, i + 1) * P
                tok = slice(i * P, (i + 1) * P)
                bank = ps[:, BANK_S + i % 2, :]
                for j in range(KD):
                    q_hi_, q_lo_ = qh[b.half][:, j, tok], ql[b.half][:, j, tok]
                    pe.matmul(bank[:, 0:n], q_hi_, hh[b.half][:, j, 0:n], start=(j == 0), stop=False)
                    if j == 0:
                        pe.matmul(bank[:, tok], identb[:, :], maskb[:, :], start=False, stop=False)
                    pe.matmul(bank[:, 0:n], q_hi_, hl[b.half][:, j, 0:n], start=False, stop=False)
                    mm = pe.matmul(bank[:, 0:n], q_lo_, hh[b.half][:, j, 0:n], start=False, stop=(j == KD - 1))
                mm.then_inc(s_done, 1)

            def probs_T(b, i):
                wait(pe, p_exp, NB * b.val + i + 1)
                wait(pe, pt_lo, NB * b.val + i)
                for j in range(i + 1):
                    mm = pe.transpose(ps[:, BANK_P, j * P:(j + 1) * P], pr[i % 2][:, j * P:(j + 1) * P], ident[:, :])
                mm.then_inc(pt_done, 1)

            def attend(b, i):
                wait(pe, pt_lo, NB * b.val + i + 1)
                if i == 0:
                    wait(pe, v_lo, 2 * (b.val + 1))
                wait(pe, o_scaled, NB * b.val + i)
                o = ps[:, BANK_O, (i % 2) * D:(i % 2 + 1) * D]
                for j in range(i + 1):
                    pe.matmul(o, pth[i % 2][:, j, :], vh[b.half][:, j, :], start=(j == 0), stop=False)
                    pe.matmul(o, pth[i % 2][:, j, :], vl[b.half][:, j, :], start=False, stop=False)
                    mm = pe.matmul(o, ptl[i % 2][:, j, :], vh[b.half][:, j, :], start=False, stop=(j == i))
                mm.then_inc(o_done, 1)

            def h2_T(b):
                n = b.val + 3
                wait(pe, h_full, KD * (min(n, B) if isinstance(n, int) else n))
                for i in range(NB):
                    wait(pe, xn2_ready, NB * b.val + i + 1)
                    for j in range(KD):
                        mm = pe.transpose(ps[:, BANK_T + j, i * P:(i + 1) * P],
                                          xn2[:, i, j * P:(j + 1) * P], ident[:, :])
                mm.then_inc(gt_done, 1)

            def logits(b):
                wait(pe, g_full, KD * (b.val + 1))
                n = b.val + 3
                wait(pe, q_lo, KD * (min(n, B) if isinstance(n, int) else n))
                for i in range(NB):
                    for j in range(KD):
                        mm = pe.matmul(ps[:, BANK_QB, i * E:(i + 1) * E], h2f[:, j, i * P:(i + 1) * P], gw[:, j, :],
                                       start=(j == 0), stop=(j == KD - 1))
                mm.then_inc(lg_done, 1)

            def places(b):
                wait(pe, ra_s, RA * (b.val + 1))
                n = b.val + 3
                wait(pe, v_lo, 2 * (min(n, B) if isinstance(n, int) else n) - 1)
                o = ps[:, BANK_QA, 0:NB * E]
                pe.matmul(o, trib[:, :], picks[:, :, :].rearrange("p i e -> p (i e)"), start=True, stop=False)
                pe.matmul(o, onesb[:, :], before[:, 0:NB, :].rearrange("p i e -> p (i e)"), start=False, stop=True) \
                  .then_inc(ps_done, 1)

            def iteration(k, a, b, g):
                more = there(a, 1)
                if k is None:
                    for m in range(KD):
                        queries(a, m)
                    wait(pe, setup_dve, SETUP_MODS)
                    modulation_T(2, 3)
                    modulation_T(3, 4).then_inc(setup_pe, 1)
                    tokens_T(a.next())
                    for p in range(2):
                        values(a, p)
                    return
                if b is not None:
                    scores(b, 0)
                    scores(b, 1)
                if a is not None:
                    queries(a, 0)
                if b is not None:
                    probs_T(b, 0)
                    scores(b, 2)
                    probs_T(b, 1)
                    attend(b, 0)
                    scores(b, 3)
                    probs_T(b, 2)
                if a is not None:
                    queries(a, 1)
                if g is not None:
                    h2_T(g)
                if b is not None:
                    attend(b, 1)
                    probs_T(b, 3)
                if a is not None:
                    values(a, 0)
                if g is not None:
                    logits(g)
                if more:
                    tokens_T(a.next())
                if b is not None:
                    attend(b, 2)
                if a is not None:
                    values(a, 1)
                if b is not None:
                    attend(b, 3)
                if g is not None:
                    places(g)

            over_batches(pe, iteration)
            pe.matmul(ps[:, BANK_S, 0:E], onesb[:, :], before[:, NB, :], start=True, stop=True)
            pe.matmul(ps[:, BANK_S, E:2 * E], trib[:, :], picks[:, NB - 1, :], start=True, stop=True) \
              .then_inc(cnt_done, 1)
            pe.wait_ge(cnt_done, 1)
            pe.sem_inc(over, 1)
            phase_over(pe)

            def tile_T(n):
                pe.wait_ge(xt_in, 16 * n + 16)
                for s in range(TB):
                    for j in range(KD):
                        mm = pe.transpose(ps[:, BANK_X, j * TT + s * P:j * TT + (s + 1) * P],
                                          xt[:, s, j * P:(j + 1) * P], ident[:, :])
                mm.then_inc(x_done, 1)

            def up(g, j, half):
                cols = slice(j * P, (j + 1) * P)
                if j == 0:
                    wait(pe, x_lo, g + 1)
                if j >= 4:
                    wait(pe, g_act, KF * g + j - 3)
                for n in range(KD):
                    mm = three(ps[:, BANK_H + j % 4, 0:TT], w1h[half][:, n, cols], w1l[half][:, n, cols],
                               xth[:, n, :], xtl[:, n, :], n == 0, n == KD - 1)
                mm.then_inc(m1_done, 1)

            def down(g, j, half):
                wait(pe, g_lo, KF * g + j + 1)
                if j == 0:
                    wait(pe, y_sum, g + 1)
                for s in range(TB):
                    y, tok = ps[:, BANK_Y + s, 0:D], slice(s * P, (s + 1) * P)
                    pe.matmul(y, gh[:, j, tok], w2h[half][:, j, :], start=(j == 0), stop=False)
                    pe.matmul(y, gh[:, j, tok], w2l[half][:, j, :], start=False, stop=False)
                    mm = pe.matmul(y, gl[:, j, tok], w2h[half][:, j, :], start=False, stop=(j == KF - 1))
                if j == KF - 1:
                    mm.then_inc(m2_done, 1)

            tile_T(0)

            def expert(e, half, later):
                lo, hi, base = tile_range(pe, e)
                wait_alone(pe, (w1_lo, CHUNKS * (e + 1)), (w2_lo, CHUNKS * (e + 1)))
                with pe.Fori(lo, hi) as g:
                    for j in range(KF):
                        up(g, j, half)
                        if j >= LAG:
                            down(g, j - LAG, half)
                    tile_T(g + 1)
                    for j in range(KF - LAG, KF):
                        down(g, j, half)

            over_experts(pe, expert)


SETUP_SILU = 5
SETUP_FIRST = SETUP_SILU + 2
SETUP_SPLIT = SETUP_FIRST + 5
SETUP_MODS = SETUP_SPLIT + 2 + 8


_INS = ["L0_attn_x", "L0_attn_Wq", "L0_attn_Wk", "L0_attn_Wv", "L0_ffn_gate_w", "L0_ffn_gate_b",
        "L0_ffn_w1", "L0_ffn_b1", "L0_ffn_w2", "L0_ffn_b2", "L0_c", "L0_wmod"]


def kernel(**inputs):
    import numpy as np
    import concourse.bacc as bacc
    from concourse.bass_utils import run_bass_kernel_spmd

    nc = bacc.Bacc("TRN2", target_bir_lowering=False, num_devices=1)
    arrays, args = {}, []
    for name in _INS:
        a = np.ascontiguousarray(inputs[name])
        arrays[f"in_{name}"] = a
        args.append(nc.dram_tensor(f"in_{name}", a.shape, mybir.dt.from_np(a.dtype), kind="ExternalInput").ap())
    args.append(nc.dram_tensor("out_0", (B, S, D), F32, kind="ExternalOutput").ap())
    layer(nc, *args)
    r = run_bass_kernel_spmd(nc, [arrays], core_ids=[0])
    return r.results[0]["out_0"]
```
